# Optimizing a Trainium2 kernel written in Bass

```python
import numpy as np
import jax
import jax.numpy as jnp

def _softmax(x, axis=-1):
    return jax.nn.softmax(x, axis=axis)

def _gelu(x):
    return jax.nn.gelu(x, approximate=True)

def _silu(x):
    return jax.nn.silu(x)

def _sigmoid(x):
    return jax.nn.sigmoid(x)

def _layernorm(x, axis=-1, eps=1e-05):
    m = jnp.mean(x, axis=axis, keepdims=True)
    v = jnp.var(x, axis=axis, keepdims=True)
    return (x - m) / jnp.sqrt(v + eps)

def _scatter_add(tgt, idx, src, axis=0):
    return tgt.at[idx].add(src)

def _segment_sum(src, seg, n):
    return jax.ops.segment_sum(src, seg, n)
kernel_name = 'mk_xattn_seq_d4_seqx_r8_43d06f'

def setup_inputs(seed: int=0):
    np.random.seed(seed)
    _w = jnp.asarray

    def _rec_inputs():
        import jax
        import jax.numpy as jnp
        _rk = jax.random.key(seed)
        x = -0.0005207 + 1.001 * jax.random.normal(jax.random.fold_in(_rk, 1), (32, 64, 256), jnp.float32)
        _lenS = 64 - jax.random.randint(jax.random.fold_in(_rk, 7), (32,), 0, max(1, 64 // 4) + 1, jnp.int32)
        _lenS2 = 64 - jax.random.randint(jax.random.fold_in(_rk, 8), (32,), 0, max(1, 64 // 4) + 1, jnp.int32)
        _ctx_2048P = jax.random.normal(jax.random.fold_in(_rk, 11), (32, 16, 256), jnp.float32)
        _ctx_2048c = jax.random.dirichlet(jax.random.fold_in(_rk, 511), 0.3 * jnp.ones((16,), jnp.float32), (32, 64))
        _ctx_2048t = jnp.einsum('bsk,bkd->bsd', _ctx_2048c, _ctx_2048P)
        _ctx_2048t = _ctx_2048t * jax.lax.rsqrt(jnp.mean(jnp.square(_ctx_2048t)) + 1e-12) * 0.953939
        ctx_2048 = 2.81802e-05 + 1.00001 * (_ctx_2048t + 0.3 * jax.random.normal(jax.random.fold_in(_rk, 611), (32, 64, 256), jnp.float32))
        _validS = jnp.arange(64)[None, :] < _lenS[:, None]
        _validS2 = jnp.arange(64)[None, :] < _lenS2[:, None]
        _causal = jnp.tril(jnp.ones((64, 64), dtype=bool))
        mask_Bx1xSxS2_ff0 = jnp.where(jnp.ones((32, 1, 64, 64), dtype=bool), 0.0, -1000000000.0).astype(jnp.float32)
        mask_1x1xSxS2_fc1 = jnp.where(jnp.broadcast_to(_validS2[0:1, None, None, :], (1, 1, 64, 64)), 1.0, 0.0).astype(jnp.float32)
        mask_Bx1xSxS2_ff1 = jnp.where(jnp.ones((32, 1, 64, 64), dtype=bool), 1.0, 0.0).astype(jnp.float32)
        return (x, ctx_2048, mask_Bx1xSxS2_ff0, mask_1x1xSxS2_fc1, mask_Bx1xSxS2_ff1)
    x, ctx_2048, mask_Bx1xSxS2_ff0, mask_1x1xSxS2_fc1, mask_Bx1xSxS2_ff1 = _rec_inputs()

    def _L0_xattn_setup():
        import jax, jax.numpy as jnp
        import numpy as np
        B, Q, S1, S2 = (4, 32, 256, 256)
        D, H, K, F = (256, 16, 128, 1024)
        LN_EPS = 1e-05

        def _layer_norm(x, scale, offset):
            mu = jnp.mean(x, axis=-1, keepdims=True)
            var = jnp.var(x, axis=-1, keepdims=True)
            return (x - mu) * jax.lax.rsqrt(var + LN_EPS) * scale + offset

        def _cross_attention(q_in, kv_in, wq, bq, wk, bk, wv, bv, wo, bo, bias_k, bias_v):
            b, q_len, _ = q_in.shape
            t = kv_in.shape[1]
            qh = (q_in @ wq + bq).reshape(b, q_len, H, K)
            kh = (kv_in @ wk + bk).reshape(b, t, H, K)
            vh = (kv_in @ wv + bv).reshape(b, t, H, K)
            kh = jnp.concatenate([kh, jnp.broadcast_to(bias_k, (b, 1, H, K))], axis=1)
            vh = jnp.concatenate([vh, jnp.broadcast_to(bias_v, (b, 1, H, K))], axis=1)
            scale = jnp.sqrt(jnp.asarray(K, q_in.dtype))
            logits = jnp.einsum('bqhk,bthk->bhqt', qh, kh) / scale
            weights = jax.nn.softmax(logits, axis=-1)
            ctx = jnp.einsum('bhqt,bthk->bqhk', weights, vh).reshape(b, q_len, H * K)
            return ctx @ wo + bo

        def _forward(x, xf_1, xf_2, ln1_scale, ln1_offset, wq1, bq1, wk1, bk1, wv1, bv1, wo1, bo1, bias_k1, bias_v1, ln2_scale, ln2_offset, wq2, bq2, wk2, bk2, wv2, bv2, wo2, bo2, bias_k2, bias_v2, ln_mlp_scale, ln_mlp_offset, w_fc1, b_fc1, w_fc2, b_fc2):
            res = x
            h = _layer_norm(x, ln1_scale, ln1_offset)
            x = res + _cross_attention(h, xf_1, wq1, bq1, wk1, bk1, wv1, bv1, wo1, bo1, bias_k1, bias_v1)
            res = x
            h = _layer_norm(x, ln2_scale, ln2_offset)
            x = res + _cross_attention(h, xf_2, wq2, bq2, wk2, bk2, wv2, bv2, wo2, bo2, bias_k2, bias_v2)
            h = _layer_norm(x, ln_mlp_scale, ln_mlp_offset)
            h = jax.nn.gelu(h @ w_fc1 + b_fc1, approximate=False) @ w_fc2 + b_fc2
            return x + h
        key = jax.random.key(seed)
        ks = iter(jax.random.split(key, 64))

        def rn(shape, s=0.02):
            return jax.random.normal(next(ks), shape, jnp.float32) * s
        inp = {'x': rn((B, Q, D), 1.0), 'xf_1': rn((B, S1, D), 1.0), 'xf_2': rn((B, S2, D), 1.0)}
        for i in (1, 2):
            inp[f'ln{i}_scale'] = jnp.ones((D,), jnp.float32)
            inp[f'ln{i}_offset'] = jnp.zeros((D,), jnp.float32)
            inp[f'wq{i}'] = rn((D, H * K))
            inp[f'bq{i}'] = jnp.zeros((H * K,), jnp.float32)
            inp[f'wk{i}'] = rn((D, H * K))
            inp[f'bk{i}'] = jnp.zeros((H * K,), jnp.float32)
            inp[f'wv{i}'] = rn((D, H * K))
            inp[f'bv{i}'] = jnp.zeros((H * K,), jnp.float32)
            inp[f'wo{i}'] = rn((H * K, D))
            inp[f'bo{i}'] = jnp.zeros((D,), jnp.float32)
            inp[f'bias_k{i}'] = rn((1, 1, H, K))
            inp[f'bias_v{i}'] = rn((1, 1, H, K))
        inp['ln_mlp_scale'] = jnp.ones((D,), jnp.float32)
        inp['ln_mlp_offset'] = jnp.zeros((D,), jnp.float32)
        inp['w_fc1'] = rn((D, F))
        inp['b_fc1'] = jnp.zeros((F,), jnp.float32)
        inp['w_fc2'] = rn((F, D))
        inp['b_fc2'] = jnp.zeros((D,), jnp.float32)
        return inp
    _L0_xattn_all = _L0_xattn_setup()
    _L0_xattn_in = {k: v for k, v in _L0_xattn_all.items() if k in ('ln1_scale', 'ln1_offset', 'wq1', 'bq1', 'wk1', 'bk1', 'wv1', 'bv1', 'wo1', 'bo1', 'bias_k1', 'bias_v1', 'ln2_scale', 'ln2_offset', 'wq2', 'bq2', 'wk2', 'bk2', 'wv2', 'bv2', 'wo2', 'bo2', 'bias_k2', 'bias_v2', 'ln_mlp_scale', 'ln_mlp_offset', 'w_fc1', 'b_fc1', 'w_fc2', 'b_fc2')}
    del _L0_xattn_all

    def _L1_xattn_setup():
        import jax, jax.numpy as jnp
        import numpy as np
        H = 256
        NH = 32
        KVH = 8
        HD = H // NH
        GROUPS = NH // KVH
        EPS = 1e-06
        B, L, S = (4, 128, 128)

        def _gqa_forward(hidden_state, encoder_hidden_state, encoder_attention_mask, Wq, bq, Wk, bk, Wv, bv, Wo, bo, gamma, beta):
            b, l, _ = hidden_state.shape
            s = encoder_hidden_state.shape[1]
            q = hidden_state @ Wq + bq
            k = encoder_hidden_state @ Wk + bk
            v = encoder_hidden_state @ Wv + bv
            q = q.reshape(b, l, KVH, GROUPS, HD).transpose(0, 2, 3, 1, 4)
            k = k.reshape(b, s, KVH, HD).transpose(0, 2, 1, 3)
            v = v.reshape(b, s, KVH, HD).transpose(0, 2, 1, 3)
            scale = 1.0 / jnp.sqrt(jnp.asarray(HD, q.dtype))
            scores = jnp.einsum('bkgld,bksd->bkgls', q, k) * scale
            scores = scores + encoder_attention_mask[:, :, None, :, :]
            attn = jax.nn.softmax(scores, axis=-1)
            out = jnp.einsum('bkgls,bksd->bkgld', attn, v)
            out = out.transpose(0, 3, 1, 2, 4).reshape(b, l, H)
            out = out @ Wo + bo
            x = out + hidden_state
            mu = jnp.mean(x, axis=-1, keepdims=True)
            var = jnp.var(x, axis=-1, keepdims=True)
            return (x - mu) * jax.lax.rsqrt(var + EPS) * gamma + beta
        key = jax.random.key(seed)
        ks = jax.random.split(key, 12)
        sd = 0.02
        return {'hidden_state': jax.random.normal(ks[0], (B, L, H), jnp.float32), 'encoder_hidden_state': jax.random.normal(ks[1], (B, S, H), jnp.float32), 'encoder_attention_mask': jnp.zeros((B, 1, L, S), jnp.float32), 'Wq': jax.random.normal(ks[2], (H, H), jnp.float32) * sd, 'bq': jnp.zeros((H,), jnp.float32), 'Wk': jax.random.normal(ks[3], (H, KVH * HD), jnp.float32) * sd, 'bk': jnp.zeros((KVH * HD,), jnp.float32), 'Wv': jax.random.normal(ks[4], (H, KVH * HD), jnp.float32) * sd, 'bv': jnp.zeros((KVH * HD,), jnp.float32), 'Wo': jax.random.normal(ks[5], (H, H), jnp.float32) * sd, 'bo': jnp.zeros((H,), jnp.float32), 'gamma': jnp.ones((H,), jnp.float32), 'beta': jnp.zeros((H,), jnp.float32)}
    _L1_xattn_all = _L1_xattn_setup()
    _L1_xattn_in = {k: v for k, v in _L1_xattn_all.items() if k in ('Wq', 'bq', 'Wk', 'bk', 'Wv', 'bv', 'Wo', 'bo', 'gamma', 'beta')}
    del _L1_xattn_all

    def _L2_xattn_setup():
        import jax, jax.numpy as jnp
        import numpy as np
        EPS = 1e-05

        def _inorm(x):
            m = jnp.mean(x, axis=-1, keepdims=True)
            v = jnp.var(x, axis=-1, keepdims=True)
            return (x - m) * jax.lax.rsqrt(v + EPS)

        def _conv1x1(W, b, x):
            return jnp.einsum('oc,bct->bot', W, x) + b[None, :, None]
        key = jax.random.key(seed)
        ks = jax.random.split(key, 10)
        B, C, T = (4, 64, 256)
        s = 1.0 / np.sqrt(C)
        return {'x_c': jax.random.normal(ks[0], (B, C, T), jnp.float32), 'x_s': jax.random.normal(ks[1], (B, C, T), jnp.float32), 'Wn': jax.random.normal(ks[2], (C, C), jnp.float32) * s, 'bn': jax.random.normal(ks[3], (C,), jnp.float32) * s, 'Wm': jax.random.normal(ks[4], (C, C), jnp.float32) * s, 'bm': jax.random.normal(ks[5], (C,), jnp.float32) * s, 'Wl': jax.random.normal(ks[6], (C, C), jnp.float32) * s, 'bl': jax.random.normal(ks[7], (C,), jnp.float32) * s, 'Wo': jax.random.normal(ks[8], (C, C), jnp.float32) * s, 'bo': jax.random.normal(ks[9], (C,), jnp.float32) * s}
    _L2_xattn_all = _L2_xattn_setup()
    _L2_xattn_in = {k: v for k, v in _L2_xattn_all.items() if k in ('Wn', 'bn', 'Wm', 'bm', 'Wl', 'bl', 'Wo', 'bo')}
    del _L2_xattn_all

    def _L3_xattn_setup():
        import jax, jax.numpy as jnp
        import numpy as np
        H = 256
        NH = 16
        HD = H // NH
        EPS = 1e-05

        def gelu(x):
            return 0.5 * x * (1.0 + jnp.tanh(0.7978845608028654 * x * (1.0 + 0.044715 * x * x)))

        def layernorm(x, scale, bias):
            m = jnp.mean(x, axis=-1, keepdims=True)
            v = jnp.mean(jnp.square(x - m), axis=-1, keepdims=True)
            return (x - m) * jax.lax.rsqrt(v + EPS) * scale + bias

        def split_heads(x):
            b, s, _ = x.shape
            return x.reshape(b, s, NH, HD).transpose(0, 2, 1, 3)

        def merge_heads(x):
            b, nh, s, hd = x.shape
            return x.transpose(0, 2, 1, 3).reshape(b, s, nh * hd)

        def attention(q, k, v, mask):
            scores = jnp.einsum('bhqd,bhkd->bhqk', q, k) / jnp.sqrt(jnp.float32(HD))
            scores = scores * mask - 10000.0 * (1.0 - mask)
            probs = jax.nn.softmax(scores, axis=-1)
            return jnp.einsum('bhqk,bhkd->bhqd', probs, v)
        key = jax.random.key(seed)
        ks = jax.random.split(key, 16)
        b, s, t = (2, 128, 128)
        w = lambda k, i, o: jax.random.normal(k, (i, o), jnp.float32) * 0.02
        inp = {'hidden_states': jax.random.normal(ks[0], (b, s, H), jnp.float32), 'encoder_states': jax.random.normal(ks[1], (b, t, H), jnp.float32), 'ltor_mask': jnp.tril(jnp.ones((1, 1, s, s), jnp.float32)), 'cross_mask': jnp.ones((b, 1, s, t), jnp.float32), 'ln1_s': jnp.ones((H,), jnp.float32), 'ln1_b': jnp.zeros((H,), jnp.float32), 'w_qkv': w(ks[2], H, 3 * H), 'b_qkv': jnp.zeros((3 * H,), jnp.float32), 'w_ao': w(ks[3], H, H), 'b_ao': jnp.zeros((H,), jnp.float32), 'ln2_s': jnp.ones((H,), jnp.float32), 'ln2_b': jnp.zeros((H,), jnp.float32), 'w_q': w(ks[4], H, H), 'b_q': jnp.zeros((H,), jnp.float32), 'w_kv': w(ks[5], H, 2 * H), 'b_kv': jnp.zeros((2 * H,), jnp.float32), 'w_co': w(ks[6], H, H), 'b_co': jnp.zeros((H,), jnp.float32), 'ln3_s': jnp.ones((H,), jnp.float32), 'ln3_b': jnp.zeros((H,), jnp.float32), 'w1': w(ks[7], H, 4 * H), 'b1': jnp.zeros((4 * H,), jnp.float32), 'w2': w(ks[8], 4 * H, H), 'b2': jnp.zeros((H,), jnp.float32)}
        return inp
    _L3_xattn_all = _L3_xattn_setup()
    _L3_xattn_in = {k: v for k, v in _L3_xattn_all.items() if k in ('ln1_s', 'ln1_b', 'w_qkv', 'b_qkv', 'w_ao', 'b_ao', 'ln2_s', 'ln2_b', 'w_q', 'b_q', 'w_kv', 'b_kv', 'w_co', 'b_co', 'ln3_s', 'ln3_b', 'w1', 'b1', 'w2', 'b2')}
    del _L3_xattn_all
    return {'x': x, 'ctx_2048': ctx_2048, 'mask_Bx1xSxS2_ff0': mask_Bx1xSxS2_ff0, 'mask_1x1xSxS2_fc1': mask_1x1xSxS2_fc1, 'mask_Bx1xSxS2_ff1': mask_Bx1xSxS2_ff1, 'L0_xattn_ln1_scale': _L0_xattn_in['ln1_scale'], 'L0_xattn_ln1_offset': _L0_xattn_in['ln1_offset'], 'L0_xattn_wq1': _L0_xattn_in['wq1'], 'L0_xattn_bq1': _L0_xattn_in['bq1'], 'L0_xattn_wk1': _L0_xattn_in['wk1'], 'L0_xattn_bk1': _L0_xattn_in['bk1'], 'L0_xattn_wv1': _L0_xattn_in['wv1'], 'L0_xattn_bv1': _L0_xattn_in['bv1'], 'L0_xattn_wo1': _L0_xattn_in['wo1'], 'L0_xattn_bo1': _L0_xattn_in['bo1'], 'L0_xattn_bias_k1': _L0_xattn_in['bias_k1'], 'L0_xattn_bias_v1': _L0_xattn_in['bias_v1'], 'L0_xattn_ln2_scale': _L0_xattn_in['ln2_scale'], 'L0_xattn_ln2_offset': _L0_xattn_in['ln2_offset'], 'L0_xattn_wq2': _L0_xattn_in['wq2'], 'L0_xattn_bq2': _L0_xattn_in['bq2'], 'L0_xattn_wk2': _L0_xattn_in['wk2'], 'L0_xattn_bk2': _L0_xattn_in['bk2'], 'L0_xattn_wv2': _L0_xattn_in['wv2'], 'L0_xattn_bv2': _L0_xattn_in['bv2'], 'L0_xattn_wo2': _L0_xattn_in['wo2'], 'L0_xattn_bo2': _L0_xattn_in['bo2'], 'L0_xattn_bias_k2': _L0_xattn_in['bias_k2'], 'L0_xattn_bias_v2': _L0_xattn_in['bias_v2'], 'L0_xattn_ln_mlp_scale': _L0_xattn_in['ln_mlp_scale'], 'L0_xattn_ln_mlp_offset': _L0_xattn_in['ln_mlp_offset'], 'L0_xattn_w_fc1': _L0_xattn_in['w_fc1'], 'L0_xattn_b_fc1': _L0_xattn_in['b_fc1'], 'L0_xattn_w_fc2': _L0_xattn_in['w_fc2'], 'L0_xattn_b_fc2': _L0_xattn_in['b_fc2'], 'L1_xattn_Wq': _L1_xattn_in['Wq'], 'L1_xattn_bq': _L1_xattn_in['bq'], 'L1_xattn_Wk': _L1_xattn_in['Wk'], 'L1_xattn_bk': _L1_xattn_in['bk'], 'L1_xattn_Wv': _L1_xattn_in['Wv'], 'L1_xattn_bv': _L1_xattn_in['bv'], 'L1_xattn_Wo': _L1_xattn_in['Wo'], 'L1_xattn_bo': _L1_xattn_in['bo'], 'L1_xattn_gamma': _L1_xattn_in['gamma'], 'L1_xattn_beta': _L1_xattn_in['beta'], 'L2_xattn_Wn': _L2_xattn_in['Wn'], 'L2_xattn_bn': _L2_xattn_in['bn'], 'L2_xattn_Wm': _L2_xattn_in['Wm'], 'L2_xattn_bm': _L2_xattn_in['bm'], 'L2_xattn_Wl': _L2_xattn_in['Wl'], 'L2_xattn_bl': _L2_xattn_in['bl'], 'L2_xattn_Wo': _L2_xattn_in['Wo'], 'L2_xattn_bo': _L2_xattn_in['bo'], 'L3_xattn_ln1_s': _L3_xattn_in['ln1_s'], 'L3_xattn_ln1_b': _L3_xattn_in['ln1_b'], 'L3_xattn_w_qkv': _L3_xattn_in['w_qkv'], 'L3_xattn_b_qkv': _L3_xattn_in['b_qkv'], 'L3_xattn_w_ao': _L3_xattn_in['w_ao'], 'L3_xattn_b_ao': _L3_xattn_in['b_ao'], 'L3_xattn_ln2_s': _L3_xattn_in['ln2_s'], 'L3_xattn_ln2_b': _L3_xattn_in['ln2_b'], 'L3_xattn_w_q': _L3_xattn_in['w_q'], 'L3_xattn_b_q': _L3_xattn_in['b_q'], 'L3_xattn_w_kv': _L3_xattn_in['w_kv'], 'L3_xattn_b_kv': _L3_xattn_in['b_kv'], 'L3_xattn_w_co': _L3_xattn_in['w_co'], 'L3_xattn_b_co': _L3_xattn_in['b_co'], 'L3_xattn_ln3_s': _L3_xattn_in['ln3_s'], 'L3_xattn_ln3_b': _L3_xattn_in['ln3_b'], 'L3_xattn_w1': _L3_xattn_in['w1'], 'L3_xattn_b1': _L3_xattn_in['b1'], 'L3_xattn_w2': _L3_xattn_in['w2'], 'L3_xattn_b2': _L3_xattn_in['b2']}

def reference(x, ctx_2048, mask_Bx1xSxS2_ff0, mask_1x1xSxS2_fc1, mask_Bx1xSxS2_ff1, L0_xattn_ln1_scale, L0_xattn_ln1_offset, L0_xattn_wq1, L0_xattn_bq1, L0_xattn_wk1, L0_xattn_bk1, L0_xattn_wv1, L0_xattn_bv1, L0_xattn_wo1, L0_xattn_bo1, L0_xattn_bias_k1, L0_xattn_bias_v1, L0_xattn_ln2_scale, L0_xattn_ln2_offset, L0_xattn_wq2, L0_xattn_bq2, L0_xattn_wk2, L0_xattn_bk2, L0_xattn_wv2, L0_xattn_bv2, L0_xattn_wo2, L0_xattn_bo2, L0_xattn_bias_k2, L0_xattn_bias_v2, L0_xattn_ln_mlp_scale, L0_xattn_ln_mlp_offset, L0_xattn_w_fc1, L0_xattn_b_fc1, L0_xattn_w_fc2, L0_xattn_b_fc2, L1_xattn_Wq, L1_xattn_bq, L1_xattn_Wk, L1_xattn_bk, L1_xattn_Wv, L1_xattn_bv, L1_xattn_Wo, L1_xattn_bo, L1_xattn_gamma, L1_xattn_beta, L2_xattn_Wn, L2_xattn_bn, L2_xattn_Wm, L2_xattn_bm, L2_xattn_Wl, L2_xattn_bl, L2_xattn_Wo, L2_xattn_bo, L3_xattn_ln1_s, L3_xattn_ln1_b, L3_xattn_w_qkv, L3_xattn_b_qkv, L3_xattn_w_ao, L3_xattn_b_ao, L3_xattn_ln2_s, L3_xattn_ln2_b, L3_xattn_w_q, L3_xattn_b_q, L3_xattn_w_kv, L3_xattn_b_kv, L3_xattn_w_co, L3_xattn_b_co, L3_xattn_ln3_s, L3_xattn_ln3_b, L3_xattn_w1, L3_xattn_b1, L3_xattn_w2, L3_xattn_b2):
    import jax
    import jax.numpy as jnp

    def _L0_xattn_ref(x, xf_1, xf_2, ln1_scale, ln1_offset, wq1, bq1, wk1, bk1, wv1, bv1, wo1, bo1, bias_k1, bias_v1, ln2_scale, ln2_offset, wq2, bq2, wk2, bk2, wv2, bv2, wo2, bo2, bias_k2, bias_v2, ln_mlp_scale, ln_mlp_offset, w_fc1, b_fc1, w_fc2, b_fc2):
        import jax, jax.numpy as jnp
        import numpy as np
        B, Q, S1, S2 = (4, 32, 256, 256)
        D, H, K, F = (256, 16, 128, 1024)
        LN_EPS = 1e-05

        def _layer_norm(x, scale, offset):
            mu = jnp.mean(x, axis=-1, keepdims=True)
            var = jnp.var(x, axis=-1, keepdims=True)
            return (x - mu) * jax.lax.rsqrt(var + LN_EPS) * scale + offset

        def _cross_attention(q_in, kv_in, wq, bq, wk, bk, wv, bv, wo, bo, bias_k, bias_v):
            b, q_len, _ = q_in.shape
            t = kv_in.shape[1]
            qh = (q_in @ wq + bq).reshape(b, q_len, H, K)
            kh = (kv_in @ wk + bk).reshape(b, t, H, K)
            vh = (kv_in @ wv + bv).reshape(b, t, H, K)
            kh = jnp.concatenate([kh, jnp.broadcast_to(bias_k, (b, 1, H, K))], axis=1)
            vh = jnp.concatenate([vh, jnp.broadcast_to(bias_v, (b, 1, H, K))], axis=1)
            scale = jnp.sqrt(jnp.asarray(K, q_in.dtype))
            logits = jnp.einsum('bqhk,bthk->bhqt', qh, kh) / scale
            weights = jax.nn.softmax(logits, axis=-1)
            ctx = jnp.einsum('bhqt,bthk->bqhk', weights, vh).reshape(b, q_len, H * K)
            return ctx @ wo + bo

        def _forward(x, xf_1, xf_2, ln1_scale, ln1_offset, wq1, bq1, wk1, bk1, wv1, bv1, wo1, bo1, bias_k1, bias_v1, ln2_scale, ln2_offset, wq2, bq2, wk2, bk2, wv2, bv2, wo2, bo2, bias_k2, bias_v2, ln_mlp_scale, ln_mlp_offset, w_fc1, b_fc1, w_fc2, b_fc2):
            res = x
            h = _layer_norm(x, ln1_scale, ln1_offset)
            x = res + _cross_attention(h, xf_1, wq1, bq1, wk1, bk1, wv1, bv1, wo1, bo1, bias_k1, bias_v1)
            res = x
            h = _layer_norm(x, ln2_scale, ln2_offset)
            x = res + _cross_attention(h, xf_2, wq2, bq2, wk2, bk2, wv2, bv2, wo2, bo2, bias_k2, bias_v2)
            h = _layer_norm(x, ln_mlp_scale, ln_mlp_offset)
            h = jax.nn.gelu(h @ w_fc1 + b_fc1, approximate=False) @ w_fc2 + b_fc2
            return x + h
        return _forward(x, xf_1, xf_2, ln1_scale, ln1_offset, wq1, bq1, wk1, bk1, wv1, bv1, wo1, bo1, bias_k1, bias_v1, ln2_scale, ln2_offset, wq2, bq2, wk2, bk2, wv2, bv2, wo2, bo2, bias_k2, bias_v2, ln_mlp_scale, ln_mlp_offset, w_fc1, b_fc1, w_fc2, b_fc2)

    def _L1_xattn_ref(hidden_state, encoder_hidden_state, encoder_attention_mask, Wq, bq, Wk, bk, Wv, bv, Wo, bo, gamma, beta):
        import jax, jax.numpy as jnp
        import numpy as np
        H = 256
        NH = 32
        KVH = 8
        HD = H // NH
        GROUPS = NH // KVH
        EPS = 1e-06
        B, L, S = (4, 128, 128)

        def _gqa_forward(hidden_state, encoder_hidden_state, encoder_attention_mask, Wq, bq, Wk, bk, Wv, bv, Wo, bo, gamma, beta):
            b, l, _ = hidden_state.shape
            s = encoder_hidden_state.shape[1]
            q = hidden_state @ Wq + bq
            k = encoder_hidden_state @ Wk + bk
            v = encoder_hidden_state @ Wv + bv
            q = q.reshape(b, l, KVH, GROUPS, HD).transpose(0, 2, 3, 1, 4)
            k = k.reshape(b, s, KVH, HD).transpose(0, 2, 1, 3)
            v = v.reshape(b, s, KVH, HD).transpose(0, 2, 1, 3)
            scale = 1.0 / jnp.sqrt(jnp.asarray(HD, q.dtype))
            scores = jnp.einsum('bkgld,bksd->bkgls', q, k) * scale
            scores = scores + encoder_attention_mask[:, :, None, :, :]
            attn = jax.nn.softmax(scores, axis=-1)
            out = jnp.einsum('bkgls,bksd->bkgld', attn, v)
            out = out.transpose(0, 3, 1, 2, 4).reshape(b, l, H)
            out = out @ Wo + bo
            x = out + hidden_state
            mu = jnp.mean(x, axis=-1, keepdims=True)
            var = jnp.var(x, axis=-1, keepdims=True)
            return (x - mu) * jax.lax.rsqrt(var + EPS) * gamma + beta
        return _gqa_forward(hidden_state, encoder_hidden_state, encoder_attention_mask, Wq, bq, Wk, bk, Wv, bv, Wo, bo, gamma, beta)

    def _L2_xattn_ref(x_c, x_s, Wn, bn, Wm, bm, Wl, bl, Wo, bo):
        import jax, jax.numpy as jnp
        import numpy as np
        EPS = 1e-05

        def _inorm(x):
            m = jnp.mean(x, axis=-1, keepdims=True)
            v = jnp.var(x, axis=-1, keepdims=True)
            return (x - m) * jax.lax.rsqrt(v + EPS)

        def _conv1x1(W, b, x):
            return jnp.einsum('oc,bct->bot', W, x) + b[None, :, None]
        Mn = _conv1x1(Wn, bn, _inorm(x_c))
        Mm = _conv1x1(Wm, bm, _inorm(x_s))
        A = jax.nn.softmax(jnp.einsum('bct,bcs->bts', Mn, Mm), axis=-1)
        Ml = _conv1x1(Wl, bl, x_s)
        Mo = jnp.einsum('bcs,bts->bct', Ml, A)
        return _conv1x1(Wo, bo, Mo) + x_c

    def _L3_xattn_ref(hidden_states, encoder_states, ltor_mask, cross_mask, ln1_s, ln1_b, w_qkv, b_qkv, w_ao, b_ao, ln2_s, ln2_b, w_q, b_q, w_kv, b_kv, w_co, b_co, ln3_s, ln3_b, w1, b1, w2, b2):
        import jax, jax.numpy as jnp
        import numpy as np
        H = 256
        NH = 16
        HD = H // NH
        EPS = 1e-05

        def gelu(x):
            return 0.5 * x * (1.0 + jnp.tanh(0.7978845608028654 * x * (1.0 + 0.044715 * x * x)))

        def layernorm(x, scale, bias):
            m = jnp.mean(x, axis=-1, keepdims=True)
            v = jnp.mean(jnp.square(x - m), axis=-1, keepdims=True)
            return (x - m) * jax.lax.rsqrt(v + EPS) * scale + bias

        def split_heads(x):
            b, s, _ = x.shape
            return x.reshape(b, s, NH, HD).transpose(0, 2, 1, 3)

        def merge_heads(x):
            b, nh, s, hd = x.shape
            return x.transpose(0, 2, 1, 3).reshape(b, s, nh * hd)

        def attention(q, k, v, mask):
            scores = jnp.einsum('bhqd,bhkd->bhqk', q, k) / jnp.sqrt(jnp.float32(HD))
            scores = scores * mask - 10000.0 * (1.0 - mask)
            probs = jax.nn.softmax(scores, axis=-1)
            return jnp.einsum('bhqk,bhkd->bhqd', probs, v)
        ln_out = layernorm(hidden_states, ln1_s, ln1_b)
        qkv = ln_out @ w_qkv + b_qkv
        q, k, v = jnp.split(qkv, 3, axis=-1)
        ctx = merge_heads(attention(split_heads(q), split_heads(k), split_heads(v), ltor_mask))
        attn_out = ctx @ w_ao + b_ao
        x = hidden_states + attn_out
        ln_out = layernorm(x, ln2_s, ln2_b)
        q = ln_out @ w_q + b_q
        kv = encoder_states @ w_kv + b_kv
        k, v = jnp.split(kv, 2, axis=-1)
        ctx = merge_heads(attention(split_heads(q), split_heads(k), split_heads(v), cross_mask))
        cross_out = ctx @ w_co + b_co
        x = x + cross_out
        ln_out = layernorm(x, ln3_s, ln3_b)
        mlp_out = gelu(ln_out @ w1 + b1) @ w2 + b2
        return x + mlp_out
    x = _L0_xattn_ref(x, ctx_2048, ctx_2048, L0_xattn_ln1_scale, L0_xattn_ln1_offset, L0_xattn_wq1, L0_xattn_bq1, L0_xattn_wk1, L0_xattn_bk1, L0_xattn_wv1, L0_xattn_bv1, L0_xattn_wo1, L0_xattn_bo1, L0_xattn_bias_k1, L0_xattn_bias_v1, L0_xattn_ln2_scale, L0_xattn_ln2_offset, L0_xattn_wq2, L0_xattn_bq2, L0_xattn_wk2, L0_xattn_bk2, L0_xattn_wv2, L0_xattn_bv2, L0_xattn_wo2, L0_xattn_bo2, L0_xattn_bias_k2, L0_xattn_bias_v2, L0_xattn_ln_mlp_scale, L0_xattn_ln_mlp_offset, L0_xattn_w_fc1, L0_xattn_b_fc1, L0_xattn_w_fc2, L0_xattn_b_fc2)
    x = _L1_xattn_ref(x, ctx_2048, mask_Bx1xSxS2_ff0, L1_xattn_Wq, L1_xattn_bq, L1_xattn_Wk, L1_xattn_bk, L1_xattn_Wv, L1_xattn_bv, L1_xattn_Wo, L1_xattn_bo, L1_xattn_gamma, L1_xattn_beta)
    x = _L2_xattn_ref(x, ctx_2048, L2_xattn_Wn, L2_xattn_bn, L2_xattn_Wm, L2_xattn_bm, L2_xattn_Wl, L2_xattn_bl, L2_xattn_Wo, L2_xattn_bo)
    x = _L3_xattn_ref(x, ctx_2048, mask_1x1xSxS2_fc1, mask_Bx1xSxS2_ff1, L3_xattn_ln1_s, L3_xattn_ln1_b, L3_xattn_w_qkv, L3_xattn_b_qkv, L3_xattn_w_ao, L3_xattn_b_ao, L3_xattn_ln2_s, L3_xattn_ln2_b, L3_xattn_w_q, L3_xattn_b_q, L3_xattn_w_kv, L3_xattn_b_kv, L3_xattn_w_co, L3_xattn_b_co, L3_xattn_ln3_s, L3_xattn_ln3_b, L3_xattn_w1, L3_xattn_b1, L3_xattn_w2, L3_xattn_b2)
    return x

_drawn_inputs = setup_inputs


def setup_inputs(seed=0):
    import zlib

    import numpy as np

    out = dict(_drawn_inputs(seed))
    spreads = {'L0_xattn_ln1_scale': (1.0, 0.6),
     'L0_xattn_ln1_offset': (0.0, 0.8),
     'L0_xattn_bq1': (0.0, 0.8),
     'L0_xattn_bk1': (0.0, 0.8),
     'L0_xattn_bv1': (0.0, 0.1),
     'L0_xattn_bo1': (0.0, 0.1),
     'L0_xattn_ln2_scale': (1.0, 0.6),
     'L0_xattn_ln2_offset': (0.0, 0.8),
     'L0_xattn_bq2': (0.0, 0.8),
     'L0_xattn_bk2': (0.0, 0.8),
     'L0_xattn_bv2': (0.0, 0.1),
     'L0_xattn_bo2': (0.0, 0.1),
     'L0_xattn_ln_mlp_scale': (1.0, 0.2),
     'L0_xattn_ln_mlp_offset': (0.0, 0.304),
     'L0_xattn_b_fc1': (0.0, 0.1),
     'L0_xattn_b_fc2': (0.0, 0.1),
     'L1_xattn_bq': (0.0, 0.8),
     'L1_xattn_bk': (0.0, 2.0),
     'L1_xattn_bv': (0.0, 0.1),
     'L1_xattn_bo': (0.0, 0.1),
     'L1_xattn_gamma': (1.0, 0.2),
     'L1_xattn_beta': (0.0, 0.1),
     'L3_xattn_ln1_s': (1.0, 0.6),
     'L3_xattn_ln1_b': (0.0, 0.8),
     'L3_xattn_b_qkv': (0.0, 0.419),
     'L3_xattn_b_ao': (0.0, 0.1),
     'L3_xattn_ln2_s': (1.0, 0.6),
     'L3_xattn_ln2_b': (0.0, 2.0),
     'L3_xattn_b_q': (0.0, 2.0),
     'L3_xattn_b_kv': (0.0, 0.429),
     'L3_xattn_b_co': (0.0, 0.1),
     'L3_xattn_ln3_s': (1.0, 0.6),
     'L3_xattn_ln3_b': (0.0, 0.8),
     'L3_xattn_b1': (0.0, 0.367),
     'L3_xattn_b2': (0.0, 0.1)}
    factors = {'L0_xattn_wq1': 6.057,
     'L0_xattn_wk1': 5.436,
     'L0_xattn_bias_k1': 39.572,
     'L0_xattn_bias_v1': 8.0,
     'L0_xattn_wq2': 5.941,
     'L0_xattn_wk2': 5.423,
     'L0_xattn_bias_k2': 55.189,
     'L0_xattn_bias_v2': 22.405,
     'L1_xattn_Wq': 8.0,
     'L1_xattn_Wk': 8.0,
     'L2_xattn_bm': 64.0,
     'L3_xattn_w_qkv': 3.302,
     'L3_xattn_w_q': 64.0}
    for name, (base, spread) in spreads.items():
        noise = np.random.default_rng([zlib.crc32(name.encode()), seed]).standard_normal(out[name].shape)
        drawn = base * np.exp(spread * noise) if base else spread * noise
        out[name] = jnp.asarray(drawn.astype(out[name].dtype))
    for name, factor in factors.items():
        out[name] = (out[name] * factor).astype(out[name].dtype)
    return out
```

```python
from contextlib import ExitStack

import numpy as np
import concourse.bass as bass
from concourse import mybir

F32 = mybir.dt.float32
F32R = mybir.dt.float32r
ALU = mybir.AluOpType
ACT = mybir.ActivationFunctionType
AX = mybir.AxisListType.X

P = 128
BATCH, SEQ, D = 32, 64, 256
TOK = BATCH * SEQ
NT = TOK // P
GT = 4
NG = NT // GT
GN = GT * P
CH = D // P
HB = P // SEQ


class Chip:

    def __init__(self, nc, inputs, stack):
        self.nc, self.inputs, self.stack = nc, inputs, stack
        self.stage_sems = []
        self.x = self.sb("x", [P, NT, D])
        self.ident = self.sb("ident", [P, P])
        self.one = self.sb("one", [P, 1])
        self.eps = self.sb("eps", [P, 2])
        self.ctx_hi = self.sb("ctx_hi", [P, CH, TOK], F32R)
        self.ctx_lo = self.sb("ctx_lo", [P, CH, TOK], F32R)
        self.h_hi = self.sb("h_hi", [P, CH, TOK], F32R)
        self.h_lo = self.sb("h_lo", [P, CH, TOK], F32R)

    def sb(self, name, shape, dtype=F32, stack=None):
        return (stack or self.stack).enter_context(self.nc.sbuf_tensor(name, shape, dtype))

    def ps(self, name, shape, stack):
        return stack.enter_context(self.nc.psum_tensor(name, shape, F32))

    def sem(self, name):
        self.stage_sems.append(self.nc.alloc_semaphore(name=name))
        return self.stage_sems[-1]

    def end_stage(self):
        self.nc.clear_and_free_semaphores(self.stage_sems)
        self.nc.all_engine_barrier()
        self.stage_sems = []


def product(pe, out, wh, wl, mh, ml, start=True, stop=True):
    pe.matmul(out, wh, mh, start=start, stop=False)
    pe.matmul(out, wh, ml, start=False, stop=False)
    return pe.matmul(out, wl, mh, start=False, stop=stop)


def columns(vector):
    return vector.rearrange("(c p) -> p c", p=P)


def load(chip):
    nc, I = chip.nc, chip.inputs
    with ExitStack() as stack:
        rows = chip.sb("ctx_rows", [P, NT, D], F32, stack)
        turned = [chip.ps(f"ctx_turned{i}", [P, CH, GN], stack) for i in range(2)]
        x_in = chip.sem("x_in")
        rows_in = [chip.sem(f"ctx_rows_in{g}") for g in range(NG)]
        eps_set, ident_set = chip.sem("eps_set"), chip.sem("ident_set")
        ctx_turned = chip.sem("ctx_turned")
        hi_done, lo_done = chip.sem("ctx_hi_done"), chip.sem("ctx_lo_done")
        x_rows = I["x"].rearrange("b s d -> (b s) d").rearrange("(t p) d -> p t d", p=P)
        ctx_rows = I["ctx_2048"].rearrange("b s d -> (b s) d").rearrange("(t p) d -> p t d", p=P)

        with nc.Block() as block:
            @block.sync
            def _(sp):
                for g in range(NG):
                    sp.dma_start(rows[:, g * GT:(g + 1) * GT, :],
                                 ctx_rows[:, g * GT:(g + 1) * GT, :]).then_inc(rows_in[g], 16)
                sp.dma_start(chip.x[:], x_rows).then_inc(x_in, 16)
                sp.wait_ge(x_in, 16)

            @block.gpsimd
            def _(pool):
                pool.memset(chip.one[:], 1.0)
                pool.memset(chip.eps[:, 0:1], 1e-5)
                pool.memset(chip.eps[:, 1:2], 1e-6)
                pool.memset(chip.ident[:], 0.0).then_inc(ident_set, 1)
                pool.wait_ge(ident_set, 1)
                pool.affine_select(out=chip.ident[:], in_=chip.ident[:], compare_op=ALU.not_equal, fill=1.0,
                                   base=0, pattern=[[-1, P]], channel_multiplier=1).then_inc(ident_set, 1)

            @block.tensor
            def _(pe):
                pe.wait_ge(ident_set, 2)
                for g in range(NG):
                    pe.wait_ge(rows_in[g], 16)
                    if g >= 2:
                        pe.wait_ge(hi_done, CH * (g - 1))
                        pe.wait_ge(lo_done, CH * (g - 1))
                    for c in range(CH):
                        for j in range(GT):
                            last = pe.transpose(turned[g % 2][:, c, j * P:(j + 1) * P],
                                                rows[:, g * GT + j, c * P:(c + 1) * P], chip.ident[:])
                        last.then_inc(ctx_turned, 1)

            @block.scalar
            def _(act):
                for g in range(NG):
                    for c in range(CH):
                        act.wait_ge(ctx_turned, CH * g + c + 1)
                        act.activation(chip.ctx_hi[:, c, g * GN:(g + 1) * GN], turned[g % 2][:, c, :],
                                       ACT.Copy).then_inc(hi_done, 1)

            @block.vector
            def _(dve):
                for g in range(NG):
                    for c in range(CH):
                        dve.wait_ge(hi_done, CH * g + c + 1)
                        dve.tensor_tensor(chip.ctx_lo[:, c, g * GN:(g + 1) * GN], turned[g % 2][:, c, :],
                                          chip.ctx_hi[:, c, g * GN:(g + 1) * GN].bitcast(F32),
                                          ALU.subtract).then_inc(lo_done, 1)


def turn_input(chip, tag, scale=None, offset=None):
    nc = chip.nc
    norm = scale is not None
    with ExitStack() as stack:
        def sb(name, shape, dtype=F32):
            return chip.sb(f"{tag}_{name}", shape, dtype, stack)
        stats, moments = sb("stats", [P, GT, 6]), sb("moments", [P, GT, 2])
        spread, inverse = sb("spread", [P, GT]), sb("inverse", [P, GT])
        rows = sb("rows", [P, GT, D])
        idle = sb("idle", [P, 1])
        whole = sb("whole", [P, CH, GN])
        gain = sb("gain", [P, 2, CH])
        turned = chip.ps(f"{tag}_turned", [P, CH, GN], stack)
        gain_in = chip.sem(f"{tag}_gain_in")
        stats_done, moments_done = chip.sem(f"{tag}_stats"), chip.sem(f"{tag}_moments")
        spread_done, inverse_done = chip.sem(f"{tag}_spread"), chip.sem(f"{tag}_inverse")
        rows_done, turned_done = chip.sem(f"{tag}_rows_done"), chip.sem(f"{tag}_turned_done")
        hi_done, whole_done, lo_done = (chip.sem(f"{tag}_{n}") for n in ("hi_done", "whole_done", "lo_done"))

        with nc.Block() as block:
            @block.sync
            def _(sp):
                if norm:
                    sp.dma_start(gain[:, 0, :], columns(scale), allow_slow_non_contiguous=True).then_inc(gain_in, 16)
                    sp.dma_start(gain[:, 1, :], columns(offset), allow_slow_non_contiguous=True).then_inc(gain_in, 16)
                    sp.wait_ge(gain_in, 32)

            @block.vector
            def _(dve):
                if norm:
                    dve.wait_ge(gain_in, 32)
                with dve.Fori(0, NG) as g:
                    if norm:
                        for j in range(GT):
                            dve.bn_stats(stats[:, j, :], chip.x[:, bass.ds(g * GT + j, 1), :]
                                         .rearrange("p a d -> p (a d)")).then_inc(stats_done, 1)
                        dve.wait_ge(stats_done, g * GT + GT)
                        dve.memset(idle[:], 0.0)
                        for j in range(GT):
                            dve.bn_aggr(moments[:, j, :], stats[:, j, :]).then_inc(moments_done, 1)
                        dve.wait_ge(spread_done, g + 1)
                        dve.reciprocal(inverse[:], spread[:]).then_inc(inverse_done, 1)
                        dve.wait_ge(inverse_done, g + 1)
                    for j in range(GT):
                        tile = chip.x[:, bass.ds(g * GT + j, 1), :].rearrange("p a d -> p (a d)")
                        if norm:
                            dve.tensor_scalar(rows[:, j, :], tile, moments[:, j, 0:1], inverse[:, j:j + 1],
                                              ALU.subtract, ALU.mult).then_inc(rows_done, 1)
                        else:
                            dve.tensor_copy(rows[:, j, :], tile).then_inc(rows_done, 1)
                    for c in range(CH):
                        dve.wait_ge(hi_done, g * CH + c + 1)
                        if norm:
                            dve.tensor_scalar(whole[:, c, :], turned[:, c, :], gain[:, 0, c:c + 1],
                                              gain[:, 1, c:c + 1], ALU.mult, ALU.add).then_inc(whole_done, 1)
                        else:
                            dve.tensor_copy(whole[:, c, :], turned[:, c, :]).then_inc(whole_done, 1)
                    for c in range(CH):
                        dve.wait_ge(whole_done, g * CH + c + 1)
                        dve.tensor_tensor(chip.h_lo[:, c, bass.ds(g * GN, GN)], whole[:, c, :],
                                          chip.h_hi[:, c, bass.ds(g * GN, GN)].bitcast(F32),
                                          ALU.subtract).then_inc(lo_done, 1)

            @block.scalar
            def _(act):
                if norm:
                    act.wait_ge(gain_in, 32)
                with act.Fori(0, NG) as g:
                    if norm:
                        act.wait_ge(moments_done, g * GT + GT)
                        act.activation(spread[:], moments[:, :, 1], ACT.Sqrt,
                                       bias=chip.eps[:, 0:1]).then_inc(spread_done, 1)
                    for c in range(CH):
                        act.wait_ge(turned_done, g * CH + c + 1)
                        if norm:
                            act.activation(chip.h_hi[:, c, bass.ds(g * GN, GN)], turned[:, c, :], ACT.Identity,
                                           bias=gain[:, 1, c:c + 1], scale=gain[:, 0, c:c + 1]).then_inc(hi_done, 1)
                        else:
                            act.activation(chip.h_hi[:, c, bass.ds(g * GN, GN)], turned[:, c, :],
                                           ACT.Copy).then_inc(hi_done, 1)

            @block.tensor
            def _(pe):
                with pe.Fori(0, NG) as g:
                    for c in range(CH):
                        for j in range(GT):
                            if c == 0:
                                pe.wait_ge(rows_done, g * GT + j + 1)
                            last = pe.transpose(turned[:, c, j * P:(j + 1) * P],
                                                rows[:, j, c * P:(c + 1) * P], chip.ident[:])
                        last.then_inc(turned_done, 1)
                    pe.wait_ge(hi_done, g * CH + CH)
                    pe.wait_ge(whole_done, g * CH + CH)


def store(chip, out):
    rows = out.rearrange("b s d -> (b s) d").rearrange("(t p) d -> p t d", p=P)
    stored = chip.sem("stored")
    with chip.nc.Block() as block:
        @block.sync
        def _(sp):
            sp.dma_start(rows, chip.x[:]).then_inc(stored, 16)
            sp.wait_ge(stored, 16)


def wide_attention(chip, tag, n):
    nc = chip.nc
    H, K = 16, 128
    SCALE = 1.0 / float(np.sqrt(np.float32(K)))
    wt = {k: chip.inputs[f"L0_xattn_{k}{n}"] for k in ("wq", "wk", "wv", "wo", "bq", "bk", "bv", "bo", "bias_k", "bias_v")}
    wq_d, wk_d, wv_d = (wt[k].rearrange("(c p) n -> p c n", p=P) for k in ("wq", "wk", "wv"))
    wo_d = wt["wo"].rearrange("(h d) n -> d h n", d=K)
    bias_k_row = wt["bias_k"].rearrange("a b h k -> (a b) (h k)")
    VW = 32

    with ExitStack() as keep:
        def sbk(name, shape, dtype=F32):
            return chip.sb(f"{tag}_{name}", shape, dtype, keep)
        bias_cols = sbk("bias_cols", [P, 4, H])
        learned_logit = sbk("learned_logit", [P, NT, H])
        learned_weight = sbk("learned_weight", [P, NT, VW])
        value_rows = sbk("value_rows", [P, D])

        with ExitStack() as stack:
            def sb(name, shape, dtype=F32):
                return chip.sb(f"{tag}_{name}", shape, dtype, stack)
            wq_all = sb("wq_all", [P, CH, H * K])
            wo_all = sb("wo_all", [P, H, D])
            key_all, bq_all = sb("key_all", [P, H * K]), sb("bq_all", [P, H * K])
            bias_rows = sb("bias_rows", [H, 4, K])
            u, u_hi, u_lo = sb("u", [P, CH, H]), sb("u_hi", [P, CH, H], F32R), sb("u_lo", [P, CH, H], F32R)
            logit_bias = sb("logit_bias", [P, H])
            spread_v = sb("spread_v", [P, H, P])
            bo_rows = sb("bo_rows", [P, D])
            cols_ps = chip.ps(f"{tag}_cols_ps", [P, 4, H], stack)
            logit_ps = chip.ps(f"{tag}_logit_ps", [P, NT, H], stack)
            value_ps = chip.ps(f"{tag}_value_ps", [P, D], stack)
            wq_in, key_in, bq_in, wo_in, rows_in, bo_in = (
                chip.sem(f"{tag}_{s}_in") for s in ("wq", "key", "bq", "wo", "rows", "bo"))
            zeroed, cols_turned, cols_done = (chip.sem(f"{tag}_{s}") for s in ("zeroed", "cols_turned", "cols_done"))
            u_step, c_step, v_step = (chip.sem(f"{tag}_{s}") for s in ("u_step", "c_step", "v_step"))
            logits_done, values_done, kept = (chip.sem(f"{tag}_{s}") for s in ("logits_done", "values_done", "kept"))

            with nc.Block() as block:
                @block.sync
                def _(sp):
                    sp.dma_start(wq_all[:], wq_d).then_inc(wq_in, 16)
                    sp.dma_start(key_all[:], bias_k_row.to_broadcast([P, H * K])).then_inc(key_in, 16)
                    sp.dma_start(bq_all[:], wt["bq"].rearrange("(a n) -> a n", a=1).to_broadcast([P, H * K])).then_inc(bq_in, 16)
                    sp.dma_start(wo_all[:], wo_d).then_inc(wo_in, 16)

                @block.scalar
                def _(act):
                    for i, name in enumerate(("bq", "bk", "bv")):
                        act.dma_start(bias_rows[:, i, :], wt[name].rearrange("(h k) -> h k", k=K)).then_inc(rows_in, 16)
                    act.dma_start(bias_rows[:, 3, :], wt["bias_v"].rearrange("a b h k -> (a b h) k")).then_inc(rows_in, 16)
                    act.wait_ge(zeroed, 3)
                    for r in range(0, P, VW):
                        act.dma_start(bo_rows[r:r + 1, :], wt["bo"].rearrange("(a n) -> a n", a=1)).then_inc(bo_in, 16)
                    act.wait_ge(u_step, 2)
                    act.activation(u_hi[:], u[:], ACT.Copy).then_inc(u_step, 1)

                @block.gpsimd
                def _(pool):
                    pool.memset(spread_v[:], 0.0).then_inc(zeroed, 1)
                    pool.memset(learned_weight[:], 0.0).then_inc(zeroed, 1)
                    pool.memset(bo_rows[:], 0.0).then_inc(zeroed, 1)
                    pool.wait_ge(zeroed, 2)
                    pool.memset(learned_weight[:, :, 0:1], 1.0)

                @block.tensor
                def _(pe):
                    pe.wait_ge(rows_in, 64)
                    for i in range(4):
                        last = pe.transpose(cols_ps[:, i, :], bias_rows[:, i, :], chip.ident[0:H, 0:H])
                    last.then_inc(cols_turned, 1)
                    pe.wait_ge(v_step, 2)
                    pe.wait_ge(wo_in, 16)
                    for h in range(H):
                        last = pe.matmul(value_ps[:], spread_v[:, h, :], wo_all[:, h, :], start=h == 0, stop=h == H - 1)
                    last.then_inc(values_done, 1)
                    pe.wait_ge(u_step, 4)
                    for t in range(NT):
                        for c in range(CH):
                            last = product(pe, logit_ps[:, t, :], chip.h_hi[:, c, t * P:(t + 1) * P],
                                           chip.h_lo[:, c, t * P:(t + 1) * P], u_hi[:, c, :], u_lo[:, c, :],
                                           start=c == 0, stop=c == CH - 1)
                    last.then_inc(logits_done, 1)

                @block.vector
                def _(dve):
                    dve.wait_ge(cols_turned, 1)
                    dve.tensor_copy(bias_cols[:], cols_ps[:]).then_inc(cols_done, 1)
                    dve.wait_ge(cols_done, 1)
                    dve.wait_ge(zeroed, 1)
                    for r in range(0, P, VW):
                        flat = spread_v[:].rearrange("p h c -> p (h c)")
                        dve.tensor_copy(spread_v[:, :, r], bias_cols[:, 2, :])
                        diag = flat[:, r + 1:r + 1 + (P + 1) * (H - 1) + 1:P + 1]
                        last = dve.tensor_tensor(diag, bias_cols[:, 3, :], bias_cols[:, 2, :], ALU.subtract)
                    last.then_inc(v_step, 2)
                    dve.wait_ge(key_in, 16)
                    dve.wait_ge(wq_in, 16)
                    dve.tensor_tensor(wq_all[:], wq_all[:], key_all[:].rearrange("p (a n) -> p a n", a=1)
                                      .to_broadcast([P, CH, H * K]), ALU.mult).then_inc(u_step, 1)
                    dve.wait_ge(u_step, 1)
                    dve.tensor_reduce(u[:], wq_all[:].rearrange("p c (h k) -> p c h k", k=K), AX, ALU.add).then_inc(u_step, 1)
                    dve.wait_ge(bq_in, 16)
                    dve.tensor_tensor(bq_all[:], bq_all[:], key_all[:], ALU.mult).then_inc(c_step, 1)
                    dve.wait_ge(u_step, 3)
                    dve.tensor_tensor(u_lo[:], u[:], u_hi[:].bitcast(F32), ALU.subtract).then_inc(u_step, 1)
                    dve.wait_ge(c_step, 1)
                    dve.tensor_reduce(logit_bias[:], bq_all[:].rearrange("p (h k) -> p h k", k=K), AX, ALU.add).then_inc(c_step, 1)
                    dve.wait_ge(values_done, 1)
                    dve.wait_ge(bo_in, 16 * (P // VW))
                    dve.tensor_tensor(value_rows[:], value_ps[:], bo_rows[:], ALU.add).then_inc(kept, 1)
                    dve.wait_ge(c_step, 2)
                    dve.wait_ge(logits_done, 1)
                    dve.tensor_tensor(learned_logit[:], logit_ps[:], logit_bias[:].rearrange("p (a h) -> p a h", a=1)
                                      .to_broadcast([P, NT, H]), ALU.add).then_inc(kept, 1)

        with ExitStack() as stack:
            def sb(name, shape, dtype=F32):
                return chip.sb(f"{tag}_{name}", shape, dtype, stack)

            def split(name, shape):
                return sb(name + "_hi", shape, F32R), sb(name + "_lo", shape, F32R)
            HP = 2
            ITEMS = HP * NG
            PASSES = H // HP
            raw = [sb(f"raw{p}", [P, 3, CH, K]) for p in range(HP)]
            raw_o = [sb(f"raw_o{p}", [P, D]) for p in range(HP)]
            w = [split(f"w{p}", [P, 3, CH, K]) for p in range(HP)]
            wo = [split(f"wo{p}", [P, D]) for p in range(HP)]
            head_bias = [sb(f"head_bias{p}", [P, 2]) for p in range(HP)]
            q, k = split("q", [P, GN]), split("k", [P, GN])
            v = [split(f"v{p}", [P, GT, K]) for p in range(HP)]
            logit = sb("logit", [P, GT, SEQ + 1])
            expd = sb("expd", [P, GT, SEQ + 1])
            top, total, inverse = sb("top", [P, GT]), sb("total", [P, GT]), sb("inverse", [P, GT])
            weight = sb("weight", [P, GT, P])
            wt_t = split("weight_t", [P, GN])
            c = [split(f"c{p}", [P, GN]) for p in range(HP)]
            q_ps, k_ps, v_ps, s_ps, t_ps, c_ps = (
                chip.ps(f"{tag}_{x}_ps", [P, GN], stack) for x in ("q", "k", "v", "s", "t", "c"))
            o_ps = chip.ps(f"{tag}_o_ps", [P, GT, D], stack)

            raw_in = [chip.sem(f"{tag}_raw_in{p}") for p in range(HP)]
            raw_o_in = [chip.sem(f"{tag}_raw_o_in{p}") for p in range(HP)]
            w_split, wo_split = chip.sem(f"{tag}_w_split"), chip.sem(f"{tag}_wo_split")
            q_made, k_made, v_made, s_made, t_made, c_made, o_made = (
                chip.sem(f"{tag}_{x}_made") for x in "qkvstco")
            q_hi, k_hi, v_hi, t_hi, c_hi, s_half, exp_done = (
                chip.sem(f"{tag}_{x}") for x in ("q_hi", "k_hi", "v_hi", "t_hi", "c_hi", "s_half", "exp_done"))
            q_lo, k_lo, v_lo, t_lo, c_lo, s_rest, top_done, total_done, inverse_done, weight_a, added = (
                chip.sem(f"{tag}_{x}") for x in ("q_lo", "k_lo", "v_lo", "t_lo", "c_lo", "s_rest", "top_done",
                                                 "total_done", "inverse_done", "weight_a", "added"))
            s_learned, shifted, weight_b, zero_done = (
                chip.sem(f"{tag}_{x}") for x in ("s_learned", "shifted", "weight_b", "zero_done"))

            def tiles(j):
                g = (j % ITEMS) // HP
                return slice(g * GT, (g + 1) * GT), slice(g * GN, (g + 1) * GN)

            def passes(engine, slots):
                slots(0, 0, True, False)
                with engine.Fori(0, PASSES - 1) as i:
                    for j in range(1, ITEMS + 1):
                        slots(i, j, True, True)
                for j in range(1, ITEMS + 1):
                    slots(PASSES - 1, j, j < ITEMS, True)

            with nc.Block() as block:
                @block.sync
                def _(sp):
                    def fetch(p, cols):
                        for x, src in enumerate((wq_d, wk_d, wv_d)):
                            sp.dma_start(raw[p][:, x, :, :], src[:, :, cols]).then_inc(raw_in[p], 16)
                        sp.dma_start(raw_o[p][:], wt["wo"][cols, :]).then_inc(raw_o_in[p], 16)
                    for p in range(HP):
                        fetch(p, slice(p * K, (p + 1) * K))
                    with sp.Fori(1, PASSES) as i:
                        starts = [sp.snap((i * HP + p) * K) for p in range(HP)]
                        ends = sp.snap(i * HP)
                        sp.wait_ge(w_split, ends)
                        sp.wait_ge(wo_split, ends)
                        for p in range(HP):
                            fetch(p, bass.ds(starts[p], K))
                    for p in range(HP):
                        sp.wait_ge(raw_in[p], 48 * PASSES)
                        sp.wait_ge(raw_o_in[p], 16 * PASSES)

                @block.gpsimd
                def _(pool):
                    def split_w(i, p):
                        pool.wait_ge(raw_in[p], i * 48 + 48)
                        pool.tensor_tensor(w[p][0][:].rearrange("p x c k -> p (x c k)"), raw[p][:].rearrange("p x c k -> p (x c k)"),
                                           chip.one[:].to_broadcast([P, 3 * CH * K]), ALU.mult).then_inc(hi_step, 1)
                        pool.tensor_copy(head_bias[p][:], bias_cols[:, 0:2, bass.ds(i * HP + p, 1)]
                                         .rearrange("p a b -> p (a b)"))
                        pool.wait_ge(hi_step, i * HP + p + 1)
                        pool.tensor_tensor(w[p][1][:], raw[p][:], w[p][0][:].bitcast(F32),
                                           ALU.subtract).then_inc(w_split, 1)

                    def split_wo(i):
                        for p in range(HP):
                            pool.wait_ge(raw_o_in[p], i * 16 + 16)
                            pool.tensor_tensor(wo[p][0][:], raw_o[p][:], chip.one[:].to_broadcast([P, D]), ALU.mult).then_inc(hi_step_o, 1)
                        for p in range(HP):
                            pool.wait_ge(hi_step_o, i * HP + p + 1)
                            pool.tensor_tensor(wo[p][1][:], raw_o[p][:], wo[p][0][:].bitcast(F32),
                                               ALU.subtract).then_inc(wo_split, 1)

                    def slots(i, j, this, prev):
                        n = i * ITEMS + j
                        if j == 0:
                            for p in range(HP):
                                split_w(0, p)
                        if prev:
                            rows, _ = tiles(j - 1)
                            head = i * HP + (j - 1) % HP
                            pool.tensor_copy(logit[:, :, SEQ:SEQ + 1],
                                             learned_logit[:, rows, bass.ds(head, 1)]).then_inc(s_learned, 1)
                            pool.wait_ge(top_done, n)
                            pool.tensor_tensor(logit[:], logit[:], top[:].rearrange("p (t a) -> p t a", a=1)
                                               .to_broadcast([P, GT, SEQ + 1]), ALU.subtract).then_inc(shifted, 1)
                            if j == 1:
                                if this:
                                    pool.wait_ge(q_made, n + 1)
                                split_wo(i)
                            pool.wait_ge(inverse_done, n)
                            pool.wait_ge(wo_split, i * HP + HP)
                            pool.tensor_tensor(weight[SEQ:P, :, SEQ:P], expd[SEQ:P, :, 0:SEQ],
                                               inverse[SEQ:P].rearrange("p (t a) -> p t a", a=1)
                                               .to_broadcast([SEQ, GT, SEQ]), ALU.mult).then_inc(weight_b, 1)
                            pool.wait_ge(weight_b, n)
                        more = not (isinstance(i, int) and i == PASSES - 1)
                        if more and j >= ITEMS - 1:
                            pool.wait_ge(v_made, n)
                            split_w(i + 1, j - ITEMS + 1)

                    hi_step, hi_step_o = chip.sem(f"{tag}_w_hi"), chip.sem(f"{tag}_wo_hi")
                    pool.memset(weight[:], 0.0).then_inc(zero_done, 1)
                    passes(pool, slots)

                @block.tensor
                def _(pe):
                    def slots(i, j, this, prev):
                        n = i * ITEMS + j
                        p, pp = j % HP, (j - 1) % HP
                        _, cols = tiles(j)
                        if this:
                            if j == 0:
                                pe.wait_ge(w_split, 1)
                            elif j == 1 or j == ITEMS:
                                pe.wait_ge(w_split, i * HP + (j if j == 1 else HP) + 1)
                            for x, (out, hi, lo, made) in enumerate(((q_ps, q_hi, q_lo, q_made), (k_ps, k_hi, k_lo, k_made))):
                                if j > 0:
                                    pe.wait_ge(hi, n)
                                    pe.wait_ge(lo, n)
                                src = (chip.h_hi, chip.h_lo) if x == 0 else (chip.ctx_hi, chip.ctx_lo)
                                for ch in range(CH):
                                    last = product(pe, out[:], w[p][0][:, x, ch, :], w[p][1][:, x, ch, :],
                                                   src[0][:, ch, cols], src[1][:, ch, cols],
                                                   start=ch == 0, stop=ch == CH - 1)
                                last.then_inc(made, 1)
                            if j > 0:
                                pe.wait_ge(v_hi, n)
                                pe.wait_ge(v_lo, n)
                            for t in range(GT):
                                tok = slice(cols.start + t * P, cols.start + (t + 1) * P)
                                for ch in range(CH):
                                    last = product(pe, v_ps[:, t * K:(t + 1) * K], chip.ctx_hi[:, ch, tok],
                                                   chip.ctx_lo[:, ch, tok], w[p][0][:, 2, ch, :], w[p][1][:, 2, ch, :],
                                                   start=ch == 0, stop=ch == CH - 1)
                            last.then_inc(v_made, 1)
                        if prev:
                            pe.wait_ge(weight_a, n)
                            pe.wait_ge(weight_b, n)
                            for t in range(GT):
                                last = pe.transpose(t_ps[:, t * P:(t + 1) * P], weight[:, t, :], chip.ident[:])
                            last.then_inc(t_made, 1)
                        if this:
                            for ready in (q_hi, q_lo, k_hi, k_lo):
                                pe.wait_ge(ready, n + 1)
                            if j > 0:
                                pe.wait_ge(s_half, n)
                                pe.wait_ge(s_rest, n)
                            for t in range(GT):
                                tok = slice(t * P, (t + 1) * P)
                                last = product(pe, s_ps[:, tok], q[0][:, tok], q[1][:, tok], k[0][:, tok], k[1][:, tok])
                            last.then_inc(s_made, 1)
                        if prev:
                            for ready in (t_hi, t_lo, v_hi, v_lo):
                                pe.wait_ge(ready, n)
                            for t in range(GT):
                                tok = slice(t * P, (t + 1) * P)
                                last = product(pe, c_ps[:, tok], v[pp][0][:, t, :], v[pp][1][:, t, :],
                                               wt_t[0][:, tok], wt_t[1][:, tok])
                            last.then_inc(c_made, 1)
                            if pp == HP - 1:
                                pe.wait_ge(c_hi, n)
                                pe.wait_ge(c_lo, n)
                                pe.wait_ge(wo_split, i * HP + HP)
                                for t in range(GT):
                                    tok = slice(t * P, (t + 1) * P)
                                    for x in range(HP):
                                        last = product(pe, o_ps[:, t, :], c[x][0][:, tok], c[x][1][:, tok],
                                                       wo[x][0][:], wo[x][1][:], start=x == 0, stop=x == HP - 1)
                                last.then_inc(o_made, 1)
                    passes(pe, slots)

                @block.scalar
                def _(act):
                    def slots(i, j, this, prev):
                        n = i * ITEMS + j
                        p, pp = j % HP, (j - 1) % HP
                        if prev:
                            act.wait_ge(s_made, n)
                            act.activation(logit[SEQ:P, :, 0:SEQ], s_ps[SEQ:P, :].rearrange("p (t k) -> p t k", t=GT)
                                           [:, :, SEQ:P], ACT.Copy).then_inc(s_half, 1)
                        if this:
                            act.wait_ge(q_made, n + 1)
                            act.activation(q[0][:], q_ps[:], ACT.Identity, bias=head_bias[p][:, 0:1]).then_inc(q_hi, 1)
                        if prev:
                            act.wait_ge(shifted, n)
                            act.activation(expd[:], logit[:], ACT.Exp, scale=SCALE).then_inc(exp_done, 1)
                        if this:
                            act.wait_ge(k_made, n + 1)
                            act.activation(k[0][:], k_ps[:], ACT.Identity, bias=head_bias[p][:, 1:2]).then_inc(k_hi, 1)
                            act.wait_ge(v_made, n + 1)
                            act.activation(v[p][0][:].rearrange("p t k -> p (t k)"), v_ps[:], ACT.Copy).then_inc(v_hi, 1)
                        if prev:
                            act.wait_ge(t_made, n)
                            act.activation(wt_t[0][:], t_ps[:], ACT.Copy).then_inc(t_hi, 1)
                            act.wait_ge(c_made, n)
                            act.activation(c[pp][0][:], c_ps[:], ACT.Copy).then_inc(c_hi, 1)
                    passes(act, slots)

                @block.vector
                def _(dve):
                    def rest(out, ps, bias, hi, made, lo):
                        if bias is None:
                            dve.tensor_tensor(out, ps, hi.bitcast(F32), ALU.subtract).then_inc(lo, 1)
                        else:
                            dve.scalar_tensor_tensor(out, ps, bias, hi.bitcast(F32), ALU.add, ALU.subtract).then_inc(lo, 1)

                    def slots(i, j, this, prev):
                        n = i * ITEMS + j
                        p, pp = j % HP, (j - 1) % HP
                        if prev:
                            dve.wait_ge(s_made, n)
                            dve.tensor_copy(logit[0:SEQ, :, 0:SEQ], s_ps[0:SEQ, :].rearrange("p (t k) -> p t k", t=GT)
                                            [:, :, 0:SEQ]).then_inc(s_rest, 1)
                            dve.wait_ge(s_rest, n)
                            dve.wait_ge(s_half, n)
                            dve.wait_ge(s_learned, n)
                            dve.tensor_reduce(top[:], logit[:], AX, ALU.max).then_inc(top_done, 1)
                        if this:
                            dve.wait_ge(q_hi, n + 1)
                            rest(q[1][:], q_ps[:], head_bias[p][:, 0:1], q[0][:], q_made, q_lo)
                            dve.wait_ge(k_hi, n + 1)
                            rest(k[1][:], k_ps[:], head_bias[p][:, 1:2], k[0][:], k_made, k_lo)
                        if prev:
                            dve.wait_ge(exp_done, n)
                            dve.tensor_reduce(total[:], expd[:], AX, ALU.add).then_inc(total_done, 1)
                            dve.wait_ge(total_done, n)
                            dve.reciprocal(inverse[:], total[:]).then_inc(inverse_done, 1)
                            dve.wait_ge(inverse_done, n)
                            dve.tensor_tensor(weight[0:SEQ, :, 0:SEQ], expd[0:SEQ, :, 0:SEQ],
                                              inverse[0:SEQ].rearrange("p (t a) -> p t a", a=1)
                                              .to_broadcast([SEQ, GT, SEQ]), ALU.mult).then_inc(weight_a, 1)
                            dve.tensor_tensor(learned_weight[:, tiles(j - 1)[0], bass.ds(i * HP + pp + 1, 1)],
                                              expd[:, :, SEQ:SEQ + 1], inverse[:].rearrange("p (t a) -> p t a", a=1),
                                              ALU.mult)
                        if this:
                            dve.wait_ge(v_hi, n + 1)
                            rest(v[p][1][:].rearrange("p t k -> p (t k)"), v_ps[:], None,
                                 v[p][0][:].rearrange("p t k -> p (t k)"), v_made, v_lo)
                        if prev and pp == 0 and j > 1:
                            add_output(i, j - 1)
                        if prev:
                            dve.wait_ge(t_hi, n)
                            rest(wt_t[1][:], t_ps[:], None, wt_t[0][:], t_made, t_lo)
                            dve.wait_ge(c_hi, n)
                            rest(c[pp][1][:], c_ps[:], None, c[pp][0][:], c_made, c_lo)
                        if j == ITEMS:
                            add_output(i, j)

                    def add_output(i, j):
                        rows, _ = tiles(j - 1)
                        dve.wait_ge(o_made, i * NG + j // HP)
                        dve.tensor_tensor(chip.x[:, rows, :], o_ps[:], chip.x[:, rows, :], ALU.add).then_inc(added, 1)

                    dve.wait_ge(zero_done, 1)
                    passes(dve, slots)

        with ExitStack() as stack:
            weights_t = chip.sb(f"{tag}_weights_t", [P, NT // GT, P], F32, stack)
            turn_ps = chip.ps(f"{tag}_turn_ps", [P, NT // GT, P], stack)
            add_ps = [chip.ps(f"{tag}_add_ps{b}", [P, GN], stack) for b in range(GT)]
            turned, taken, tile_made, tile_added = (chip.sem(f"{tag}_{s}") for s in ("turned", "taken", "tile_made", "tile_added"))
            with nc.Block() as block:
                @block.tensor
                def _(pe):
                    for g in range(NG):
                        last = pe.transpose(turn_ps[:, g, :], learned_weight[:, g * GT:(g + 1) * GT, :]
                                            .rearrange("p t w -> p (t w)"), chip.ident[:])
                    last.then_inc(turned, 1)
                    pe.wait_ge(taken, 1)
                    for t in range(NT):
                        if t >= GT:
                            pe.wait_ge(tile_added, t - GT + 1)
                        r = VW * (t % GT)
                        pe.matmul(add_ps[t % GT][:, 0:D], weights_t[r:r + VW, t // GT, :],
                                  value_rows[r:r + VW, :], start=True, stop=True).then_inc(tile_made, 1)

                @block.vector
                def _(dve):
                    dve.wait_ge(turned, 1)
                    dve.tensor_copy(weights_t[:], turn_ps[:]).then_inc(taken, 1)
                    for t in range(NT):
                        dve.wait_ge(tile_made, t + 1)
                        dve.tensor_tensor(chip.x[:, t, :], add_ps[t % GT][:, 0:D], chip.x[:, t, :],
                                          ALU.add).then_inc(tile_added, 1)


def dense_mlp(chip, tag, w1, b1, w2, b2, function):
    nc = chip.nc
    FC = w1.shape[1] // P
    with ExitStack() as stack:
        def sb(name, shape, dtype=F32):
            return chip.sb(f"{tag}_{name}", shape, dtype, stack)
        raw1, raw2 = sb("raw1", [P, CH, FC * P]), sb("raw2", [P, FC, D])
        w1_hi, w1_lo = sb("w1_hi", [P, CH, FC * P], F32R), sb("w1_lo", [P, CH, FC * P], F32R)
        w2_hi, w2_lo = sb("w2_hi", [P, FC, D], F32R), sb("w2_lo", [P, FC, D], F32R)
        b1_rows, b1_cols, b2_row = sb("b1_rows", [FC, P]), sb("b1_cols", [P, FC]), sb("b2_row", [P, D])
        hidden = [sb(f"hidden{b}", [P, GN]) for b in range(2)]
        hidden_hi = [sb(f"hidden_hi{b}", [P, GN], F32R) for b in range(2)]
        hidden_lo = [sb(f"hidden_lo{b}", [P, GN], F32R) for b in range(2)]
        hidden_ps = [chip.ps(f"{tag}_hidden_ps{b}", [P, GN], stack) for b in range(2)]
        out_ps = chip.ps(f"{tag}_out_ps", [P, GT, 512], stack)
        b1_in, b2_in, w1_in, w2_in = (chip.sem(f"{tag}_{s}_in") for s in ("b1", "b2", "w1", "w2"))
        b1_turned, b1_ready, w_hi_done, w_lo_done, b2_added = (
            chip.sem(f"{tag}_{s}") for s in ("b1_turned", "b1_ready", "w_hi_done", "w_lo_done", "b2_added"))
        hidden_made, hidden_done, hi_done, lo_done, used, out_made, out_added = (
            chip.sem(f"{tag}_{s}") for s in ("hidden_made", "hidden_done", "hi_done", "lo_done", "used", "out_made", "out_added"))

        with nc.Block() as block:
            @block.sync
            def _(sp):
                sp.dma_start(b1_rows[:], b1.rearrange("(f p) -> f p", p=P)).then_inc(b1_in, 16)
                sp.dma_start(b2_row[:], b2.rearrange("(a n) -> a n", a=1).to_broadcast([P, D])).then_inc(b2_in, 16)
                sp.dma_start(raw1[:], w1.rearrange("(c p) n -> p c n", p=P)).then_inc(w1_in, 16)
                sp.dma_start(raw2[:], w2.rearrange("(f p) n -> p f n", p=P)).then_inc(w2_in, 16)

            @block.gpsimd
            def _(pool):
                pool.wait_ge(b2_in, 16)
                pool.tensor_tensor(chip.x[:], chip.x[:], b2_row[:].rearrange("p (a n) -> p a n", a=1)
                                   .to_broadcast([P, NT, D]), ALU.add).then_inc(b2_added, 1)

            @block.tensor
            def _(pe):
                pe.wait_ge(b1_in, 16)
                pe.transpose(hidden_ps[0][:, 0:FC], b1_rows[:], chip.ident[0:FC, 0:FC]).then_inc(b1_turned, 1)
                pe.wait_ge(b1_ready, 1)
                pe.wait_ge(w_lo_done, 1)
                with pe.Fori(0, NG) as g:
                    def first(f):
                        if f >= 2:
                            pe.wait_ge(hidden_done, g * FC + f - 1)
                        for c in range(CH):
                            last = product(pe, hidden_ps[f % 2][:], w1_hi[:, c, f * P:(f + 1) * P],
                                           w1_lo[:, c, f * P:(f + 1) * P], chip.h_hi[:, c, bass.ds(g * GN, GN)],
                                           chip.h_lo[:, c, bass.ds(g * GN, GN)], start=c == 0, stop=c == CH - 1)
                        last.then_inc(hidden_made, 1)

                    def second(f):
                        pe.wait_ge(hi_done, g * FC + f + 1)
                        pe.wait_ge(lo_done, g * FC + f + 1)
                        for t in range(GT):
                            tok = slice(t * P, (t + 1) * P)
                            last = product(pe, out_ps[:, t, 0:D], hidden_hi[f % 2][:, tok], hidden_lo[f % 2][:, tok],
                                           w2_hi[:, f, :], w2_lo[:, f, :], start=f == 0, stop=f == FC - 1)
                        last.then_inc(used, 1)
                    first(0)
                    for f in range(FC):
                        if f + 1 < FC:
                            first(f + 1)
                        if f == 0:
                            pe.wait_ge(w_lo_done, 2)
                        second(f)
                    pe.wait_ge(out_added, g + 1)

            @block.scalar
            def _(act):
                act.wait_ge(w1_in, 16)
                act.activation(w1_hi[:], raw1[:], ACT.Copy).then_inc(w_hi_done, 1)
                act.wait_ge(w2_in, 16)
                act.activation(w2_hi[:], raw2[:], ACT.Copy).then_inc(w_hi_done, 1)
                with act.Fori(0, NG) as g:
                    for f in range(FC):
                        act.wait_ge(hidden_made, g * FC + f + 1)
                        if f >= 2:
                            act.wait_ge(lo_done, g * FC + f - 1)
                            act.wait_ge(used, g * FC + f - 1)
                        act.activation(hidden[f % 2][:], hidden_ps[f % 2][:], function,
                                       bias=b1_cols[:, f:f + 1]).then_inc(hidden_done, 1)
                        act.wait_ge(hidden_done, g * FC + f + 1)
                        act.activation(hidden_hi[f % 2][:], hidden[f % 2][:], ACT.Copy).then_inc(hi_done, 1)

            @block.vector
            def _(dve):
                dve.wait_ge(b1_turned, 1)
                dve.tensor_copy(b1_cols[:], hidden_ps[0][:, 0:FC]).then_inc(b1_ready, 1)
                for i, (raw, hi, lo) in enumerate(((raw1, w1_hi, w1_lo), (raw2, w2_hi, w2_lo))):
                    dve.wait_ge(w_hi_done, i + 1)
                    dve.tensor_tensor(lo[:], raw[:], hi[:].bitcast(F32), ALU.subtract).then_inc(w_lo_done, 1)
                dve.wait_ge(b2_added, 1)
                with dve.Fori(0, NG) as g:
                    for f in range(FC):
                        dve.wait_ge(hi_done, g * FC + f + 1)
                        dve.tensor_tensor(hidden_lo[f % 2][:], hidden[f % 2][:], hidden_hi[f % 2][:].bitcast(F32),
                                          ALU.subtract).then_inc(lo_done, 1)
                    dve.wait_ge(used, g * FC + FC)
                    rows = chip.x[:, bass.ds(g * GT, GT), :]
                    dve.tensor_tensor(rows, out_ps[:, :, 0:D], rows, ALU.add).then_inc(out_added, 1)


def narrow_attention(chip, tag, heads, kv_heads, q_in, k_in, v_in, out_in, source, mask, multiply, score_scale):
    nc = chip.nc
    HD = D // heads
    GROUPS = heads // kv_heads
    HALF = 64
    QS = 4
    KS = kv_heads * HD // HALF
    PER = HALF // HD
    UT = 2
    UN = UT * P
    UNITS = NT // UT
    CHUNK = 16
    CT = heads // CHUNK
    SC = CT * UT
    VC = kv_heads * HD
    HW = HD + 1
    STEPS = 2 + (2 if KS == 4 else 1) + UT

    with ExitStack() as stack:
        def sb(name, shape, dtype=F32):
            return chip.sb(f"{tag}_{name}", shape, dtype, stack)

        def split(name, shape):
            return sb(name + "_hi", shape, F32R), sb(name + "_lo", shape, F32R)

        def sem(name):
            return chip.sem(f"{tag}_{name}")
        raw_q, raw_k, raw_v, raw_o = sb("raw_q", [P, CH, D]), sb("raw_k", [P, CH, VC]), sb("raw_v", [P, CH, VC]), sb("raw_o", [P, CH, D])
        dup_q, dup_k = sb("dup_q", [P, CH, QS, P]), sb("dup_k", [P, CH, KS, P])
        wq, wk, wv, wo = split("wq", [P, CH, QS, P]), split("wk", [P, CH, KS, P]), split("wv", [P, CH, VC]), split("wo", [P, CH, D])
        NV = QS + KS + CH
        bias_in_rows, bias_rows, bias_cols = sb("bias_in_rows", [1, D + 2 * VC]), sb("bias_rows", [1, NV, P]), sb("bias_cols", [P, NV])
        bo_row = sb("bo_row", [P, D])
        mask_tiles = 1 if multiply and mask.shape[0] == 1 else NT
        masks = sb("masks", [P, mask_tiles, SEQ])
        mask_bias = sb("mask_bias", [P, mask_tiles, SEQ]) if multiply else None
        head_pick = sb("head_pick", [P, 2, PER])
        head_mask = sb("head_mask", [P, PER])
        side_mask = sb("side_mask", [P, kv_heads, HD])
        q = [sb(f"q{b}", [P, QS, UT, P]) for b in range(2)]
        kc = [sb(f"kc{b}", [P, UT * max(1, KS // 2), SEQ]) for b in range(2)]
        kb = [sb(f"kb{b}", [P, UT * KS, PER, SEQ]) for b in range(2)]
        vb = [sb(f"vb{b}", [P, UT * HB, kv_heads, HW]) for b in range(2)]
        score = [sb(f"score{b}", [P, CHUNK, SEQ]) for b in range(2)]
        top = [sb(f"top{b}", [P, CHUNK]) for b in range(2)]
        weight_t = sb("weight_t", [P, CHUNK // 2, P])
        inverse = sb("inverse", [P, heads])
        rows = sb("rows", [P, D])
        o_whole = sb("o_whole", [P, CH, P])
        o_t = split("o_t", [P, CH, P])
        proj_ps = [chip.ps(f"{tag}_proj_ps{b}", [P, 512], stack) for b in range(2)]
        score_ps = [chip.ps(f"{tag}_score_ps{b}", [P, CHUNK, SEQ], stack) for b in range(2)]
        attn_ps = chip.ps(f"{tag}_attn_ps", [P, 512], stack)
        out_ps = chip.ps(f"{tag}_out_ps", [P, 2, D], stack)

        params_in, mask_in, bias_in, bo_in, masks_made = (sem(s) for s in ("params_in", "mask_in", "bias_in", "bo_in", "masks_made"))
        bias_spread, bias_turned, bias_ready, mask_ready, dup_done, w_hi_done, w_lo_done, bo_added, cleared = (
            sem(s) for s in ("bias_spread", "bias_turned", "bias_ready", "mask_ready", "dup_done", "w_hi_done", "w_lo_done", "bo_added", "cleared"))
        proj_made, qk_taken, v_taken, kb_made, scores_made, masked, biased, top_done, shifted, exp_done = (
            sem(s) for s in ("proj_made", "qk_taken", "v_taken", "kb_made", "scores_made", "masked", "biased", "top_done", "shifted", "exp_done"))
        turned, turned_taken, attn_made, inverse_done, rows_done, rows_turned, o_hi_done, o_whole_done, o_lo_done, out_made, out_added = (
            sem(s) for s in ("turned", "turned_taken", "attn_made", "inverse_done", "rows_done", "rows_turned", "o_hi_done", "o_whole_done", "o_lo_done", "out_made", "out_added"))

        chip_h = (chip.h_hi, chip.h_lo)
        stage = [split(f"stage{b}", [P, CH, UT * HB * P]) for b in range(2)]
        staged = sem("staged")

        def chunked(w):
            return w.rearrange("(c p) n -> p c n", p=P)

        def sets(t, n):
            if GROUPS == 1:
                return t.rearrange("p (s f) -> p s f", f=HALF)
            return t.rearrange("p (k s f) -> p s k f", s=QS, f=HD)

        def halves(t, side):
            part = t[:, :, side * HALF:(side + 1) * HALF]
            return part if GROUPS == 1 else part.rearrange("p s (k f) -> p s k f", f=HD)
        ksteps = 2 if KS == 4 else 1
        QK = 2 + ksteps

        def units(engine, slot):
            slot(0, 0, True, False)
            with engine.Fori(0, UNITS // 2 - 1) as i:
                for j in (1, 2):
                    slot(i * 2 + j, j, True, True)
            for j in (1, 2):
                slot(UNITS - 2 + j, j, j == 1, True)

        with nc.Block() as block:
            @block.sync
            def _(sp):
                for t, src in ((raw_q, q_in), (raw_k, k_in), (raw_v, v_in), (raw_o, out_in)):
                    sp.dma_start(t[:], chunked(src[0])).then_inc(params_in, 16)

            @block.gpsimd
            def _(pool):
                for b in range(2):
                    pool.memset(q[b][:], 0.0)
                pool.memset(head_pick[:], 1.0)
                pool.memset(side_mask[:], 1.0).then_inc(masks_made, 1)
                pool.wait_ge(masks_made, 1)
                pool.affine_select(out=head_pick[:], in_=head_pick[:], compare_op=ALU.is_ge, fill=0.0, base=0,
                                   pattern=[[-HALF, 2], [-HD, PER]], channel_multiplier=1).then_inc(masks_made, 1)
                pool.wait_ge(masks_made, 2)
                pool.affine_select(out=head_pick[:], in_=head_pick[:], compare_op=ALU.is_ge, fill=0.0, base=HD - 1,
                                   pattern=[[HALF, 2], [HD, PER]], channel_multiplier=-1).then_inc(masks_made, 1)
                side = side_mask[:].rearrange("p (m j) d -> p m j d", j=2)
                pool.affine_select(out=side, in_=side, compare_op=ALU.is_ge, fill=0.0, base=0,
                                   pattern=[[0, kv_heads // 2], [-SEQ, 2], [0, HD]], channel_multiplier=1).then_inc(masks_made, 1)
                pool.wait_ge(masks_made, 4)
                pool.affine_select(out=side, in_=side, compare_op=ALU.is_ge, fill=0.0, base=SEQ - 1,
                                   pattern=[[0, kv_heads // 2], [SEQ, 2], [0, HD]], channel_multiplier=-1).then_inc(masks_made, 1)
                pool.wait_ge(masks_made, 5)
                pool.tensor_tensor(head_mask[:], head_pick[:, 0, :], head_pick[:, 1, :], ALU.add).then_inc(masks_made, 1)
                for b in range(2):
                    pool.tensor_copy(vb[b][:, :, :, HD], side_mask[:, :, 0].rearrange("p (a h) -> p a h", a=1)
                                     .to_broadcast([P, UT * HB, kv_heads])).then_inc(masks_made, 1)
                pool.wait_ge(masks_made, 6 + 2)
                pool.wait_ge(bo_in, 16)
                pool.tensor_tensor(chip.x[:], chip.x[:], bo_row[:].rearrange("p (a n) -> p a n", a=1)
                                   .to_broadcast([P, NT, D]), ALU.add).then_inc(bo_added, 1)

                def slot(n, j, this, prev):
                    u, v = j % 2, (j - 1) % 2
                    if prev:
                        for s in range(SC):
                            m = n * SC - SC + s
                            if multiply:
                                mb = mask_bias[:, 0:1, :] if mask_tiles == 1 else mask_bias[:, bass.ds((n - 1) * UT + s // CT, 1), :]
                                pool.wait_ge(masked, m + 1)
                                pool.tensor_tensor(score[s % 2][:], score[s % 2][:], mb.to_broadcast([P, CHUNK, SEQ]),
                                                   ALU.add).then_inc(biased, 1)
                            pool.wait_ge(top_done, m + 1)
                            pool.tensor_tensor(score[s % 2][:], score[s % 2][:], top[s % 2][:].rearrange("p (h a) -> p h a", a=1)
                                               .to_broadcast([P, CHUNK, SEQ]), ALU.subtract).then_inc(shifted, 1)
                    if this:
                        for s in range(ksteps):
                            pool.wait_ge(qk_taken, n * QK + 2 + s + 1)
                            B = UT * KS // ksteps
                            pool.tensor_tensor(kb[u][:, s * B:(s + 1) * B, :, :],
                                               kc[s % 2][:].rearrange("p t (a k) -> p t a k", a=1).to_broadcast([P, B, PER, SEQ]),
                                               head_mask[:].rearrange("p (a h b) -> p a h b", a=1, b=1).to_broadcast([P, B, PER, SEQ]),
                                               ALU.mult).then_inc(kb_made, 1)
                units(pool, slot)

            @block.tensor
            def _(pe):
                pe.wait_ge(bias_spread, 1)
                for i in range(NV):
                    last = pe.matmul(attn_ps[:, i:i + 1], bias_rows[0:1, i, :], chip.one[0:1, 0:1], start=True, stop=True)
                last.then_inc(bias_turned, 1)
                pe.wait_ge(w_lo_done, 4)

                def project(n, u, s):
                    tokens = bass.ds(n * UN, UN) if not isinstance(n, int) else slice(n * UN, (n + 1) * UN)
                    out = proj_ps[s % 2]
                    if s >= 2:
                        if s - 2 < QK:
                            pe.wait_ge(qk_taken, n * QK + s - 1)
                        else:
                            pe.wait_ge(v_taken, n * UT + s - 2 - QK + 1)
                    if s < QK:
                        src, w_, first = (chip_h, wq, 2 * s) if s < 2 else (source, wk, 2 * (s - 2))
                        for x in range(2 if s < 2 or KS == 4 else 1):
                            for c in range(CH):
                                last = product(pe, out[:, x * UN:(x + 1) * UN], w_[0][:, c, first + x, :], w_[1][:, c, first + x, :],
                                               src[0][:, c, tokens], src[1][:, c, tokens], start=c == 0, stop=c == CH - 1)
                    else:
                        t = s - QK
                        for b in range(HB):
                            for c in range(CH):
                                both = [stage[u][x][:, c, (t * HB + b) * P:(t * HB + b + 1) * P] for x in range(2)]
                                last = product(pe, out[:, b * VC:(b + 1) * VC], both[0], both[1], wv[0][:, c, :], wv[1][:, c, :],
                                               start=c == 0, stop=c == CH - 1)
                    last.then_inc(proj_made, 1)

                def scores(n, v, s):
                    m = n * SC - SC + s
                    t, part = s // CT, s % CT
                    if s >= 2:
                        pe.wait_ge(turned_taken, m - 1)
                    flat = score_ps[s % 2][:].rearrange("p h k -> p (h k)")
                    if CT == 1:
                        for x in range(QS):
                            last = pe.matmul(flat[:, x * PER * SEQ:(x + 1) * PER * SEQ], q[v][:, x, t, :],
                                             kb[v][:, x * UT + t, :, :].rearrange("p h k -> p (h k)"), start=True, stop=True)
                    else:
                        for x in range(2):
                            last = pe.matmul(flat[:, x * PER * SEQ:(x + 1) * PER * SEQ], q[v][:, part * 2 + x, t, :],
                                             kb[v][:, t, :, :].rearrange("p h k -> p (h k)"), start=True, stop=True)
                    last.then_inc(scores_made, 1)

                def turn(n, s):
                    m = n * SC - SC + s
                    pe.wait_ge(exp_done, m + 1)
                    flat = score[s % 2][:].rearrange("p h k -> p (h k)")
                    out = score_ps[s % 2][:].rearrange("p h k -> p (h k)")
                    for x in range(CHUNK // 2):
                        last = pe.transpose(out[:, x * P:(x + 1) * P], flat[:, x * P:(x + 1) * P], chip.ident[:])
                    last.then_inc(turned, 1)

                def attend(n, v, s):
                    m = n * SC - SC + s
                    t, part = s // CT, s % CT
                    pe.wait_ge(turned_taken, m + 1)
                    if part == 0 and t > 0:
                        pe.wait_ge(rows_done, n * UT - UT + t)
                    for x in range(CHUNK // 2):
                        pair = x % (kv_heads // 2)
                        col = (part * CHUNK + 2 * x) * HW
                        for b in range(HB):
                            last = pe.matmul(attn_ps[b * SEQ:(b + 1) * SEQ, col:col + 2 * HW],
                                             weight_t[:, x, b * SEQ:(b + 1) * SEQ],
                                             vb[v][:, t * HB + b, 2 * pair:2 * pair + 2, :].rearrange("p h w -> p (h w)"),
                                             start=True, stop=True)
                    last.then_inc(attn_made, 1)

                def output(n, t):
                    m = n * UT - UT + t
                    pe.wait_ge(rows_done, m + 1)
                    if t > 0:
                        pe.wait_ge(out_added, m)
                    for c in range(CH):
                        last = pe.transpose(out_ps[:, 0, c * P:(c + 1) * P], rows[:, c * P:(c + 1) * P], chip.ident[:])
                    last.then_inc(rows_turned, 1)
                    pe.wait_ge(o_hi_done, m + 1)
                    pe.wait_ge(o_lo_done, m + 1)
                    for c in range(CH):
                        last = product(pe, out_ps[:, 1, :], o_t[0][:, c, :], o_t[1][:, c, :], wo[0][:, c, :], wo[1][:, c, :],
                                       start=c == 0, stop=c == CH - 1)
                    last.then_inc(out_made, 1)

                def slot(n, j, this, prev):
                    u, v = j % 2, (j - 1) % 2
                    if prev:
                        pe.wait_ge(kb_made, n * ksteps)
                        pe.wait_ge(qk_taken, n * QK)
                        pe.wait_ge(v_taken, n * UT)
                        scores(n, v, 0)
                        scores(n, v, 1)
                    if this:
                        for s in range(QK):
                            project(n, u, s)
                    if prev:
                        turn(n, 0)
                        attend(n, v, 0)
                        if SC > 2:
                            scores(n, v, 2)
                    if this:
                        pe.wait_ge(staged, 2 * n + 2)
                        project(n, u, QK)
                    if prev:
                        turn(n, 1)
                        attend(n, v, 1)
                        if SC > 2:
                            scores(n, v, 3)
                        output(n, 0)
                    if this:
                        project(n, u, QK + 1)
                    if prev:
                        for s in range(2, SC):
                            turn(n, s)
                            attend(n, v, s)
                        output(n, 1)
                    if this:
                        pe.wait_ge(v_taken, n * UT + UT)
                    if prev:
                        pe.wait_ge(out_added, n * UT)
                units(pe, slot)

            @block.scalar
            def _(act):
                act.dma_start(bias_in_rows[0:1, 0:D], q_in[1].rearrange("(a n) -> a n", a=1)).then_inc(bias_in, 16)
                act.dma_start(bias_in_rows[0:1, D:D + VC], k_in[1].rearrange("(a n) -> a n", a=1)).then_inc(bias_in, 16)
                act.dma_start(bias_in_rows[0:1, D + VC:D + 2 * VC], v_in[1].rearrange("(a n) -> a n", a=1)).then_inc(bias_in, 16)
                if mask_tiles == 1:
                    for b in range(HB):
                        act.dma_start(masks[b * SEQ:(b + 1) * SEQ, 0, :], mask[0, 0]).then_inc(mask_in, 16)
                else:
                    act.dma_start(masks[:], mask.rearrange("b a q k -> (b a q) k")
                                  .rearrange("(t p) k -> p t k", p=P)).then_inc(mask_in, 16)
                act.dma_start(bo_row[:], out_in[1].rearrange("(a n) -> a n", a=1).to_broadcast([P, D])).then_inc(bo_in, 16)
                for i, (w_, src) in enumerate(((wq, dup_q), (wk, dup_k), (wv, raw_v), (wo, raw_o))):
                    if i == 0:
                        act.wait_ge(dup_done, 1)
                        act.wait_ge(params_in, 64)
                    act.activation(w_[0][:], src[:], ACT.Copy).then_inc(w_hi_done, 1)
                act.wait_ge(bias_ready, 1)
                act.wait_ge(masks_made, 8)

                def slot(n, j, this, prev):
                    u, v = j % 2, (j - 1) % 2

                    def take(s):
                        act.wait_ge(proj_made, n * STEPS + s + 1)
                        pair = range(2 if s < 2 or KS == 4 else 1)
                        if s == 2 and prev:
                            act.wait_ge(kb_made, n * ksteps)
                        for x in pair:
                            part = proj_ps[s % 2][:, x * UN:(x + 1) * UN].rearrange("p (t b k) -> p t b k", b=HB, k=SEQ)
                            for b in range(HB):
                                half = slice(b * HALF, (b + 1) * HALF)
                                if s < 2:
                                    out = q[u][half, 2 * s + x, :, b * SEQ:(b + 1) * SEQ]
                                    bias = bias_cols[half, 2 * s + x:2 * s + x + 1]
                                else:
                                    out = kc[(s - 2) % 2][half, x * UT:(x + 1) * UT, :]
                                    i = QS + 2 * (s - 2) + x
                                    bias = bias_cols[half, i:i + 1]
                                last = act.activation(out, part[half, :, b, :], ACT.Identity, bias=bias)
                        last.then_inc(qk_taken, 1)

                    def exps(s):
                        act.wait_ge(shifted, n * SC - SC + s + 1)
                        act.activation(score[s % 2][:], score[s % 2][:], ACT.Exp).then_inc(exp_done, 1)

                    def take_turned(s):
                        act.wait_ge(turned, n * SC - SC + s + 1)
                        act.activation(weight_t[:].rearrange("p x q -> p (x q)"),
                                       score_ps[s % 2][:].rearrange("p h k -> p (h k)"), ACT.Copy).then_inc(turned_taken, 1)

                    def take_output(t):
                        act.wait_ge(rows_turned, n * UT - UT + t + 1)
                        for c in range(CH):
                            last = act.activation(o_whole[:, c, :], out_ps[:, 0, c * P:(c + 1) * P], ACT.Identity,
                                                  bias=bias_cols[:, QS + KS + c:QS + KS + c + 1])
                        last.then_inc(o_whole_done, 1)
                        act.wait_ge(o_whole_done, n * UT - UT + t + 1)
                        act.activation(o_t[0][:], o_whole[:], ACT.Copy).then_inc(o_hi_done, 1)
                    if this:
                        take(0)
                        take(1)
                    if prev:
                        exps(0)
                    if this:
                        for s in range(2, QK):
                            take(s)
                        tokens = bass.ds(n * UN, UN) if not isinstance(n, int) else slice(n * UN, (n + 1) * UN)
                        for x in range(2):
                            for c in range(CH):
                                last = act.activation(
                                    stage[u][x][:, c, :].rearrange("p (b r k) -> p b r k", r=2, k=SEQ),
                                    source[x][:, c, tokens].bitcast(F32).rearrange("p (b a k) -> p b a k", a=1, k=SEQ)
                                    .to_broadcast([P, UT * HB, 2, SEQ]), ACT.Copy)
                            last.then_inc(staged, 1)
                    if prev:
                        take_turned(0)
                        exps(1)
                        take_turned(1)
                        if SC > 2:
                            exps(2)
                        take_output(0)
                        for s in range(2, SC):
                            if s == 3:
                                exps(3)
                            take_turned(s)
                        take_output(1)
                units(act, slot)

            @block.vector
            def _(dve):
                dve.wait_ge(bias_in, 48)
                dve.wait_ge(masks_made, 8)
                for side in range(2):
                    dve.tensor_copy(halves(bias_rows[:, 0:QS, :], side), sets(bias_in_rows[:, 0:D], D))
                    dve.tensor_copy(bias_rows[:, QS:QS + KS, side * HALF:(side + 1) * HALF],
                                    bias_in_rows[:, D:D + VC].rearrange("p (s f) -> p s f", f=HALF))
                value_bias = bias_in_rows[:, D + VC:D + 2 * VC]
                if GROUPS == 1:
                    last = dve.tensor_copy(bias_rows[:, QS + KS:NV, :].rearrange("p c f -> p (c f)"), value_bias)
                else:
                    last = dve.tensor_copy(bias_rows[:, QS + KS:NV, :].rearrange("p c (k g f) -> p (c k) g f", g=GROUPS, f=HD),
                                           value_bias.rearrange("p (k a f) -> p k a f", a=1, f=HD)
                                           .to_broadcast([1, kv_heads, GROUPS, HD]))
                last.then_inc(bias_spread, 1)
                dve.wait_ge(bias_turned, 1)
                dve.tensor_copy(bias_cols[:], attn_ps[:, 0:NV]).then_inc(bias_ready, 1)
                if multiply:
                    dve.wait_ge(mask_in, 32 if mask_tiles == 1 else 16)
                    dve.tensor_scalar(mask_bias[:], masks[:], -1.0, 10000.0, ALU.add, ALU.mult).then_inc(mask_ready, 1)
                    dve.wait_ge(mask_ready, 1)
                    dve.tensor_scalar(masks[:], masks[:], score_scale, None, ALU.mult).then_inc(mask_ready, 1)
                    dve.wait_ge(mask_ready, 2)
                else:
                    dve.wait_ge(mask_in, 32 if mask_tiles == 1 else 16)
                dve.wait_ge(params_in, 64)
                for c in range(CH):
                    for side in range(2):
                        dve.tensor_copy(halves(dup_q[:, c, :, :], side), sets(raw_q[:, c, :], D))
                        last = dve.tensor_copy(dup_k[:, c, :, side * HALF:(side + 1) * HALF],
                                               raw_k[:, c, :].rearrange("p (s f) -> p s f", f=HALF))
                last.then_inc(dup_done, 1)
                dve.wait_ge(dup_done, 1)
                for i, (w_, src) in enumerate(((wq, dup_q), (wk, dup_k), (wv, raw_v), (wo, raw_o))):
                    dve.wait_ge(w_hi_done, i + 1)
                    dve.tensor_tensor(w_[1][:], src[:], w_[0][:].bitcast(F32), ALU.subtract).then_inc(w_lo_done, 1)
                dve.wait_ge(bo_added, 1)

                def slot(n, j, this, prev):
                    u, v = j % 2, (j - 1) % 2

                    def mask_scores(s):
                        m = n * SC - SC + s
                        mk = masks[:, 0:1, :] if mask_tiles == 1 else masks[:, bass.ds((n - 1) * UT + s // CT, 1), :]
                        mk = mk.to_broadcast([P, CHUNK, SEQ])
                        dve.wait_ge(scores_made, m + 1)
                        if multiply:
                            dve.tensor_tensor(score[s % 2][:], score_ps[s % 2][:], mk, ALU.mult).then_inc(masked, 1)
                            dve.wait_ge(biased, m + 1)
                        else:
                            dve.scalar_tensor_tensor(score[s % 2][:], score_ps[s % 2][:], score_scale, mk,
                                                     ALU.mult, ALU.add).then_inc(masked, 1)
                            dve.wait_ge(masked, m + 1)
                        dve.tensor_reduce(top[s % 2][:], score[s % 2][:], AX, ALU.max).then_inc(top_done, 1)

                    def take_values(t):
                        dve.wait_ge(proj_made, n * STEPS + QK + t + 1)
                        dve.tensor_tensor(vb[u][:, t * HB:(t + 1) * HB, :, 0:HD],
                                          proj_ps[(QK + t) % 2][:, 0:HB * VC].rearrange("p (b h f) -> p b h f", b=HB, f=HD),
                                          side_mask[:].rearrange("p (a h) f -> p a h f", a=1).to_broadcast([P, HB, kv_heads, HD]),
                                          ALU.mult).then_inc(v_taken, 1)

                    def normalise(t):
                        m = n * UT - UT + t
                        dve.wait_ge(attn_made, n * SC - SC + (t + 1) * CT)
                        done = attn_ps[:, 0:heads * HW].rearrange("p (h w) -> p h w", w=HW)
                        dve.reciprocal(inverse[:], done[:, :, HD]).then_inc(inverse_done, 1)
                        dve.wait_ge(inverse_done, m + 1)
                        if GROUPS == 1:
                            dve.tensor_tensor(rows[:].rearrange("p (h f) -> p h f", f=HD), done[:, :, 0:HD],
                                              inverse[:].rearrange("p (h a) -> p h a", a=1).to_broadcast([P, heads, HD]),
                                              ALU.mult).then_inc(rows_done, 1)
                        else:
                            dve.tensor_tensor(rows[:].rearrange("p (k g f) -> p g k f", g=GROUPS, f=HD),
                                              done[:, :, 0:HD].rearrange("p (g k) f -> p g k f", g=GROUPS),
                                              inverse[:].rearrange("p (g k a) -> p g k a", g=GROUPS, a=1)
                                              .to_broadcast([P, GROUPS, kv_heads, HD]), ALU.mult).then_inc(rows_done, 1)

                    def finish(t):
                        m = n * UT - UT + t
                        dve.wait_ge(o_hi_done, m + 1)
                        dve.tensor_tensor(o_t[1][:], o_whole[:], o_t[0][:].bitcast(F32), ALU.subtract).then_inc(o_lo_done, 1)
                        dve.wait_ge(out_made, m + 1)
                        tile = chip.x[:, bass.ds(m, 1), :].rearrange("p a d -> p (a d)")
                        dve.tensor_tensor(tile, out_ps[:, 1, :], tile, ALU.add).then_inc(out_added, 1)
                    if prev:
                        mask_scores(0)
                        mask_scores(1)
                        if CT == 1:
                            normalise(0)
                        if SC > 2:
                            mask_scores(2)
                    if this:
                        take_values(0)
                    if prev:
                        if CT == 2:
                            normalise(0)
                        if SC > 2:
                            mask_scores(3)
                        finish(0)
                    if this:
                        take_values(1)
                    if prev:
                        normalise(1)
                        finish(1)
                units(dve, slot)


def normalise_rows(chip, tag, gamma, beta):
    nc = chip.nc
    with ExitStack() as stack:
        def sb(name, shape):
            return chip.sb(f"{tag}_{name}", shape, F32, stack)
        stats, moments = sb("stats", [P, GT, 6]), sb("moments", [P, GT, 2])
        spread, inverse, idle = sb("spread", [P, GT]), sb("inverse", [P, GT]), sb("idle", [P, 1])
        gain, shift = sb("gain", [P, D]), sb("shift", [P, D])
        rows = sb("rows", [P, GT, D])
        gain_in, stats_done, moments_done, spread_done, inverse_done, rows_done, scaled, shifted, done = (
            chip.sem(f"{tag}_{s}") for s in ("gain_in", "stats_done", "moments_done", "spread_done", "inverse_done",
                                             "rows_done", "scaled", "shifted", "done"))
        with nc.Block() as block:
            @block.sync
            def _(sp):
                sp.dma_start(gain[:], gamma.rearrange("(a n) -> a n", a=1).to_broadcast([P, D])).then_inc(gain_in, 16)
                sp.dma_start(shift[:], beta.rearrange("(a n) -> a n", a=1).to_broadcast([P, D])).then_inc(gain_in, 16)

            @block.scalar
            def _(act):
                with act.Fori(0, NG) as g:
                    act.wait_ge(moments_done, g * GT + GT)
                    act.activation(spread[:], moments[:, :, 1], ACT.Sqrt, bias=chip.eps[:, 1:2]).then_inc(spread_done, 1)

            @block.vector
            def _(dve):
                with dve.Fori(0, NG) as g:
                    tiles = [chip.x[:, bass.ds(g * GT + j, 1), :].rearrange("p a d -> p (a d)") for j in range(GT)]
                    for j in range(GT):
                        dve.bn_stats(stats[:, j, :], tiles[j]).then_inc(stats_done, 1)
                    dve.wait_ge(stats_done, g * GT + GT)
                    dve.memset(idle[:], 0.0)
                    for j in range(GT):
                        dve.bn_aggr(moments[:, j, :], stats[:, j, :]).then_inc(moments_done, 1)
                    dve.wait_ge(spread_done, g + 1)
                    dve.reciprocal(inverse[:], spread[:]).then_inc(inverse_done, 1)
                    dve.wait_ge(inverse_done, g + 1)
                    for j in range(GT):
                        dve.tensor_scalar(rows[:, j, :], tiles[j], moments[:, j, 0:1], inverse[:, j:j + 1],
                                          ALU.subtract, ALU.mult).then_inc(rows_done, 1)
                    dve.wait_ge(done, g + 1)

            @block.gpsimd
            def _(pool):
                pool.wait_ge(gain_in, 32)
                with pool.Fori(0, NG) as g:
                    group = chip.x[:, bass.ds(g * GT, GT), :]
                    pool.wait_ge(rows_done, g * GT + GT)
                    pool.tensor_tensor(rows[:], rows[:], gain[:].rearrange("p (a n) -> p a n", a=1)
                                       .to_broadcast([P, GT, D]), ALU.mult).then_inc(scaled, 1)
                    pool.wait_ge(scaled, g + 1)
                    pool.tensor_tensor(rows[:], rows[:], shift[:].rearrange("p (a n) -> p a n", a=1)
                                       .to_broadcast([P, GT, D]), ALU.add).then_inc(shifted, 1)
                    pool.wait_ge(shifted, g + 1)
                    pool.tensor_copy(group, rows[:]).then_inc(done, 1)


def layer0(chip):
    I = chip.inputs
    for n in (1, 2):
        turn_input(chip, f"l0n{n}", I[f"L0_xattn_ln{n}_scale"], I[f"L0_xattn_ln{n}_offset"])
        wide_attention(chip, f"l0a{n}", n)
        chip.end_stage()
    layer0_mlp(chip)


def layer0_mlp(chip):
    I = chip.inputs
    turn_input(chip, "l0n3", I["L0_xattn_ln_mlp_scale"], I["L0_xattn_ln_mlp_offset"])
    dense_mlp(chip, "l0m", I["L0_xattn_w_fc1"], I["L0_xattn_b_fc1"], I["L0_xattn_w_fc2"], I["L0_xattn_b_fc2"], ACT.Gelu)
    chip.end_stage()


def layer1(chip):
    I = {k[9:]: v for k, v in chip.inputs.items() if k.startswith("L1_xattn_")}
    turn_input(chip, "l1t")
    narrow_attention(chip, "l1a", 32, 8, (I["Wq"], I["bq"]), (I["Wk"], I["bk"]), (I["Wv"], I["bv"]), (I["Wo"], I["bo"]),
                     (chip.ctx_hi, chip.ctx_lo), chip.inputs["mask_Bx1xSxS2_ff0"], False,
                     1.0 / float(np.sqrt(np.float32(8))))
    normalise_rows(chip, "l1n", I["gamma"], I["beta"])
    chip.end_stage()


def layer3(chip):
    I = {k[9:]: v for k, v in chip.inputs.items() if k.startswith("L3_xattn_")}
    scale = 1.0 / float(np.sqrt(np.float32(16)))
    turn_input(chip, "l3n1", I["ln1_s"], I["ln1_b"])
    w, b = I["w_qkv"], I["b_qkv"]
    parts = [(w[:, i * D:(i + 1) * D], b[i * D:(i + 1) * D]) for i in range(3)]
    narrow_attention(chip, "l3a1", 16, 16, *parts, (I["w_ao"], I["b_ao"]), (chip.h_hi, chip.h_lo),
                     chip.inputs["mask_1x1xSxS2_fc1"], True, scale)
    chip.end_stage()
    turn_input(chip, "l3n2", I["ln2_s"], I["ln2_b"])
    w, b = I["w_kv"], I["b_kv"]
    parts = [(w[:, i * D:(i + 1) * D], b[i * D:(i + 1) * D]) for i in range(2)]
    narrow_attention(chip, "l3a2", 16, 16, (I["w_q"], I["b_q"]), *parts, (I["w_co"], I["b_co"]), (chip.ctx_hi, chip.ctx_lo),
                     chip.inputs["mask_Bx1xSxS2_ff1"], True, scale)
    chip.end_stage()
    turn_input(chip, "l3n3", I["ln3_s"], I["ln3_b"])
    dense_mlp(chip, "l3m", I["w1"], I["b1"], I["w2"], I["b2"], ACT.Gelu_apprx_tanh)


def layer2(chip):
    nc = chip.nc
    I = {k[9:]: v for k, v in chip.inputs.items() if k.startswith("L2_xattn_")}
    NB = HB * CH
    tag = "l2"
    with ExitStack() as stack:
        def sb(name, shape):
            return chip.sb(f"{tag}_{name}", shape, F32, stack)

        def sem(name):
            return chip.sem(f"{tag}_{name}")
        context = sb("context", [P, NT, D])
        w_rows, w_cols = sb("w_rows", [P, 4, P]), sb("w_cols", [P, 4, P])
        bias = sb("bias", [P, 4])
        stats = [sb(f"stats{i}", [P, 6]) for i in range(2)]
        moments = sb("moments", [P, 2, NT, 2])
        pair_moments, pair_done = sb("pair_moments", [P, 2, 2]), sem("pair_done")
        spread, inverse = sb("spread", [P, 2, NT]), sb("inverse", [P, 2, NT])
        normed = [sb(f"normed{b}", [P, 2, D]) for b in range(2)]
        held = [sb(f"held{b}", [P, D]) for b in range(2)]
        maps = [sb(f"maps{b}", [P, 2, D]) for b in range(2)]
        value_t = [sb(f"value_t{b}", [P, CH, P]) for b in range(2)]
        top, total, inv = sb("top", [P, NB]), sb("total", [P, NB]), sb("inv", [P, NB])
        expd, weight = sb("expd", [P, NB, D]), sb("weight", [P, NB, D])
        weight_t = sb("weight_t", [P, HB, CH, D])
        attended = sb("attended", [P, D])
        conv_ps = chip.ps(f"{tag}_conv_ps", [P, 2, D], stack)
        value_ps = chip.ps(f"{tag}_value_ps", [P, 512], stack)
        score_ps = chip.ps(f"{tag}_score_ps", [P, HB, CH, D], stack)
        turned_ps = chip.ps(f"{tag}_turned_ps", [P, HB, CH, D], stack)
        mo_ps, out_ps = chip.ps(f"{tag}_mo_ps", [P, 512], stack), chip.ps(f"{tag}_out_ps", [P, 512], stack)
        w_zeroed, w_in, b_in, ctx_in, w_turned, w_ready = (sem(s) for s in ("w_zeroed", "w_in", "b_in", "ctx_in", "w_turned", "w_ready"))
        stats_done, moments_done, spread_done, inverse_done, normed_done = (
            sem(s) for s in ("stats_done", "moments_done", "spread_done", "inverse_done", "normed_done"))
        conv_made, value_made, maps_done, value_done, score_made, top_done, exp_done, inv_done, weight_done = (
            sem(s) for s in ("conv_made", "value_made", "maps_done", "value_done", "score_made", "top_done", "exp_done", "inv_done", "weight_done"))
        turned, turned_taken, mo_made, mo_done, out_made, out_done = (
            sem(s) for s in ("turned", "turned_taken", "mo_made", "mo_done", "out_made", "out_done"))

        with nc.Block() as block:
            @block.sync
            def _(sp):
                sp.dma_start(context[:], chip.inputs["ctx_2048"].rearrange("b s d -> (b s) d")
                             .rearrange("(t p) d -> p t d", p=P)).then_inc(ctx_in, 16)
                sp.wait_ge(w_zeroed, 1)
                for i, k in enumerate(("Wn", "Wm", "Wl", "Wo")):
                    for b in range(HB):
                        half = slice(b * SEQ, (b + 1) * SEQ)
                        sp.dma_start(w_rows[half, i, half], I[k]).then_inc(w_in, 16)
                        sp.dma_start(bias[half, i:i + 1], I["b" + k[1]].rearrange("(p a) -> p a", a=1)).then_inc(b_in, 16)

            @block.gpsimd
            def _(pool):
                pool.memset(w_rows[:], 0.0).then_inc(w_zeroed, 1)

            @block.scalar
            def _(act):
                act.wait_ge(moments_done, 2 * NT)
                act.activation(spread[:], moments[:, :, :, 1], ACT.Sqrt, bias=chip.eps[:, 0:1]).then_inc(spread_done, 1)

            @block.tensor
            def _(pe):
                pe.wait_ge(w_in, 16 * 4 * HB)
                for i in range(4):
                    last = pe.transpose(value_ps[:, i * P:(i + 1) * P], w_rows[:, i, :], chip.ident[:])
                last.then_inc(w_turned, 1)

            @block.vector
            def _(dve):
                dve.wait_ge(ctx_in, 16)
                with dve.Fori(0, NT) as t:
                    for i, src in enumerate((chip.x, context)):
                        dve.bn_stats(stats[i][:], src[:, bass.ds(t, 1), :].rearrange("p a d -> p (a d)")).then_inc(stats_done, 1)
                    dve.wait_ge(stats_done, t * 2 + 2)
                    dve.memset(top[:, 0:1], 0.0)
                    for i in range(2):
                        dve.bn_aggr(pair_moments[:, i, :], stats[i][:]).then_inc(pair_done, 1)
                    dve.wait_ge(pair_done, t * 2 + 2)
                    dve.tensor_copy(moments[:, :, bass.ds(t, 1), :].rearrange("p i a m -> p i (a m)"),
                                    pair_moments[:]).then_inc(moments_done, 2)
                dve.wait_ge(spread_done, 1)
                dve.reciprocal(inverse[:], spread[:]).then_inc(inverse_done, 1)
                dve.wait_ge(w_turned, 1)
                dve.tensor_copy(w_cols[:].rearrange("p i n -> p (i n)"), value_ps[:]).then_inc(w_ready, 1)

        def tiles(engine, slot):
            slot(0, 0, True, False, True)
            with engine.Fori(0, NT // 2 - 1) as i:
                for j in (1, 2):
                    slot(i * 2 + j, j, True, True, True)
            for j in (1, 2):
                slot(NT - 2 + j, j, j == 1, True, False)

        with nc.Block() as block:
            @block.sync
            def _(sp):
                sp.wait_ge(b_in, 16 * 4 * HB)

            @block.tensor
            def _(pe):
                def slot(n, j, this, prev, more):
                    u, v = j % 2, (j - 1) % 2
                    if this:
                        pe.wait_ge(normed_done, n + 1)
                        if prev:
                            pe.wait_ge(maps_done, n)
                        for i in range(2):
                            last = pe.matmul(conv_ps[:, i, :], w_cols[:, i, :], normed[u][:, i, :], start=True, stop=True)
                        last.then_inc(conv_made, 1)
                        if prev:
                            pe.wait_ge(value_done, n)
                        for c in range(CH):
                            last = pe.matmul(value_ps[:, c * P:(c + 1) * P], held[u][:, c * P:(c + 1) * P], w_cols[:, 2, :],
                                             start=True, stop=True)
                        last.then_inc(value_made, 1)
                    if prev:
                        pe.wait_ge(weight_done, n)
                        for b in range(HB):
                            for t in range(CH):
                                for c in range(CH):
                                    last = pe.transpose(turned_ps[:, b, c, t * P:(t + 1) * P],
                                                        weight[:, b * CH + t, c * P:(c + 1) * P], chip.ident[:])
                        last.then_inc(turned, 1)
                    if this:
                        pe.wait_ge(maps_done, n + 1)
                        for b in range(HB):
                            half = slice(b * SEQ, (b + 1) * SEQ)
                            for t in range(CH):
                                last = pe.matmul(score_ps[:, b, t, :], maps[u][half, 0, t * P:(t + 1) * P], maps[u][half, 1, :],
                                                 start=True, stop=True)
                        last.then_inc(score_made, 1)
                    if prev:
                        pe.wait_ge(turned_taken, n)
                        pe.wait_ge(value_done, n)
                        for b in range(HB):
                            half = slice(b * SEQ, (b + 1) * SEQ)
                            for c in range(CH):
                                last = pe.matmul(mo_ps[half, 0:D], value_t[v][:, c, half], weight_t[:, b, c, :],
                                                 start=c == 0, stop=c == CH - 1)
                        last.then_inc(mo_made, 1)
                        pe.wait_ge(mo_done, n)
                        pe.matmul(out_ps[:, 0:D], w_cols[:, 3, :], attended[:], start=True, stop=True).then_inc(out_made, 1)
                tiles(pe, slot)

            @block.scalar
            def _(act):
                def slot(n, j, this, prev, more):
                    u, v = j % 2, (j - 1) % 2
                    if this:
                        act.wait_ge(conv_made, n + 1)
                        for i in range(2):
                            last = act.activation(maps[u][:, i, :], conv_ps[:, i, :], ACT.Identity, bias=bias[:, i:i + 1])
                        last.then_inc(maps_done, 1)
                    if prev:
                        act.wait_ge(top_done, n * 2)
                        for i in range(NB):
                            last = act.activation(expd[:, i, :], score_ps[:, i // CH, i % CH, :], ACT.Exp,
                                                  bias=top[:, i:i + 1], accum_out=total[:, i:i + 1])
                        last.then_inc(exp_done, 1)
                        act.wait_ge(turned, n)
                        act.activation(weight_t[:].rearrange("p b c t -> p (b c t)"),
                                       turned_ps[:].rearrange("p b c t -> p (b c t)"), ACT.Copy).then_inc(turned_taken, 1)
                        act.wait_ge(mo_made, n)
                        act.activation(attended[:], mo_ps[:, 0:D], ACT.Identity, bias=bias[:, 2:3]).then_inc(mo_done, 1)
                act.wait_ge(b_in, 16 * 4 * HB)
                tiles(act, slot)

            @block.vector
            def _(dve):
                def prepare(n, u):
                    for i, src in enumerate((chip.x, context)):
                        tile = src[:, bass.ds(n, 1), :].rearrange("p a d -> p (a d)")
                        dve.tensor_scalar(normed[u][:, i, :], tile,
                                          moments[:, i, bass.ds(n, 1), 0], inverse[:, i, bass.ds(n, 1)],
                                          ALU.subtract, ALU.mult)
                    dve.tensor_copy(held[u][:], tile).then_inc(normed_done, 1)

                def slot(n, j, this, prev, more):
                    u, v = j % 2, (j - 1) % 2
                    if prev:
                        dve.wait_ge(score_made, n)
                        dve.tensor_reduce(top[:], score_ps[:].rearrange("p b t s -> p (b t) s"), AX, ALU.max).then_inc(top_done, 1)
                        dve.wait_ge(top_done, n * 2 - 1)
                        dve.tensor_scalar(top[:], top[:], -1.0, None, ALU.mult).then_inc(top_done, 1)
                    if this:
                        dve.wait_ge(value_made, n + 1)
                        dve.tensor_copy(value_t[u][:].rearrange("p c n -> p (c n)"), value_ps[:, 0:D]).then_inc(value_done, 1)
                    if more:
                        prepare(n + 1, 1 - u)
                    if prev:
                        dve.wait_ge(exp_done, n)
                        dve.reciprocal(inv[:], total[:]).then_inc(inv_done, 1)
                        dve.wait_ge(inv_done, n)
                        for i in range(NB):
                            last = dve.tensor_scalar(weight[:, i, :], expd[:, i, :], inv[:, i:i + 1], None, ALU.mult)
                        last.then_inc(weight_done, 1)
                        dve.wait_ge(out_made, n)
                        tile = chip.x[:, bass.ds(n - 1, 1), :].rearrange("p a d -> p (a d)")
                        dve.scalar_tensor_tensor(tile, out_ps[:, 0:D], bias[:, 3:4], tile, ALU.add, ALU.add).then_inc(out_done, 1)
                dve.wait_ge(b_in, 16 * 4 * HB)
                prepare(0, 0)
                tiles(dve, slot)
    chip.end_stage()


def build(nc, inputs, out):
    with ExitStack() as stack:
        chip = Chip(nc, inputs, stack)
        load(chip)
        layer0(chip)
        layer1(chip)
        layer2(chip)
        layer3(chip)
        store(chip, out)


_OUT = (BATCH, SEQ, D)


def kernel(**inputs):
    import concourse.bacc as _bacc
    from concourse.bass_utils import run_bass_kernel_spmd as _run

    nc = _bacc.Bacc("TRN2", target_bir_lowering=False, num_devices=1)
    arrays, aps = {}, {}
    for name, a in inputs.items():
        a = np.ascontiguousarray(a)
        arrays[f"in_{name}_dram"] = a
        aps[name] = nc.dram_tensor(f"in_{name}_dram", a.shape, mybir.dt.from_np(a.dtype), kind="ExternalInput").ap()
    out = nc.dram_tensor("out_0_dram", _OUT, F32, kind="ExternalOutput").ap()
    build(nc, aps, out)
    r = _run(nc, [arrays], core_ids=[0])
    return r.results[0]["out_0_dram"]
```

```python
from contextlib import ExitStack

import numpy as np
import concourse.bass as bass
from concourse import mybir

F32 = mybir.dt.float32
F32R = mybir.dt.float32r
ALU = mybir.AluOpType
ACT = mybir.ActivationFunctionType
AX = mybir.AxisListType.X

P = 128
BATCH, SEQ, D = 32, 64, 256
TOK = BATCH * SEQ
NT = TOK // P
GT = 4
NG = NT // GT
GN = GT * P
CH = D // P
HB = P // SEQ


class Chip:

    def __init__(self, nc, inputs, stack):
        self.nc, self.inputs, self.stack = nc, inputs, stack
        self.stage_sems = []
        self.x = self.sb("x", [P, NT, D])
        self.ident = self.sb("ident", [P, P])
        self.one = self.sb("one", [P, 1])
        self.eps = self.sb("eps", [P, 2])
        self.ctx_hi = self.sb("ctx_hi", [P, CH, TOK], F32R)
        self.ctx_lo = self.sb("ctx_lo", [P, CH, TOK], F32R)
        self.h_hi = self.sb("h_hi", [P, CH, TOK], F32R)
        self.h_lo = self.sb("h_lo", [P, CH, TOK], F32R)

    def sb(self, name, shape, dtype=F32, stack=None):
        return (stack or self.stack).enter_context(self.nc.sbuf_tensor(name, shape, dtype))

    def ps(self, name, shape, stack):
        return stack.enter_context(self.nc.psum_tensor(name, shape, F32))

    def sem(self, name):
        self.stage_sems.append(self.nc.alloc_semaphore(name=name))
        return self.stage_sems[-1]

    def end_stage(self):
        self.nc.clear_and_free_semaphores(self.stage_sems)
        self.nc.all_engine_barrier()
        self.stage_sems = []


def product(pe, out, wh, wl, mh, ml, start=True, stop=True):
    pe.matmul(out, wh, mh, start=start, stop=False)
    pe.matmul(out, wh, ml, start=False, stop=False)
    return pe.matmul(out, wl, mh, start=False, stop=stop)


def columns(vector):
    return vector.rearrange("(c p) -> p c", p=P)


def load(chip):
    nc, I = chip.nc, chip.inputs
    with ExitStack() as stack:
        rows = chip.sb("ctx_rows", [P, NT, D], F32, stack)
        turned = [chip.ps(f"ctx_turned{i}", [P, CH, GN], stack) for i in range(2)]
        x_in = chip.sem("x_in")
        rows_in = [chip.sem(f"ctx_rows_in{g}") for g in range(NG)]
        eps_set, ident_set = chip.sem("eps_set"), chip.sem("ident_set")
        ctx_turned = chip.sem("ctx_turned")
        hi_done, lo_done = chip.sem("ctx_hi_done"), chip.sem("ctx_lo_done")
        x_rows = I["x"].rearrange("b s d -> (b s) d").rearrange("(t p) d -> p t d", p=P)
        ctx_rows = I["ctx_2048"].rearrange("b s d -> (b s) d").rearrange("(t p) d -> p t d", p=P)

        with nc.Block() as block:
            @block.sync
            def _(sp):
                for g in range(NG):
                    sp.dma_start(rows[:, g * GT:(g + 1) * GT, :],
                                 ctx_rows[:, g * GT:(g + 1) * GT, :]).then_inc(rows_in[g], 16)
                sp.dma_start(chip.x[:], x_rows).then_inc(x_in, 16)
                sp.wait_ge(x_in, 16)

            @block.gpsimd
            def _(pool):
                pool.memset(chip.one[:], 1.0)
                pool.memset(chip.eps[:, 0:1], 1e-5)
                pool.memset(chip.eps[:, 1:2], 1e-6)
                pool.memset(chip.ident[:], 0.0).then_inc(ident_set, 1)
                pool.wait_ge(ident_set, 1)
                pool.affine_select(out=chip.ident[:], in_=chip.ident[:], compare_op=ALU.not_equal, fill=1.0,
                                   base=0, pattern=[[-1, P]], channel_multiplier=1).then_inc(ident_set, 1)

            @block.tensor
            def _(pe):
                pe.wait_ge(ident_set, 2)
                for g in range(NG):
                    pe.wait_ge(rows_in[g], 16)
                    if g >= 2:
                        pe.wait_ge(hi_done, CH * (g - 1))
                        pe.wait_ge(lo_done, CH * (g - 1))
                    for c in range(CH):
                        for j in range(GT):
                            last = pe.transpose(turned[g % 2][:, c, j * P:(j + 1) * P],
                                                rows[:, g * GT + j, c * P:(c + 1) * P], chip.ident[:])
                        last.then_inc(ctx_turned, 1)

            @block.scalar
            def _(act):
                for g in range(NG):
                    for c in range(CH):
                        act.wait_ge(ctx_turned, CH * g + c + 1)
                        act.activation(chip.ctx_hi[:, c, g * GN:(g + 1) * GN], turned[g % 2][:, c, :],
                                       ACT.Copy).then_inc(hi_done, 1)

            @block.vector
            def _(dve):
                for g in range(NG):
                    for c in range(CH):
                        dve.wait_ge(hi_done, CH * g + c + 1)
                        dve.tensor_tensor(chip.ctx_lo[:, c, g * GN:(g + 1) * GN], turned[g % 2][:, c, :],
                                          chip.ctx_hi[:, c, g * GN:(g + 1) * GN].bitcast(F32),
                                          ALU.subtract).then_inc(lo_done, 1)


def turn_input(chip, tag, scale=None, offset=None):
    nc = chip.nc
    norm = scale is not None
    with ExitStack() as stack:
        def sb(name, shape, dtype=F32):
            return chip.sb(f"{tag}_{name}", shape, dtype, stack)
        stats, moments = sb("stats", [P, GT, 6]), sb("moments", [P, GT, 2])
        spread, inverse = sb("spread", [P, GT]), sb("inverse", [P, GT])
        rows = sb("rows", [P, GT, D])
        idle = sb("idle", [P, 1])
        whole = sb("whole", [P, CH, GN])
        gain = sb("gain", [P, 2, CH])
        turned = chip.ps(f"{tag}_turned", [P, CH, GN], stack)
        gain_in = chip.sem(f"{tag}_gain_in")
        stats_done, moments_done = chip.sem(f"{tag}_stats"), chip.sem(f"{tag}_moments")
        spread_done, inverse_done = chip.sem(f"{tag}_spread"), chip.sem(f"{tag}_inverse")
        rows_done, turned_done = chip.sem(f"{tag}_rows_done"), chip.sem(f"{tag}_turned_done")
        hi_done, whole_done, lo_done = (chip.sem(f"{tag}_{n}") for n in ("hi_done", "whole_done", "lo_done"))

        with nc.Block() as block:
            @block.sync
            def _(sp):
                if norm:
                    sp.dma_start(gain[:, 0, :], columns(scale), allow_slow_non_contiguous=True).then_inc(gain_in, 16)
                    sp.dma_start(gain[:, 1, :], columns(offset), allow_slow_non_contiguous=True).then_inc(gain_in, 16)
                    sp.wait_ge(gain_in, 32)

            @block.vector
            def _(dve):
                if norm:
                    dve.wait_ge(gain_in, 32)
                with dve.Fori(0, NG) as g:
                    if norm:
                        for j in range(GT):
                            dve.bn_stats(stats[:, j, :], chip.x[:, bass.ds(g * GT + j, 1), :]
                                         .rearrange("p a d -> p (a d)")).then_inc(stats_done, 1)
                        dve.wait_ge(stats_done, g * GT + GT)
                        dve.memset(idle[:], 0.0)
                        for j in range(GT):
                            dve.bn_aggr(moments[:, j, :], stats[:, j, :]).then_inc(moments_done, 1)
                        dve.wait_ge(spread_done, g + 1)
                        dve.reciprocal(inverse[:], spread[:]).then_inc(inverse_done, 1)
                        dve.wait_ge(inverse_done, g + 1)
                    for j in range(GT):
                        tile = chip.x[:, bass.ds(g * GT + j, 1), :].rearrange("p a d -> p (a d)")
                        if norm:
                            dve.tensor_scalar(rows[:, j, :], tile, moments[:, j, 0:1], inverse[:, j:j + 1],
                                              ALU.subtract, ALU.mult).then_inc(rows_done, 1)
                        else:
                            dve.tensor_copy(rows[:, j, :], tile).then_inc(rows_done, 1)
                    for c in range(CH):
                        dve.wait_ge(hi_done, g * CH + c + 1)
                        if norm:
                            dve.tensor_scalar(whole[:, c, :], turned[:, c, :], gain[:, 0, c:c + 1],
                                              gain[:, 1, c:c + 1], ALU.mult, ALU.add).then_inc(whole_done, 1)
                        else:
                            dve.tensor_copy(whole[:, c, :], turned[:, c, :]).then_inc(whole_done, 1)
                    for c in range(CH):
                        dve.wait_ge(whole_done, g * CH + c + 1)
                        dve.tensor_tensor(chip.h_lo[:, c, bass.ds(g * GN, GN)], whole[:, c, :],
                                          chip.h_hi[:, c, bass.ds(g * GN, GN)].bitcast(F32),
                                          ALU.subtract).then_inc(lo_done, 1)

            @block.scalar
            def _(act):
                if norm:
                    act.wait_ge(gain_in, 32)
                with act.Fori(0, NG) as g:
                    if norm:
                        act.wait_ge(moments_done, g * GT + GT)
                        act.activation(spread[:], moments[:, :, 1], ACT.Sqrt,
                                       bias=chip.eps[:, 0:1]).then_inc(spread_done, 1)
                    for c in range(CH):
                        act.wait_ge(turned_done, g * CH + c + 1)
                        if norm:
                            act.activation(chip.h_hi[:, c, bass.ds(g * GN, GN)], turned[:, c, :], ACT.Identity,
                                           bias=gain[:, 1, c:c + 1], scale=gain[:, 0, c:c + 1]).then_inc(hi_done, 1)
                        else:
                            act.activation(chip.h_hi[:, c, bass.ds(g * GN, GN)], turned[:, c, :],
                                           ACT.Copy).then_inc(hi_done, 1)

            @block.tensor
            def _(pe):
                with pe.Fori(0, NG) as g:
                    for c in range(CH):
                        for j in range(GT):
                            if c == 0:
                                pe.wait_ge(rows_done, g * GT + j + 1)
                            last = pe.transpose(turned[:, c, j * P:(j + 1) * P],
                                                rows[:, j, c * P:(c + 1) * P], chip.ident[:])
                        last.then_inc(turned_done, 1)
                    pe.wait_ge(hi_done, g * CH + CH)
                    pe.wait_ge(whole_done, g * CH + CH)


def store(chip, out):
    rows = out.rearrange("b s d -> (b s) d").rearrange("(t p) d -> p t d", p=P)
    stored = chip.sem("stored")
    with chip.nc.Block() as block:
        @block.sync
        def _(sp):
            sp.dma_start(rows, chip.x[:]).then_inc(stored, 16)
            sp.wait_ge(stored, 16)


def wide_attention(chip, tag, n):
    nc = chip.nc
    H, K = 16, 128
    SCALE = 1.0 / float(np.sqrt(np.float32(K)))
    wt = {k: chip.inputs[f"L0_xattn_{k}{n}"] for k in ("wq", "wk", "wv", "wo", "bq", "bk", "bv", "bo", "bias_k", "bias_v")}
    wq_d, wk_d, wv_d = (wt[k].rearrange("(c p) n -> p c n", p=P) for k in ("wq", "wk", "wv"))
    wo_d = wt["wo"].rearrange("(h d) n -> d h n", d=K)
    bias_k_row = wt["bias_k"].rearrange("a b h k -> (a b) (h k)")
    VW = 32

    with ExitStack() as keep:
        def sbk(name, shape, dtype=F32):
            return chip.sb(f"{tag}_{name}", shape, dtype, keep)
        bias_cols = sbk("bias_cols", [P, 4, H])
        learned_logit = sbk("learned_logit", [P, NT, H])
        learned_weight = sbk("learned_weight", [P, NT, VW])
        value_rows = sbk("value_rows", [P, D])

        with ExitStack() as stack:
            def sb(name, shape, dtype=F32):
                return chip.sb(f"{tag}_{name}", shape, dtype, stack)
            wq_all = sb("wq_all", [P, CH, H * K])
            wo_all = sb("wo_all", [P, H, D])
            key_all, bq_all = sb("key_all", [P, H * K]), sb("bq_all", [P, H * K])
            bias_rows = sb("bias_rows", [H, 4, K])
            u, u_hi, u_lo = sb("u", [P, CH, H]), sb("u_hi", [P, CH, H], F32R), sb("u_lo", [P, CH, H], F32R)
            logit_bias = sb("logit_bias", [P, H])
            spread_v = sb("spread_v", [P, H, P])
            bo_rows = sb("bo_rows", [P, D])
            cols_ps = chip.ps(f"{tag}_cols_ps", [P, 4, H], stack)
            logit_ps = chip.ps(f"{tag}_logit_ps", [P, NT, H], stack)
            value_ps = chip.ps(f"{tag}_value_ps", [P, D], stack)
            wq_in, key_in, bq_in, wo_in, rows_in, bo_in = (
                chip.sem(f"{tag}_{s}_in") for s in ("wq", "key", "bq", "wo", "rows", "bo"))
            zeroed, cols_turned, cols_done = (chip.sem(f"{tag}_{s}") for s in ("zeroed", "cols_turned", "cols_done"))
            u_step, c_step, v_step = (chip.sem(f"{tag}_{s}") for s in ("u_step", "c_step", "v_step"))
            logits_done, values_done, kept = (chip.sem(f"{tag}_{s}") for s in ("logits_done", "values_done", "kept"))

            with nc.Block() as block:
                @block.sync
                def _(sp):
                    sp.dma_start(wq_all[:], wq_d).then_inc(wq_in, 16)
                    sp.dma_start(key_all[:], bias_k_row.to_broadcast([P, H * K])).then_inc(key_in, 16)
                    sp.dma_start(bq_all[:], wt["bq"].rearrange("(a n) -> a n", a=1).to_broadcast([P, H * K])).then_inc(bq_in, 16)
                    sp.dma_start(wo_all[:], wo_d).then_inc(wo_in, 16)

                @block.scalar
                def _(act):
                    for i, name in enumerate(("bq", "bk", "bv")):
                        act.dma_start(bias_rows[:, i, :], wt[name].rearrange("(h k) -> h k", k=K)).then_inc(rows_in, 16)
                    act.dma_start(bias_rows[:, 3, :], wt["bias_v"].rearrange("a b h k -> (a b h) k")).then_inc(rows_in, 16)
                    act.wait_ge(zeroed, 3)
                    for r in range(0, P, VW):
                        act.dma_start(bo_rows[r:r + 1, :], wt["bo"].rearrange("(a n) -> a n", a=1)).then_inc(bo_in, 16)
                    act.wait_ge(u_step, 2)
                    act.activation(u_hi[:], u[:], ACT.Copy).then_inc(u_step, 1)

                @block.gpsimd
                def _(pool):
                    pool.memset(spread_v[:], 0.0).then_inc(zeroed, 1)
                    pool.memset(learned_weight[:], 0.0).then_inc(zeroed, 1)
                    pool.memset(bo_rows[:], 0.0).then_inc(zeroed, 1)
                    pool.wait_ge(zeroed, 2)
                    pool.memset(learned_weight[:, :, 0:1], 1.0)

                @block.tensor
                def _(pe):
                    pe.wait_ge(rows_in, 64)
                    for i in range(4):
                        last = pe.transpose(cols_ps[:, i, :], bias_rows[:, i, :], chip.ident[0:H, 0:H])
                    last.then_inc(cols_turned, 1)
                    pe.wait_ge(v_step, 2)
                    pe.wait_ge(wo_in, 16)
                    for h in range(H):
                        last = pe.matmul(value_ps[:], spread_v[:, h, :], wo_all[:, h, :], start=h == 0, stop=h == H - 1)
                    last.then_inc(values_done, 1)
                    pe.wait_ge(u_step, 4)
                    for t in range(NT):
                        for c in range(CH):
                            last = product(pe, logit_ps[:, t, :], chip.h_hi[:, c, t * P:(t + 1) * P],
                                           chip.h_lo[:, c, t * P:(t + 1) * P], u_hi[:, c, :], u_lo[:, c, :],
                                           start=c == 0, stop=c == CH - 1)
                    last.then_inc(logits_done, 1)

                @block.vector
                def _(dve):
                    dve.wait_ge(cols_turned, 1)
                    dve.tensor_copy(bias_cols[:], cols_ps[:]).then_inc(cols_done, 1)
                    dve.wait_ge(cols_done, 1)
                    dve.wait_ge(zeroed, 1)
                    for r in range(0, P, VW):
                        flat = spread_v[:].rearrange("p h c -> p (h c)")
                        dve.tensor_copy(spread_v[:, :, r], bias_cols[:, 2, :])
                        diag = flat[:, r + 1:r + 1 + (P + 1) * (H - 1) + 1:P + 1]
                        last = dve.tensor_tensor(diag, bias_cols[:, 3, :], bias_cols[:, 2, :], ALU.subtract)
                    last.then_inc(v_step, 2)
                    dve.wait_ge(key_in, 16)
                    dve.wait_ge(wq_in, 16)
                    dve.tensor_tensor(wq_all[:], wq_all[:], key_all[:].rearrange("p (a n) -> p a n", a=1)
                                      .to_broadcast([P, CH, H * K]), ALU.mult).then_inc(u_step, 1)
                    dve.wait_ge(u_step, 1)
                    dve.tensor_reduce(u[:], wq_all[:].rearrange("p c (h k) -> p c h k", k=K), AX, ALU.add).then_inc(u_step, 1)
                    dve.wait_ge(bq_in, 16)
                    dve.tensor_tensor(bq_all[:], bq_all[:], key_all[:], ALU.mult).then_inc(c_step, 1)
                    dve.wait_ge(u_step, 3)
                    dve.tensor_tensor(u_lo[:], u[:], u_hi[:].bitcast(F32), ALU.subtract).then_inc(u_step, 1)
                    dve.wait_ge(c_step, 1)
                    dve.tensor_reduce(logit_bias[:], bq_all[:].rearrange("p (h k) -> p h k", k=K), AX, ALU.add).then_inc(c_step, 1)
                    dve.wait_ge(values_done, 1)
                    dve.wait_ge(bo_in, 16 * (P // VW))
                    dve.tensor_tensor(value_rows[:], value_ps[:], bo_rows[:], ALU.add).then_inc(kept, 1)
                    dve.wait_ge(c_step, 2)
                    dve.wait_ge(logits_done, 1)
                    dve.tensor_tensor(learned_logit[:], logit_ps[:], logit_bias[:].rearrange("p (a h) -> p a h", a=1)
                                      .to_broadcast([P, NT, H]), ALU.add).then_inc(kept, 1)

        with ExitStack() as stack:
            def sb(name, shape, dtype=F32):
                return chip.sb(f"{tag}_{name}", shape, dtype, stack)

            def split(name, shape):
                return sb(name + "_hi", shape, F32R), sb(name + "_lo", shape, F32R)
            HP = 2
            ITEMS = HP * NG
            PASSES = H // HP
            raw = [sb(f"raw{p}", [P, 2, CH, K]) for p in range(HP)]
            raw_v, raw_o = sb("raw_v", [P, CH, HP * K]), sb("raw_o", [P, HP, D])
            w = [split(f"w{p}", [P, 2, CH, K]) for p in range(HP)]
            wv, wo = split("wv", [P, CH, HP * K]), split("wo", [P, HP, D])
            head_bias = [sb(f"head_bias{p}", [P, 2]) for p in range(HP)]
            q, k = sb("q", [P, GN]), sb("k", [P, GN])
            v = [sb(f"v{b}", [P, GT, HP * K]) for b in range(2)]
            logit = sb("logit", [P, GT, SEQ + 1])
            expd = sb("expd", [P, GT, SEQ + 1])
            top, total, inverse = sb("top", [P, GT]), sb("total", [P, GT]), sb("inverse", [P, GT])
            weight = sb("weight", [P, GT, P])
            weight_t = sb("weight_t", [P, GN])
            c = [split(f"c{p}", [P, GN]) for p in range(HP)]
            q_ps, k_ps, v_ps, s_ps, t_ps, c_ps = (
                chip.ps(f"{tag}_{x}_ps", [P, GN], stack) for x in ("q", "k", "v", "s", "t", "c"))
            o_ps = chip.ps(f"{tag}_o_ps", [P, GT, D], stack)

            raw_in = [chip.sem(f"{tag}_raw_in{p}") for p in range(HP)]
            raw_v_in, raw_o_in = chip.sem(f"{tag}_raw_v_in"), chip.sem(f"{tag}_raw_o_in")
            w_hi_done, w_split, wv_hi_done, wv_split, wo_hi_done, wo_split = (
                chip.sem(f"{tag}_{s}") for s in ("w_hi_done", "w_split", "wv_hi_done", "wv_split", "wo_hi_done", "wo_split"))
            q_made, k_made, v_made, s_made, t_made, c_made, o_made = (
                chip.sem(f"{tag}_{x}_made") for x in "qkvstco")
            q_done, v_done, t_done, c_hi, s_half, exp_done = (
                chip.sem(f"{tag}_{x}") for x in ("q_done", "v_done", "t_done", "c_hi", "s_half", "exp_done"))
            k_done, c_lo, s_rest, top_done, total_done, inverse_done, weight_a, added = (
                chip.sem(f"{tag}_{x}") for x in ("k_done", "c_lo", "s_rest", "top_done",
                                                 "total_done", "inverse_done", "weight_a", "added"))
            s_learned, shifted, weight_b, zero_done = (
                chip.sem(f"{tag}_{x}") for x in ("s_learned", "shifted", "weight_b", "zero_done"))

            def tiles(j):
                g = (j % ITEMS) // HP
                return slice(g * GT, (g + 1) * GT), slice(g * GN, (g + 1) * GN)

            def passes(engine, slots):
                slots(0, 0, True, False, False)
                slots(0, 1, True, True, False)
                with engine.Fori(0, PASSES - 1) as i:
                    for j in range(2, ITEMS + 2):
                        slots(i, j, True, True, True)
                for j in range(2, ITEMS + 2):
                    slots(PASSES - 1, j, j < ITEMS, j <= ITEMS, True)

            def next_head(i, j):
                more = not (isinstance(i, int) and i == PASSES - 1)
                return j - ITEMS + 1 if more and ITEMS - 1 <= j <= ITEMS else None

            with nc.Block() as block:
                @block.sync
                def _(sp):
                    def fetch(cols, both):
                        for p in range(HP):
                            for x, src in enumerate((wq_d, wk_d)):
                                sp.dma_start(raw[p][:, x, :, :], src[:, :, cols[p]]).then_inc(raw_in[p], 16)
                        sp.dma_start(raw_v[:], wv_d[:, :, both]).then_inc(raw_v_in, 16)
                        for p in range(HP):
                            sp.dma_start(raw_o[:, p, :], wt["wo"][cols[p], :]).then_inc(raw_o_in, 16)
                    fetch([slice(p * K, (p + 1) * K) for p in range(HP)], slice(0, HP * K))
                    with sp.Fori(1, PASSES) as i:
                        starts = [sp.snap((i * HP + p) * K) for p in range(HP)]
                        ends, count = sp.snap(i * HP), sp.snap(i * 1)
                        sp.wait_ge(w_split, ends)
                        sp.wait_ge(wv_split, count)
                        sp.wait_ge(wo_split, count)
                        fetch([bass.ds(start, K) for start in starts], bass.ds(starts[0], HP * K))
                    for p in range(HP):
                        sp.wait_ge(raw_in[p], 32 * PASSES)
                    sp.wait_ge(raw_v_in, 16 * PASSES)
                    sp.wait_ge(raw_o_in, 32 * PASSES)

                @block.gpsimd
                def _(pool):
                    def split_w(i, p):
                        pool.tensor_copy(head_bias[p][:], bias_cols[:, 0:2, bass.ds(i * HP + p, 1)]
                                         .rearrange("p a b -> p (a b)"))
                        pool.wait_ge(w_hi_done, i * HP + p + 1)
                        pool.tensor_tensor(w[p][1][:], raw[p][:], w[p][0][:].bitcast(F32),
                                           ALU.subtract).then_inc(w_split, 1)

                    def slots(i, j, this, mid, prev):
                        n = i * ITEMS + j
                        if j < HP and not prev:
                            split_w(0, j)
                        if mid:
                            rows, _ = tiles(j - 1)
                            head = (i + (j - 1) // ITEMS) * HP + (j - 1) % HP
                            if j >= 2:
                                pool.wait_ge(exp_done, n - 1)
                            pool.tensor_copy(logit[:, :, SEQ:SEQ + 1],
                                             learned_logit[:, rows, bass.ds(head, 1)]).then_inc(s_learned, 1)
                            pool.wait_ge(top_done, n)
                            pool.tensor_tensor(logit[:], logit[:], top[:].rearrange("p (t a) -> p t a", a=1)
                                               .to_broadcast([P, GT, SEQ + 1]), ALU.subtract).then_inc(shifted, 1)
                            if next_head(i, j) is not None:
                                split_w(i + 1, next_head(i, j))
                                pool.wait_ge(w_split, (i + 1) * HP + next_head(i, j) + 1)
                            pool.wait_ge(inverse_done, n)
                            pool.tensor_tensor(weight[SEQ:P, :, SEQ:P], expd[SEQ:P, :, 0:SEQ],
                                               inverse[SEQ:P].rearrange("p (t a) -> p t a", a=1)
                                               .to_broadcast([SEQ, GT, SEQ]), ALU.mult).then_inc(weight_b, 1)
                            pool.wait_ge(weight_b, n)
                        if prev and j == 2:
                            pool.wait_ge(wo_hi_done, i + 1)
                            pool.tensor_tensor(wo[1][:], raw_o[:], wo[0][:].bitcast(F32),
                                               ALU.subtract).then_inc(wo_split, 1)

                    pool.memset(weight[:], 0.0).then_inc(zero_done, 1)
                    passes(pool, slots)

                @block.tensor
                def _(pe):
                    def slots(i, j, this, mid, prev):
                        n = i * ITEMS + j
                        p = j % HP
                        _, cols = tiles(j)

                        def project(x):
                            out, made = ((q_ps, q_made), (k_ps, k_made))[x]
                            src = ((chip.h_hi, chip.h_lo), (chip.ctx_hi, chip.ctx_lo))[x]
                            for ch in range(CH):
                                last = product(pe, out[:], w[p][0][:, x, ch, :], w[p][1][:, x, ch, :],
                                               src[0][:, ch, cols], src[1][:, ch, cols],
                                               start=ch == 0, stop=ch == CH - 1)
                            last.then_inc(made, 1)
                        if prev:
                            pe.wait_ge(weight_a, n - 1)
                            pe.wait_ge(weight_b, n - 1)
                            for t in range(GT):
                                last = pe.transpose(t_ps[:, t * P:(t + 1) * P], weight[:, t, :], chip.ident[:])
                            last.then_inc(t_made, 1)
                        if this:
                            if j % ITEMS < HP:
                                pe.wait_ge(w_split, (i + j // ITEMS) * HP + p + 1)
                            project(0)
                        if prev:
                            pe.wait_ge(t_done, n - 1)
                            if p == 0:
                                pe.wait_ge(v_done, n)
                            for t in range(GT):
                                last = pe.matmul(c_ps[:, t * P:(t + 1) * P], v[(j - HP) // HP % 2][:, t, p * K:(p + 1) * K],
                                                 weight_t[:, t * P:(t + 1) * P], start=True, stop=True)
                            last.then_inc(c_made, 1)
                        if this:
                            project(1)
                        if prev and p == HP - 1:
                            pe.wait_ge(c_hi, n - 1)
                            pe.wait_ge(c_lo, n - 1)
                            pe.wait_ge(wo_split, i + 1)
                            for t in range(GT):
                                tok = slice(t * P, (t + 1) * P)
                                for x in range(HP):
                                    last = product(pe, o_ps[:, t, :], c[x][0][:, tok], c[x][1][:, tok],
                                                   wo[0][:, x, :], wo[1][:, x, :], start=x == 0, stop=x == HP - 1)
                            last.then_inc(o_made, 1)
                        if this:
                            if j % ITEMS == 0:
                                pe.wait_ge(wv_split, i + j // ITEMS + 1)
                            if mid:
                                pe.wait_ge(v_done, n)
                            for t in range(GT // HP):
                                start = cols.start + (p * GT // HP + t) * P
                                tok = slice(start, start + P)
                                for ch in range(CH):
                                    last = product(pe, v_ps[:, t * HP * K:(t + 1) * HP * K], chip.ctx_hi[:, ch, tok],
                                                   chip.ctx_lo[:, ch, tok], wv[0][:, ch, :], wv[1][:, ch, :],
                                                   start=ch == 0, stop=ch == CH - 1)
                            last.then_inc(v_made, 1)
                            pe.wait_ge(q_done, n + 1)
                            pe.wait_ge(k_done, n + 1)
                            if mid:
                                pe.wait_ge(s_half, n)
                                pe.wait_ge(s_rest, n)
                            for t in range(GT):
                                tok = slice(t * P, (t + 1) * P)
                                last = pe.matmul(s_ps[:, tok], q[:, tok], k[:, tok], start=True, stop=True)
                            last.then_inc(s_made, 1)
                        if prev and p == 0:
                            pe.wait_ge(c_hi, n - 1)
                            pe.wait_ge(c_lo, n - 1)
                    passes(pe, slots)

                @block.scalar
                def _(act):
                    def split_w(i, p):
                        act.wait_ge(raw_in[p], i * 32 + 32)
                        act.activation(w[p][0][:].rearrange("p x c k -> p (x c k)"),
                                       raw[p][:].rearrange("p x c k -> p (x c k)"), ACT.Copy).then_inc(w_hi_done, 1)

                    def split_wv(i):
                        act.wait_ge(raw_v_in, i * 16 + 16)
                        act.activation(wv[0][:], raw_v[:], ACT.Copy).then_inc(wv_hi_done, 1)

                    def slots(i, j, this, mid, prev):
                        n = i * ITEMS + j
                        p = j % HP
                        if j < HP and not prev:
                            split_w(0, j)
                            if j == 0:
                                split_wv(0)
                        if mid:
                            act.wait_ge(s_made, n)
                            act.activation(logit[SEQ:P, :, 0:SEQ], s_ps[SEQ:P, :].rearrange("p (t k) -> p t k", t=GT)
                                           [:, :, SEQ:P], ACT.Copy).then_inc(s_half, 1)
                        if prev:
                            act.wait_ge(t_made, n - 1)
                            act.activation(weight_t[:], t_ps[:], ACT.Copy).then_inc(t_done, 1)
                        if next_head(i, j) == HP - 1:
                            split_wv(i + 1)
                        if next_head(i, j) == 0:
                            split_w(i + 1, 0)
                        if this:
                            act.wait_ge(q_made, n + 1)
                            act.activation(q[:], q_ps[:], ACT.Identity, bias=head_bias[p][:, 0:1]).then_inc(q_done, 1)
                        if prev:
                            act.wait_ge(c_made, n - 1)
                            act.activation(c[p][0][:], c_ps[:], ACT.Copy).then_inc(c_hi, 1)
                        if mid:
                            act.wait_ge(shifted, n)
                            act.activation(expd[:], logit[:], ACT.Exp, scale=SCALE).then_inc(exp_done, 1)
                        if next_head(i, j) == HP - 1:
                            split_w(i + 1, HP - 1)
                        if prev and j == 2:
                            act.wait_ge(raw_o_in, i * 32 + 32)
                            act.activation(wo[0][:], raw_o[:], ACT.Copy).then_inc(wo_hi_done, 1)
                        if this:
                            act.wait_ge(v_made, n + 1)
                            act.activation(v[j // HP % 2][:, p * GT // HP:(p + 1) * GT // HP, :]
                                           .rearrange("p t k -> p (t k)"), v_ps[:], ACT.Copy).then_inc(v_done, 1)
                    passes(act, slots)

                @block.vector
                def _(dve):
                    def split_wv(i):
                        dve.wait_ge(wv_hi_done, i + 1)
                        dve.tensor_tensor(wv[1][:], raw_v[:], wv[0][:].bitcast(F32), ALU.subtract).then_inc(wv_split, 1)

                    def slots(i, j, this, mid, prev):
                        n = i * ITEMS + j
                        p = j % HP
                        if j == 0:
                            split_wv(0)
                        if mid:
                            dve.wait_ge(s_made, n)
                            dve.tensor_copy(logit[0:SEQ, :, 0:SEQ], s_ps[0:SEQ, :].rearrange("p (t k) -> p t k", t=GT)
                                            [:, :, 0:SEQ]).then_inc(s_rest, 1)
                            dve.wait_ge(s_rest, n)
                            dve.wait_ge(s_half, n)
                            dve.wait_ge(s_learned, n)
                            dve.tensor_reduce(top[:], logit[:], AX, ALU.max).then_inc(top_done, 1)
                        if next_head(i, j) == HP - 1:
                            split_wv(i + 1)
                        if prev:
                            dve.wait_ge(c_hi, n - 1)
                            dve.tensor_tensor(c[p][1][:], c_ps[:], c[p][0][:].bitcast(F32), ALU.subtract).then_inc(c_lo, 1)
                        if mid:
                            dve.wait_ge(exp_done, n)
                            dve.tensor_reduce(total[:], expd[:], AX, ALU.add).then_inc(total_done, 1)
                            dve.wait_ge(total_done, n)
                            dve.reciprocal(inverse[:], total[:]).then_inc(inverse_done, 1)
                        if this:
                            dve.wait_ge(k_made, n + 1)
                            dve.tensor_scalar(k[:], k_ps[:], head_bias[p][:, 1:2], None, ALU.add).then_inc(k_done, 1)
                        if mid:
                            dve.wait_ge(inverse_done, n)
                            dve.tensor_tensor(weight[0:SEQ, :, 0:SEQ], expd[0:SEQ, :, 0:SEQ],
                                              inverse[0:SEQ].rearrange("p (t a) -> p t a", a=1)
                                              .to_broadcast([SEQ, GT, SEQ]), ALU.mult).then_inc(weight_a, 1)
                            dve.tensor_tensor(learned_weight[:, tiles(j - 1)[0],
                                                             bass.ds((i + (j - 1) // ITEMS) * HP + (j - 1) % HP + 1, 1)],
                                              expd[:, :, SEQ:SEQ + 1], inverse[:].rearrange("p (t a) -> p t a", a=1),
                                              ALU.mult)
                        if prev and p == HP - 1:
                            rows, _ = tiles(j - 2)
                            dve.wait_ge(o_made, i * NG + (j - 1) // HP)
                            dve.tensor_tensor(chip.x[:, rows, :], o_ps[:], chip.x[:, rows, :], ALU.add).then_inc(added, 1)

                    dve.wait_ge(zero_done, 1)
                    passes(dve, slots)

        with ExitStack() as stack:
            weights_t = chip.sb(f"{tag}_weights_t", [P, NT // GT, P], F32, stack)
            turn_ps = chip.ps(f"{tag}_turn_ps", [P, NT // GT, P], stack)
            add_ps = [chip.ps(f"{tag}_add_ps{b}", [P, GN], stack) for b in range(GT)]
            turned, taken, tile_made, tile_added = (chip.sem(f"{tag}_{s}") for s in ("turned", "taken", "tile_made", "tile_added"))
            with nc.Block() as block:
                @block.tensor
                def _(pe):
                    for g in range(NG):
                        last = pe.transpose(turn_ps[:, g, :], learned_weight[:, g * GT:(g + 1) * GT, :]
                                            .rearrange("p t w -> p (t w)"), chip.ident[:])
                    last.then_inc(turned, 1)
                    pe.wait_ge(taken, 1)
                    for t in range(NT):
                        if t >= GT:
                            pe.wait_ge(tile_added, t - GT + 1)
                        r = VW * (t % GT)
                        pe.matmul(add_ps[t % GT][:, 0:D], weights_t[r:r + VW, t // GT, :],
                                  value_rows[r:r + VW, :], start=True, stop=True).then_inc(tile_made, 1)

                @block.vector
                def _(dve):
                    dve.wait_ge(turned, 1)
                    dve.tensor_copy(weights_t[:], turn_ps[:]).then_inc(taken, 1)
                    for t in range(NT):
                        dve.wait_ge(tile_made, t + 1)
                        dve.tensor_tensor(chip.x[:, t, :], add_ps[t % GT][:, 0:D], chip.x[:, t, :],
                                          ALU.add).then_inc(tile_added, 1)


def dense_mlp(chip, tag, w1, b1, w2, b2, function):
    nc = chip.nc
    FC = w1.shape[1] // P
    with ExitStack() as stack:
        def sb(name, shape, dtype=F32):
            return chip.sb(f"{tag}_{name}", shape, dtype, stack)
        raw1, raw2 = sb("raw1", [P, CH, FC * P]), sb("raw2", [P, FC, D])
        w1_hi, w1_lo = sb("w1_hi", [P, CH, FC * P], F32R), sb("w1_lo", [P, CH, FC * P], F32R)
        w2_hi, w2_lo = sb("w2_hi", [P, FC, D], F32R), sb("w2_lo", [P, FC, D], F32R)
        b1_rows, b1_cols, b2_row = sb("b1_rows", [FC, P]), sb("b1_cols", [P, FC]), sb("b2_row", [P, D])
        hidden = [sb(f"hidden{b}", [P, GN]) for b in range(2)]
        hidden_hi = [sb(f"hidden_hi{b}", [P, GN], F32R) for b in range(2)]
        hidden_lo = [sb(f"hidden_lo{b}", [P, GN], F32R) for b in range(2)]
        hidden_ps = [chip.ps(f"{tag}_hidden_ps{b}", [P, GN], stack) for b in range(2)]
        out_ps = chip.ps(f"{tag}_out_ps", [P, GT, 512], stack)
        b1_in, b2_in, w1_in, w2_in = (chip.sem(f"{tag}_{s}_in") for s in ("b1", "b2", "w1", "w2"))
        b1_turned, b1_ready, w_hi_done, w_lo_done, b2_added = (
            chip.sem(f"{tag}_{s}") for s in ("b1_turned", "b1_ready", "w_hi_done", "w_lo_done", "b2_added"))
        hidden_made, hidden_done, hi_done, lo_done, used, out_made, out_added = (
            chip.sem(f"{tag}_{s}") for s in ("hidden_made", "hidden_done", "hi_done", "lo_done", "used", "out_made", "out_added"))

        with nc.Block() as block:
            @block.sync
            def _(sp):
                sp.dma_start(b1_rows[:], b1.rearrange("(f p) -> f p", p=P)).then_inc(b1_in, 16)
                sp.dma_start(b2_row[:], b2.rearrange("(a n) -> a n", a=1).to_broadcast([P, D])).then_inc(b2_in, 16)
                sp.dma_start(raw1[:], w1.rearrange("(c p) n -> p c n", p=P)).then_inc(w1_in, 16)
                sp.dma_start(raw2[:], w2.rearrange("(f p) n -> p f n", p=P)).then_inc(w2_in, 16)

            @block.gpsimd
            def _(pool):
                pool.wait_ge(b2_in, 16)
                pool.tensor_tensor(chip.x[:], chip.x[:], b2_row[:].rearrange("p (a n) -> p a n", a=1)
                                   .to_broadcast([P, NT, D]), ALU.add).then_inc(b2_added, 1)

            @block.tensor
            def _(pe):
                pe.wait_ge(b1_in, 16)
                pe.transpose(hidden_ps[0][:, 0:FC], b1_rows[:], chip.ident[0:FC, 0:FC]).then_inc(b1_turned, 1)
                pe.wait_ge(b1_ready, 1)
                pe.wait_ge(w_lo_done, 1)
                with pe.Fori(0, NG) as g:
                    def first(f):
                        if f >= 2:
                            pe.wait_ge(hidden_done, g * FC + f - 1)
                        for c in range(CH):
                            last = product(pe, hidden_ps[f % 2][:], w1_hi[:, c, f * P:(f + 1) * P],
                                           w1_lo[:, c, f * P:(f + 1) * P], chip.h_hi[:, c, bass.ds(g * GN, GN)],
                                           chip.h_lo[:, c, bass.ds(g * GN, GN)], start=c == 0, stop=c == CH - 1)
                        last.then_inc(hidden_made, 1)

                    def second(f):
                        pe.wait_ge(hi_done, g * FC + f + 1)
                        pe.wait_ge(lo_done, g * FC + f + 1)
                        for t in range(GT):
                            tok = slice(t * P, (t + 1) * P)
                            last = product(pe, out_ps[:, t, 0:D], hidden_hi[f % 2][:, tok], hidden_lo[f % 2][:, tok],
                                           w2_hi[:, f, :], w2_lo[:, f, :], start=f == 0, stop=f == FC - 1)
                        last.then_inc(used, 1)
                    first(0)
                    for f in range(FC):
                        if f + 1 < FC:
                            first(f + 1)
                        if f == 0:
                            pe.wait_ge(w_lo_done, 2)
                        second(f)
                    pe.wait_ge(out_added, g + 1)

            @block.scalar
            def _(act):
                act.wait_ge(w1_in, 16)
                act.activation(w1_hi[:], raw1[:], ACT.Copy).then_inc(w_hi_done, 1)
                act.wait_ge(w2_in, 16)
                act.activation(w2_hi[:], raw2[:], ACT.Copy).then_inc(w_hi_done, 1)
                with act.Fori(0, NG) as g:
                    for f in range(FC):
                        act.wait_ge(hidden_made, g * FC + f + 1)
                        if f >= 2:
                            act.wait_ge(lo_done, g * FC + f - 1)
                            act.wait_ge(used, g * FC + f - 1)
                        act.activation(hidden[f % 2][:], hidden_ps[f % 2][:], function,
                                       bias=b1_cols[:, f:f + 1]).then_inc(hidden_done, 1)
                        act.wait_ge(hidden_done, g * FC + f + 1)
                        act.activation(hidden_hi[f % 2][:], hidden[f % 2][:], ACT.Copy).then_inc(hi_done, 1)

            @block.vector
            def _(dve):
                dve.wait_ge(b1_turned, 1)
                dve.tensor_copy(b1_cols[:], hidden_ps[0][:, 0:FC]).then_inc(b1_ready, 1)
                for i, (raw, hi, lo) in enumerate(((raw1, w1_hi, w1_lo), (raw2, w2_hi, w2_lo))):
                    dve.wait_ge(w_hi_done, i + 1)
                    dve.tensor_tensor(lo[:], raw[:], hi[:].bitcast(F32), ALU.subtract).then_inc(w_lo_done, 1)
                dve.wait_ge(b2_added, 1)
                with dve.Fori(0, NG) as g:
                    for f in range(FC):
                        dve.wait_ge(hi_done, g * FC + f + 1)
                        dve.tensor_tensor(hidden_lo[f % 2][:], hidden[f % 2][:], hidden_hi[f % 2][:].bitcast(F32),
                                          ALU.subtract).then_inc(lo_done, 1)
                    dve.wait_ge(used, g * FC + FC)
                    rows = chip.x[:, bass.ds(g * GT, GT), :]
                    dve.tensor_tensor(rows, out_ps[:, :, 0:D], rows, ALU.add).then_inc(out_added, 1)


def narrow_attention(chip, tag, heads, kv_heads, q_in, k_in, v_in, out_in, source, mask, multiply, score_scale):
    nc = chip.nc
    HD = D // heads
    GROUPS = heads // kv_heads
    HALF = 64
    QS = 4
    KS = kv_heads * HD // HALF
    PER = HALF // HD
    UT = 2
    UN = UT * P
    UNITS = NT // UT
    CHUNK = 16
    CT = heads // CHUNK
    SC = CT * UT
    VC = kv_heads * HD
    HW = HD + 1
    STEPS = 2 + (2 if KS == 4 else 1) + UT

    with ExitStack() as stack:
        def sb(name, shape, dtype=F32):
            return chip.sb(f"{tag}_{name}", shape, dtype, stack)

        def split(name, shape):
            return sb(name + "_hi", shape, F32R), sb(name + "_lo", shape, F32R)

        def sem(name):
            return chip.sem(f"{tag}_{name}")
        raw_q, raw_k, raw_v, raw_o = sb("raw_q", [P, CH, D]), sb("raw_k", [P, CH, VC]), sb("raw_v", [P, CH, VC]), sb("raw_o", [P, CH, D])
        dup_q, dup_k = sb("dup_q", [P, CH, QS, P]), sb("dup_k", [P, CH, KS, P])
        wq, wk, wv, wo = split("wq", [P, CH, QS, P]), split("wk", [P, CH, KS, P]), split("wv", [P, CH, VC]), split("wo", [P, CH, D])
        NV = QS + KS + CH
        bias_in_rows, bias_rows, bias_cols = sb("bias_in_rows", [1, D + 2 * VC]), sb("bias_rows", [1, NV, P]), sb("bias_cols", [P, NV])
        bo_row = sb("bo_row", [P, D])
        mask_tiles = 1 if multiply and mask.shape[0] == 1 else NT
        masks = sb("masks", [P, mask_tiles, SEQ])
        mask_bias = sb("mask_bias", [P, mask_tiles, SEQ]) if multiply else None
        head_pick = sb("head_pick", [P, 2, PER])
        head_mask = sb("head_mask", [P, PER])
        side_mask = sb("side_mask", [P, kv_heads, HD])
        q = [sb(f"q{b}", [P, QS, UT, P]) for b in range(2)]
        kc = [sb(f"kc{b}", [P, UT * max(1, KS // 2), SEQ]) for b in range(2)]
        kb = [sb(f"kb{b}", [P, UT * KS, PER, SEQ]) for b in range(2)]
        vb = [sb(f"vb{b}", [P, UT * HB, kv_heads, HW]) for b in range(2)]
        score = [sb(f"score{b}", [P, CHUNK, SEQ]) for b in range(2)]
        top = [sb(f"top{b}", [P, CHUNK]) for b in range(2)]
        weight_t = sb("weight_t", [P, CHUNK // 2, P])
        inverse = sb("inverse", [P, heads])
        rows = sb("rows", [P, D])
        o_t = split("o_t", [P, CH, P])
        proj_ps = [chip.ps(f"{tag}_proj_ps{b}", [P, 512], stack) for b in range(2)]
        score_ps = [chip.ps(f"{tag}_score_ps{b}", [P, CHUNK, SEQ], stack) for b in range(2)]
        attn_ps = chip.ps(f"{tag}_attn_ps", [P, 512], stack)
        out_ps = chip.ps(f"{tag}_out_ps", [P, 2, D], stack)

        params_in, mask_in, bias_in, bo_in, masks_made = (sem(s) for s in ("params_in", "mask_in", "bias_in", "bo_in", "masks_made"))
        bias_spread, bias_turned, bias_ready, mask_ready, dup_done, w_hi_done, w_lo_done, bo_added, cleared = (
            sem(s) for s in ("bias_spread", "bias_turned", "bias_ready", "mask_ready", "dup_done", "w_hi_done", "w_lo_done", "bo_added", "cleared"))
        proj_made, qk_taken, v_taken, kb_made, scores_made, masked, biased, top_done, shifted, exp_done = (
            sem(s) for s in ("proj_made", "qk_taken", "v_taken", "kb_made", "scores_made", "masked", "biased", "top_done", "shifted", "exp_done"))
        turned, turned_taken, attn_made, inverse_done, rows_done, rows_turned, o_hi_done, o_lo_done, out_made, out_added = (
            sem(s) for s in ("turned", "turned_taken", "attn_made", "inverse_done", "rows_done", "rows_turned", "o_hi_done", "o_lo_done", "out_made", "out_added"))

        chip_h = (chip.h_hi, chip.h_lo)
        stage = [split(f"stage{b}", [P, CH, UT * HB * P]) for b in range(2)]
        staged_hi, staged_lo = sem("staged_hi"), sem("staged_lo")

        def chunked(w):
            return w.rearrange("(c p) n -> p c n", p=P)

        def sets(t, n):
            if GROUPS == 1:
                return t.rearrange("p (s f) -> p s f", f=HALF)
            return t.rearrange("p (k s f) -> p s k f", s=QS, f=HD)

        def halves(t, side):
            part = t[:, :, side * HALF:(side + 1) * HALF]
            return part if GROUPS == 1 else part.rearrange("p s (k f) -> p s k f", f=HD)
        ksteps = 2 if KS == 4 else 1
        QK = 2 + ksteps

        FILL = ([([0, 1], [2]), ([3, 4], [5])] if SC == 2 else
                [([], [0]), ([1], []), ([], [2]), ([3], [4])])
        KB_SLOT = SC - 1

        def units(engine, slot):
            slot(0, 0, True, False, False)
            slot(1, 1, True, True, False)
            with engine.Fori(0, UNITS // 2 - 1) as i:
                for j in (2, 3):
                    slot(i * 2 + j, j, True, True, True)
            slot(UNITS, UNITS, False, True, True)
            slot(UNITS + 1, UNITS + 1, False, False, True)

        def steps(n, mid, prev):
            for s in range(SC):
                back = [(mid if s >= k else prev) for k in range(3)]
                ended = n * UT - UT + (s - 2) // CT if back[2] and (s - 2) % CT == CT - 1 else None
                yield s, n * SC - SC + s, back[1], ended

        def token_range(n):
            return bass.ds(n * UN, UN) if not isinstance(n, int) else slice(n * UN, (n + 1) * UN)

        with nc.Block() as block:
            @block.sync
            def _(sp):
                for t, src in ((raw_q, q_in), (raw_k, k_in), (raw_v, v_in), (raw_o, out_in)):
                    sp.dma_start(t[:], chunked(src[0])).then_inc(params_in, 16)

            @block.gpsimd
            def _(pool):
                for b in range(2):
                    pool.memset(q[b][:], 0.0)
                pool.memset(head_pick[:], 1.0)
                pool.memset(side_mask[:], 1.0).then_inc(masks_made, 1)
                pool.wait_ge(masks_made, 1)
                pool.affine_select(out=head_pick[:], in_=head_pick[:], compare_op=ALU.is_ge, fill=0.0, base=0,
                                   pattern=[[-HALF, 2], [-HD, PER]], channel_multiplier=1).then_inc(masks_made, 1)
                pool.wait_ge(masks_made, 2)
                pool.affine_select(out=head_pick[:], in_=head_pick[:], compare_op=ALU.is_ge, fill=0.0, base=HD - 1,
                                   pattern=[[HALF, 2], [HD, PER]], channel_multiplier=-1).then_inc(masks_made, 1)
                side = side_mask[:].rearrange("p (m j) d -> p m j d", j=2)
                pool.affine_select(out=side, in_=side, compare_op=ALU.is_ge, fill=0.0, base=0,
                                   pattern=[[0, kv_heads // 2], [-SEQ, 2], [0, HD]], channel_multiplier=1).then_inc(masks_made, 1)
                pool.wait_ge(masks_made, 4)
                pool.affine_select(out=side, in_=side, compare_op=ALU.is_ge, fill=0.0, base=SEQ - 1,
                                   pattern=[[0, kv_heads // 2], [SEQ, 2], [0, HD]], channel_multiplier=-1).then_inc(masks_made, 1)
                pool.wait_ge(masks_made, 5)
                pool.tensor_tensor(head_mask[:], head_pick[:, 0, :], head_pick[:, 1, :], ALU.add).then_inc(masks_made, 1)
                for b in range(2):
                    pool.tensor_copy(vb[b][:, :, :, HD], side_mask[:, :, 0].rearrange("p (a h) -> p a h", a=1)
                                     .to_broadcast([P, UT * HB, kv_heads])).then_inc(masks_made, 1)
                pool.wait_ge(masks_made, 6 + 2)
                pool.wait_ge(bo_in, 16)
                pool.tensor_tensor(chip.x[:], chip.x[:], bo_row[:].rearrange("p (a n) -> p a n", a=1)
                                   .to_broadcast([P, NT, D]), ALU.add).then_inc(bo_added, 1)

                def spread_keys(n, u, s):
                    B = UT * KS // ksteps
                    pool.wait_ge(qk_taken, n * QK + 2 + s + 1)
                    pool.tensor_tensor(kb[u][:, s * B:(s + 1) * B, :, :],
                                       kc[s % 2][:].rearrange("p t (a k) -> p t a k", a=1).to_broadcast([P, B, PER, SEQ]),
                                       head_mask[:].rearrange("p (a h b) -> p a h b", a=1, b=1).to_broadcast([P, B, PER, SEQ]),
                                       ALU.mult).then_inc(kb_made, 1)

                def slot(n, j, this, mid, prev):
                    u = j % 2
                    for s, m, last, ended in steps(n, mid, prev):
                        if this and s == KB_SLOT:
                            spread_keys(n, u, 0)
                        if mid:
                            score_ = score[s % 2]
                            if multiply:
                                mb = mask_bias[:, 0:1, :] if mask_tiles == 1 else mask_bias[:, bass.ds((n - 1) * UT + s // CT, 1), :]
                                pool.wait_ge(masked, m + 1)
                                pool.tensor_tensor(score_[:], score_[:], mb.to_broadcast([P, CHUNK, SEQ]),
                                                   ALU.add).then_inc(biased, 1)
                        if this and s == KB_SLOT and ksteps == 2:
                            spread_keys(n, u, 1)
                        if mid:
                            pool.wait_ge(top_done, m + 1)
                            pool.tensor_tensor(score_[:], score_[:], top[s % 2][:].rearrange("p (h a) -> p h a", a=1)
                                               .to_broadcast([P, CHUNK, SEQ]), ALU.subtract).then_inc(shifted, 1)
                units(pool, slot)

            @block.tensor
            def _(pe):
                pe.wait_ge(bias_spread, 1)
                for i in range(NV):
                    last = pe.matmul(attn_ps[:, i:i + 1], bias_rows[0:1, i, :], chip.one[0:1, 0:1], start=True, stop=True)
                last.then_inc(bias_turned, 1)
                pe.wait_ge(w_lo_done, 4)

                def project(n, u, s):
                    tokens = token_range(n)
                    out = proj_ps[s % 2]
                    if s == 0 and (not isinstance(n, int) or n > 0):
                        pe.wait_ge(v_taken, n * UT)
                    if s == QK:
                        pe.wait_ge(staged_hi, n + 1)
                        pe.wait_ge(staged_lo, n + 1)
                    if s >= 2:
                        if s - 2 < QK:
                            pe.wait_ge(qk_taken, n * QK + s - 1)
                        else:
                            pe.wait_ge(v_taken, n * UT + s - 2 - QK + 1)
                    if s < QK:
                        src, w_, first = (chip_h, wq, 2 * s) if s < 2 else (source, wk, 2 * (s - 2))
                        for x in range(2 if s < 2 or KS == 4 else 1):
                            for c in range(CH):
                                last = product(pe, out[:, x * UN:(x + 1) * UN], w_[0][:, c, first + x, :], w_[1][:, c, first + x, :],
                                               src[0][:, c, tokens], src[1][:, c, tokens], start=c == 0, stop=c == CH - 1)
                    else:
                        t = s - QK
                        for b in range(HB):
                            for c in range(CH):
                                both = [stage[u][x][:, c, (t * HB + b) * P:(t * HB + b + 1) * P] for x in range(2)]
                                last = product(pe, out[:, b * VC:(b + 1) * VC], both[0], both[1], wv[0][:, c, :], wv[1][:, c, :],
                                               start=c == 0, stop=c == CH - 1)
                    last.then_inc(proj_made, 1)

                def scores(n, v, s, m):
                    t, part = s // CT, s % CT
                    if s == 0:
                        pe.wait_ge(kb_made, n * ksteps)
                        pe.wait_ge(qk_taken, n * QK)
                    if not isinstance(m, int) or m >= 2:
                        pe.wait_ge(turned_taken, m - 1)
                    flat = score_ps[s % 2][:].rearrange("p h k -> p (h k)")
                    if CT == 1:
                        for x in range(QS):
                            last = pe.matmul(flat[:, x * PER * SEQ:(x + 1) * PER * SEQ], q[v][:, x, t, :],
                                             kb[v][:, x * UT + t, :, :].rearrange("p h k -> p (h k)"), start=True, stop=True)
                    else:
                        for x in range(2):
                            last = pe.matmul(flat[:, x * PER * SEQ:(x + 1) * PER * SEQ], q[v][:, part * 2 + x, t, :],
                                             kb[v][:, t, :, :].rearrange("p h k -> p (h k)"), start=True, stop=True)
                    last.then_inc(scores_made, 1)

                def turn(m, b):
                    pe.wait_ge(exp_done, m + 1)
                    flat = score[b][:].rearrange("p h k -> p (h k)")
                    out = score_ps[b][:].rearrange("p h k -> p (h k)")
                    for x in range(CHUNK // 2):
                        last = pe.transpose(out[:, x * P:(x + 1) * P], flat[:, x * P:(x + 1) * P], chip.ident[:])
                    last.then_inc(turned, 1)

                def attend(n, m, s, values):
                    tile, t, part = n * UT - UT + s // CT, s // CT % UT, s % CT
                    pe.wait_ge(turned_taken, m + 1)
                    if s == 0:
                        pe.wait_ge(v_taken, n * UT)
                    if part == 0 and (not isinstance(tile, int) or tile > 0):
                        pe.wait_ge(rows_done, tile)
                    for x in range(CHUNK // 2):
                        pair = x % (kv_heads // 2)
                        col = (part * CHUNK + 2 * x) * HW
                        for b in range(HB):
                            last = pe.matmul(attn_ps[b * SEQ:(b + 1) * SEQ, col:col + 2 * HW],
                                             weight_t[:, x, b * SEQ:(b + 1) * SEQ],
                                             values[:, t * HB + b, 2 * pair:2 * pair + 2, :].rearrange("p h w -> p (h w)"),
                                             start=True, stop=True)
                    last.then_inc(attn_made, 1)

                def turn_rows(tile):
                    pe.wait_ge(rows_done, tile + 1)
                    if not isinstance(tile, int) or tile > 0:
                        pe.wait_ge(out_added, tile)
                    for c in range(CH):
                        last = pe.transpose(out_ps[:, 0, c * P:(c + 1) * P], rows[:, c * P:(c + 1) * P], chip.ident[:])
                    last.then_inc(rows_turned, 1)

                def output(tile):
                    pe.wait_ge(o_hi_done, tile + 1)
                    pe.wait_ge(o_lo_done, tile + 1)
                    for c in range(CH):
                        last = product(pe, out_ps[:, 1, :], o_t[0][:, c, :], o_t[1][:, c, :], wo[0][:, c, :], wo[1][:, c, :],
                                       start=c == 0, stop=c == CH - 1)
                    last.then_inc(out_made, 1)

                def slot(n, j, this, mid, prev):
                    u, v = j % 2, (j - 1) % 2
                    for s, m, last, ended in steps(n, mid, prev):
                        if mid:
                            scores(n, v, s, m)
                        if ended is not None:
                            turn_rows(ended)
                        if this:
                            for x in FILL[s][0]:
                                project(n, u, x)
                        if last:
                            turn(m - 1, (s - 1) % 2)
                        if ended is not None:
                            output(ended)
                        if this:
                            for x in FILL[s][1]:
                                project(n, u, x)
                        if last:
                            attend(n, m - 1, s - 1, vb[v] if s > 0 else vb[u])
                units(pe, slot)

            @block.scalar
            def _(act):
                act.dma_start(bias_in_rows[0:1, 0:D], q_in[1].rearrange("(a n) -> a n", a=1)).then_inc(bias_in, 16)
                act.dma_start(bias_in_rows[0:1, D:D + VC], k_in[1].rearrange("(a n) -> a n", a=1)).then_inc(bias_in, 16)
                act.dma_start(bias_in_rows[0:1, D + VC:D + 2 * VC], v_in[1].rearrange("(a n) -> a n", a=1)).then_inc(bias_in, 16)
                if mask_tiles == 1:
                    for b in range(HB):
                        act.dma_start(masks[b * SEQ:(b + 1) * SEQ, 0, :], mask[0, 0]).then_inc(mask_in, 16)
                else:
                    act.dma_start(masks[:], mask.rearrange("b a q k -> (b a q) k")
                                  .rearrange("(t p) k -> p t k", p=P)).then_inc(mask_in, 16)
                act.dma_start(bo_row[:], out_in[1].rearrange("(a n) -> a n", a=1).to_broadcast([P, D])).then_inc(bo_in, 16)
                for i, (w_, src) in enumerate(((wq, dup_q), (wk, dup_k), (wv, raw_v), (wo, raw_o))):
                    if i == 0:
                        act.wait_ge(dup_done, 1)
                        act.wait_ge(params_in, 64)
                    act.activation(w_[0][:], src[:], ACT.Copy).then_inc(w_hi_done, 1)
                act.wait_ge(bias_ready, 1)
                act.wait_ge(masks_made, 8)

                def slot(n, j, this, mid, prev):
                    u = j % 2

                    def take(s):
                        if s >= QK:
                            return
                        act.wait_ge(proj_made, n * STEPS + s + 1)
                        pair = range(2 if s < 2 or KS == 4 else 1)
                        if s == 2 and mid:
                            act.wait_ge(kb_made, n * ksteps)
                        for x in pair:
                            part = proj_ps[s % 2][:, x * UN:(x + 1) * UN].rearrange("p (t b k) -> p t b k", b=HB, k=SEQ)
                            for b in range(HB):
                                half = slice(b * HALF, (b + 1) * HALF)
                                if s < 2:
                                    out = q[u][half, 2 * s + x, :, b * SEQ:(b + 1) * SEQ]
                                    bias = bias_cols[half, 2 * s + x:2 * s + x + 1]
                                else:
                                    out = kc[(s - 2) % 2][half, x * UT:(x + 1) * UT, :]
                                    i = QS + 2 * (s - 2) + x
                                    bias = bias_cols[half, i:i + 1]
                                last = act.activation(out, part[half, :, b, :], ACT.Identity, bias=bias)
                        last.then_inc(qk_taken, 1)

                    for s, m, last, ended in steps(n, mid, prev):
                        if ended is not None:
                            act.wait_ge(rows_turned, ended + 1)
                            for c in range(CH):
                                hi = act.activation(o_t[0][:, c, :], out_ps[:, 0, c * P:(c + 1) * P], ACT.Identity,
                                                    bias=bias_cols[:, QS + KS + c:QS + KS + c + 1])
                            hi.then_inc(o_hi_done, 1)
                        if last:
                            act.wait_ge(shifted, m)
                            act.activation(score[(s - 1) % 2][:], score[(s - 1) % 2][:], ACT.Exp).then_inc(exp_done, 1)
                        if this:
                            for x in FILL[s][0]:
                                take(x)
                        if last:
                            act.wait_ge(turned, m)
                            act.activation(weight_t[:].rearrange("p x q -> p (x q)"),
                                           score_ps[(s - 1) % 2][:].rearrange("p h k -> p (h k)"), ACT.Copy).then_inc(turned_taken, 1)
                        if this:
                            for x in FILL[s][1]:
                                take(x)
                            if s == 0:
                                for c in range(CH):
                                    hi = act.activation(
                                        stage[u][0][:, c, :].rearrange("p (b r k) -> p b r k", r=2, k=SEQ),
                                        source[0][:, c, token_range(n)].bitcast(F32).rearrange("p (b a k) -> p b a k", a=1, k=SEQ)
                                        .to_broadcast([P, UT * HB, 2, SEQ]), ACT.Copy)
                                hi.then_inc(staged_hi, 1)
                units(act, slot)

            @block.vector
            def _(dve):
                dve.wait_ge(bias_in, 48)
                dve.wait_ge(masks_made, 8)
                for side in range(2):
                    dve.tensor_copy(halves(bias_rows[:, 0:QS, :], side), sets(bias_in_rows[:, 0:D], D))
                    dve.tensor_copy(bias_rows[:, QS:QS + KS, side * HALF:(side + 1) * HALF],
                                    bias_in_rows[:, D:D + VC].rearrange("p (s f) -> p s f", f=HALF))
                value_bias = bias_in_rows[:, D + VC:D + 2 * VC]
                if GROUPS == 1:
                    last = dve.tensor_copy(bias_rows[:, QS + KS:NV, :].rearrange("p c f -> p (c f)"), value_bias)
                else:
                    last = dve.tensor_copy(bias_rows[:, QS + KS:NV, :].rearrange("p c (k g f) -> p (c k) g f", g=GROUPS, f=HD),
                                           value_bias.rearrange("p (k a f) -> p k a f", a=1, f=HD)
                                           .to_broadcast([1, kv_heads, GROUPS, HD]))
                last.then_inc(bias_spread, 1)
                dve.wait_ge(bias_turned, 1)
                dve.tensor_copy(bias_cols[:], attn_ps[:, 0:NV]).then_inc(bias_ready, 1)
                if multiply:
                    dve.wait_ge(mask_in, 32 if mask_tiles == 1 else 16)
                    dve.tensor_scalar(mask_bias[:], masks[:], -1.0, 10000.0, ALU.add, ALU.mult).then_inc(mask_ready, 1)
                    dve.wait_ge(mask_ready, 1)
                    dve.tensor_scalar(masks[:], masks[:], score_scale, None, ALU.mult).then_inc(mask_ready, 1)
                    dve.wait_ge(mask_ready, 2)
                else:
                    dve.wait_ge(mask_in, 32 if mask_tiles == 1 else 16)
                dve.wait_ge(params_in, 64)
                for c in range(CH):
                    for side in range(2):
                        dve.tensor_copy(halves(dup_q[:, c, :, :], side), sets(raw_q[:, c, :], D))
                        last = dve.tensor_copy(dup_k[:, c, :, side * HALF:(side + 1) * HALF],
                                               raw_k[:, c, :].rearrange("p (s f) -> p s f", f=HALF))
                last.then_inc(dup_done, 1)
                dve.wait_ge(dup_done, 1)
                for i, (w_, src) in enumerate(((wq, dup_q), (wk, dup_k), (wv, raw_v), (wo, raw_o))):
                    dve.wait_ge(w_hi_done, i + 1)
                    dve.tensor_tensor(w_[1][:], src[:], w_[0][:].bitcast(F32), ALU.subtract).then_inc(w_lo_done, 1)
                dve.wait_ge(bo_added, 1)

                def slot(n, j, this, mid, prev):
                    u = j % 2

                    def mask_scores(s, m):
                        mk = masks[:, 0:1, :] if mask_tiles == 1 else masks[:, bass.ds((n - 1) * UT + s // CT, 1), :]
                        mk = mk.to_broadcast([P, CHUNK, SEQ])
                        dve.wait_ge(scores_made, m + 1)
                        if multiply:
                            dve.tensor_tensor(score[s % 2][:], score_ps[s % 2][:], mk, ALU.mult).then_inc(masked, 1)
                        else:
                            dve.scalar_tensor_tensor(score[s % 2][:], score_ps[s % 2][:], score_scale, mk,
                                                     ALU.mult, ALU.add).then_inc(masked, 1)

                    def take_values(x):
                        if x < QK:
                            return
                        t = x - QK
                        dve.wait_ge(proj_made, n * STEPS + x + 1)
                        dve.tensor_tensor(vb[u][:, t * HB:(t + 1) * HB, :, 0:HD],
                                          proj_ps[x % 2][:, 0:HB * VC].rearrange("p (b h f) -> p b h f", b=HB, f=HD),
                                          side_mask[:].rearrange("p (a h) f -> p a h f", a=1).to_broadcast([P, HB, kv_heads, HD]),
                                          ALU.mult).then_inc(v_taken, 1)

                    def normalise(tile):
                        dve.wait_ge(attn_made, tile * CT + CT)
                        done = attn_ps[:, 0:heads * HW].rearrange("p (h w) -> p h w", w=HW)
                        dve.reciprocal(inverse[:], done[:, :, HD]).then_inc(inverse_done, 1)
                        dve.wait_ge(inverse_done, tile + 1)
                        if GROUPS == 1:
                            dve.tensor_tensor(rows[:].rearrange("p (h f) -> p h f", f=HD), done[:, :, 0:HD],
                                              inverse[:].rearrange("p (h a) -> p h a", a=1).to_broadcast([P, heads, HD]),
                                              ALU.mult).then_inc(rows_done, 1)
                        else:
                            dve.tensor_tensor(rows[:].rearrange("p (k g f) -> p g k f", g=GROUPS, f=HD),
                                              done[:, :, 0:HD].rearrange("p (g k) f -> p g k f", g=GROUPS),
                                              inverse[:].rearrange("p (g k a) -> p g k a", g=GROUPS, a=1)
                                              .to_broadcast([P, GROUPS, kv_heads, HD]), ALU.mult).then_inc(rows_done, 1)

                    for s, m, last, ended in steps(n, mid, prev):
                        if ended is not None:
                            normalise(ended)
                        if mid:
                            mask_scores(s, m)
                        if ended is not None:
                            dve.wait_ge(o_hi_done, ended + 1)
                            for c in range(CH):
                                lo = dve.scalar_tensor_tensor(o_t[1][:, c, :], out_ps[:, 0, c * P:(c + 1) * P],
                                                              bias_cols[:, QS + KS + c:QS + KS + c + 1],
                                                              o_t[0][:, c, :].bitcast(F32), ALU.add, ALU.subtract)
                            lo.then_inc(o_lo_done, 1)
                        if this and s == 0:
                            for c in range(CH):
                                lo = dve.tensor_copy(
                                    stage[u][1][:, c, :].rearrange("p (b r k) -> p b r k", r=2, k=SEQ),
                                    source[1][:, c, token_range(n)].bitcast(F32).rearrange("p (b a k) -> p b a k", a=1, k=SEQ)
                                    .to_broadcast([P, UT * HB, 2, SEQ]))
                            lo.then_inc(staged_lo, 1)
                        if mid:
                            dve.wait_ge(biased if multiply else masked, m + 1)
                            dve.tensor_reduce(top[s % 2][:], score[s % 2][:], AX, ALU.max).then_inc(top_done, 1)
                        if this:
                            for x in FILL[s][0]:
                                take_values(x)
                        if ended is not None:
                            dve.wait_ge(out_made, ended + 1)
                            tile = (chip.x[:, ended, :] if isinstance(ended, int) else
                                    chip.x[:, bass.ds(ended, 1), :].rearrange("p a d -> p (a d)"))
                            dve.tensor_tensor(tile, out_ps[:, 1, :], tile, ALU.add).then_inc(out_added, 1)
                        if this:
                            for x in FILL[s][1]:
                                take_values(x)
                units(dve, slot)


def normalise_rows(chip, tag, gamma, beta):
    nc = chip.nc
    with ExitStack() as stack:
        def sb(name, shape):
            return chip.sb(f"{tag}_{name}", shape, F32, stack)
        stats, moments = sb("stats", [P, GT, 6]), sb("moments", [P, GT, 2])
        spread, inverse, idle = sb("spread", [P, GT]), sb("inverse", [P, GT]), sb("idle", [P, 1])
        gain, shift = sb("gain", [P, D]), sb("shift", [P, D])
        rows = sb("rows", [P, GT, D])
        gain_in, stats_done, moments_done, spread_done, inverse_done, rows_done, scaled, shifted, done = (
            chip.sem(f"{tag}_{s}") for s in ("gain_in", "stats_done", "moments_done", "spread_done", "inverse_done",
                                             "rows_done", "scaled", "shifted", "done"))
        with nc.Block() as block:
            @block.sync
            def _(sp):
                sp.dma_start(gain[:], gamma.rearrange("(a n) -> a n", a=1).to_broadcast([P, D])).then_inc(gain_in, 16)
                sp.dma_start(shift[:], beta.rearrange("(a n) -> a n", a=1).to_broadcast([P, D])).then_inc(gain_in, 16)

            @block.scalar
            def _(act):
                with act.Fori(0, NG) as g:
                    act.wait_ge(moments_done, g * GT + GT)
                    act.activation(spread[:], moments[:, :, 1], ACT.Sqrt, bias=chip.eps[:, 1:2]).then_inc(spread_done, 1)

            @block.vector
            def _(dve):
                with dve.Fori(0, NG) as g:
                    tiles = [chip.x[:, bass.ds(g * GT + j, 1), :].rearrange("p a d -> p (a d)") for j in range(GT)]
                    for j in range(GT):
                        dve.bn_stats(stats[:, j, :], tiles[j]).then_inc(stats_done, 1)
                    dve.wait_ge(stats_done, g * GT + GT)
                    dve.memset(idle[:], 0.0)
                    for j in range(GT):
                        dve.bn_aggr(moments[:, j, :], stats[:, j, :]).then_inc(moments_done, 1)
                    dve.wait_ge(spread_done, g + 1)
                    dve.reciprocal(inverse[:], spread[:]).then_inc(inverse_done, 1)
                    dve.wait_ge(inverse_done, g + 1)
                    for j in range(GT):
                        dve.tensor_scalar(rows[:, j, :], tiles[j], moments[:, j, 0:1], inverse[:, j:j + 1],
                                          ALU.subtract, ALU.mult).then_inc(rows_done, 1)
                    dve.wait_ge(done, g + 1)

            @block.gpsimd
            def _(pool):
                pool.wait_ge(gain_in, 32)
                with pool.Fori(0, NG) as g:
                    group = chip.x[:, bass.ds(g * GT, GT), :]
                    pool.wait_ge(rows_done, g * GT + GT)
                    pool.tensor_tensor(rows[:], rows[:], gain[:].rearrange("p (a n) -> p a n", a=1)
                                       .to_broadcast([P, GT, D]), ALU.mult).then_inc(scaled, 1)
                    pool.wait_ge(scaled, g + 1)
                    pool.tensor_tensor(rows[:], rows[:], shift[:].rearrange("p (a n) -> p a n", a=1)
                                       .to_broadcast([P, GT, D]), ALU.add).then_inc(shifted, 1)
                    pool.wait_ge(shifted, g + 1)
                    pool.tensor_copy(group, rows[:]).then_inc(done, 1)


def layer0(chip):
    I = chip.inputs
    for n in (1, 2):
        turn_input(chip, f"l0n{n}", I[f"L0_xattn_ln{n}_scale"], I[f"L0_xattn_ln{n}_offset"])
        wide_attention(chip, f"l0a{n}", n)
        chip.end_stage()
    layer0_mlp(chip)


def layer0_mlp(chip):
    I = chip.inputs
    turn_input(chip, "l0n3", I["L0_xattn_ln_mlp_scale"], I["L0_xattn_ln_mlp_offset"])
    dense_mlp(chip, "l0m", I["L0_xattn_w_fc1"], I["L0_xattn_b_fc1"], I["L0_xattn_w_fc2"], I["L0_xattn_b_fc2"], ACT.Gelu)
    chip.end_stage()


def layer1(chip):
    I = {k[9:]: v for k, v in chip.inputs.items() if k.startswith("L1_xattn_")}
    turn_input(chip, "l1t")
    narrow_attention(chip, "l1a", 32, 8, (I["Wq"], I["bq"]), (I["Wk"], I["bk"]), (I["Wv"], I["bv"]), (I["Wo"], I["bo"]),
                     (chip.ctx_hi, chip.ctx_lo), chip.inputs["mask_Bx1xSxS2_ff0"], False,
                     1.0 / float(np.sqrt(np.float32(8))))
    normalise_rows(chip, "l1n", I["gamma"], I["beta"])
    chip.end_stage()


def layer3(chip):
    I = {k[9:]: v for k, v in chip.inputs.items() if k.startswith("L3_xattn_")}
    scale = 1.0 / float(np.sqrt(np.float32(16)))
    turn_input(chip, "l3n1", I["ln1_s"], I["ln1_b"])
    w, b = I["w_qkv"], I["b_qkv"]
    parts = [(w[:, i * D:(i + 1) * D], b[i * D:(i + 1) * D]) for i in range(3)]
    narrow_attention(chip, "l3a1", 16, 16, *parts, (I["w_ao"], I["b_ao"]), (chip.h_hi, chip.h_lo),
                     chip.inputs["mask_1x1xSxS2_fc1"], True, scale)
    chip.end_stage()
    turn_input(chip, "l3n2", I["ln2_s"], I["ln2_b"])
    w, b = I["w_kv"], I["b_kv"]
    parts = [(w[:, i * D:(i + 1) * D], b[i * D:(i + 1) * D]) for i in range(2)]
    narrow_attention(chip, "l3a2", 16, 16, (I["w_q"], I["b_q"]), *parts, (I["w_co"], I["b_co"]), (chip.ctx_hi, chip.ctx_lo),
                     chip.inputs["mask_Bx1xSxS2_ff1"], True, scale)
    chip.end_stage()
    turn_input(chip, "l3n3", I["ln3_s"], I["ln3_b"])
    dense_mlp(chip, "l3m", I["w1"], I["b1"], I["w2"], I["b2"], ACT.Gelu_apprx_tanh)


def layer2(chip):
    nc = chip.nc
    I = {k[9:]: v for k, v in chip.inputs.items() if k.startswith("L2_xattn_")}
    NB = HB * CH
    tag = "l2"
    with ExitStack() as stack:
        def sb(name, shape):
            return chip.sb(f"{tag}_{name}", shape, F32, stack)

        def sem(name):
            return chip.sem(f"{tag}_{name}")
        context = sb("context", [P, NT, D])
        w_rows, w_cols = sb("w_rows", [P, 4, P]), sb("w_cols", [P, 4, P])
        bias = sb("bias", [P, 4])
        stats = [sb(f"stats{i}", [P, 6]) for i in range(2)]
        moments = sb("moments", [P, 2, NT, 2])
        pair_moments, pair_done = sb("pair_moments", [P, 2, 2]), sem("pair_done")
        spread, inverse = sb("spread", [P, 2, NT]), sb("inverse", [P, 2, NT])
        normed = [sb(f"normed{b}", [P, 2, D]) for b in range(2)]
        held = [sb(f"held{b}", [P, D]) for b in range(2)]
        maps = [sb(f"maps{b}", [P, 2, D]) for b in range(2)]
        value_t = [sb(f"value_t{b}", [P, CH, P]) for b in range(2)]
        top, total, inv = sb("top", [P, NB]), sb("total", [P, NB]), sb("inv", [P, NB])
        expd, weight = sb("expd", [P, NB, D]), sb("weight", [P, NB, D])
        weight_t = sb("weight_t", [P, HB, CH, D])
        attended = sb("attended", [P, D])
        conv_ps = chip.ps(f"{tag}_conv_ps", [P, 2, D], stack)
        value_ps = chip.ps(f"{tag}_value_ps", [P, 512], stack)
        score_ps = chip.ps(f"{tag}_score_ps", [P, HB, CH, D], stack)
        turned_ps = chip.ps(f"{tag}_turned_ps", [P, HB, CH, D], stack)
        mo_ps, out_ps = chip.ps(f"{tag}_mo_ps", [P, 512], stack), chip.ps(f"{tag}_out_ps", [P, 512], stack)
        w_zeroed, w_in, b_in, ctx_in, w_turned, w_ready = (sem(s) for s in ("w_zeroed", "w_in", "b_in", "ctx_in", "w_turned", "w_ready"))
        stats_done, moments_done, spread_done, inverse_done, normed_done = (
            sem(s) for s in ("stats_done", "moments_done", "spread_done", "inverse_done", "normed_done"))
        conv_made, value_made, maps_done, value_done, score_made, top_done, exp_done, inv_done, weight_done = (
            sem(s) for s in ("conv_made", "value_made", "maps_done", "value_done", "score_made", "top_done", "exp_done", "inv_done", "weight_done"))
        turned, turned_taken, mo_made, mo_done, out_made, out_done = (
            sem(s) for s in ("turned", "turned_taken", "mo_made", "mo_done", "out_made", "out_done"))

        with nc.Block() as block:
            @block.sync
            def _(sp):
                sp.dma_start(context[:], chip.inputs["ctx_2048"].rearrange("b s d -> (b s) d")
                             .rearrange("(t p) d -> p t d", p=P)).then_inc(ctx_in, 16)
                sp.wait_ge(w_zeroed, 1)
                for i, k in enumerate(("Wn", "Wm", "Wl", "Wo")):
                    for b in range(HB):
                        half = slice(b * SEQ, (b + 1) * SEQ)
                        sp.dma_start(w_rows[half, i, half], I[k]).then_inc(w_in, 16)
                        sp.dma_start(bias[half, i:i + 1], I["b" + k[1]].rearrange("(p a) -> p a", a=1)).then_inc(b_in, 16)

            @block.gpsimd
            def _(pool):
                pool.memset(w_rows[:], 0.0).then_inc(w_zeroed, 1)

            @block.scalar
            def _(act):
                act.wait_ge(moments_done, 2 * NT)
                act.activation(spread[:], moments[:, :, :, 1], ACT.Sqrt, bias=chip.eps[:, 0:1]).then_inc(spread_done, 1)

            @block.tensor
            def _(pe):
                pe.wait_ge(w_in, 16 * 4 * HB)
                for i in range(4):
                    last = pe.transpose(value_ps[:, i * P:(i + 1) * P], w_rows[:, i, :], chip.ident[:])
                last.then_inc(w_turned, 1)

            @block.vector
            def _(dve):
                dve.wait_ge(ctx_in, 16)
                with dve.Fori(0, NT) as t:
                    for i, src in enumerate((chip.x, context)):
                        dve.bn_stats(stats[i][:], src[:, bass.ds(t, 1), :].rearrange("p a d -> p (a d)")).then_inc(stats_done, 1)
                    dve.wait_ge(stats_done, t * 2 + 2)
                    dve.memset(top[:, 0:1], 0.0)
                    for i in range(2):
                        dve.bn_aggr(pair_moments[:, i, :], stats[i][:]).then_inc(pair_done, 1)
                    dve.wait_ge(pair_done, t * 2 + 2)
                    dve.tensor_copy(moments[:, :, bass.ds(t, 1), :].rearrange("p i a m -> p i (a m)"),
                                    pair_moments[:]).then_inc(moments_done, 2)
                dve.wait_ge(spread_done, 1)
                dve.reciprocal(inverse[:], spread[:]).then_inc(inverse_done, 1)
                dve.wait_ge(w_turned, 1)
                dve.tensor_copy(w_cols[:].rearrange("p i n -> p (i n)"), value_ps[:]).then_inc(w_ready, 1)

        def tiles(engine, slot):
            slot(0, 0, True, False, True)
            with engine.Fori(0, NT // 2 - 1) as i:
                for j in (1, 2):
                    slot(i * 2 + j, j, True, True, True)
            for j in (1, 2):
                slot(NT - 2 + j, j, j == 1, True, False)

        with nc.Block() as block:
            @block.sync
            def _(sp):
                sp.wait_ge(b_in, 16 * 4 * HB)

            @block.tensor
            def _(pe):
                def slot(n, j, this, prev, more):
                    u, v = j % 2, (j - 1) % 2
                    if this:
                        pe.wait_ge(normed_done, n + 1)
                        if prev:
                            pe.wait_ge(maps_done, n)
                        for i in range(2):
                            last = pe.matmul(conv_ps[:, i, :], w_cols[:, i, :], normed[u][:, i, :], start=True, stop=True)
                        last.then_inc(conv_made, 1)
                        if prev:
                            pe.wait_ge(value_done, n)
                        for c in range(CH):
                            last = pe.matmul(value_ps[:, c * P:(c + 1) * P], held[u][:, c * P:(c + 1) * P], w_cols[:, 2, :],
                                             start=True, stop=True)
                        last.then_inc(value_made, 1)
                    if prev:
                        pe.wait_ge(weight_done, n)
                        for b in range(HB):
                            for t in range(CH):
                                for c in range(CH):
                                    last = pe.transpose(turned_ps[:, b, c, t * P:(t + 1) * P],
                                                        weight[:, b * CH + t, c * P:(c + 1) * P], chip.ident[:])
                        last.then_inc(turned, 1)
                    if this:
                        pe.wait_ge(maps_done, n + 1)
                        for b in range(HB):
                            half = slice(b * SEQ, (b + 1) * SEQ)
                            for t in range(CH):
                                last = pe.matmul(score_ps[:, b, t, :], maps[u][half, 0, t * P:(t + 1) * P], maps[u][half, 1, :],
                                                 start=True, stop=True)
                        last.then_inc(score_made, 1)
                    if prev:
                        pe.wait_ge(turned_taken, n)
                        pe.wait_ge(value_done, n)
                        for b in range(HB):
                            half = slice(b * SEQ, (b + 1) * SEQ)
                            for c in range(CH):
                                last = pe.matmul(mo_ps[half, 0:D], value_t[v][:, c, half], weight_t[:, b, c, :],
                                                 start=c == 0, stop=c == CH - 1)
                        last.then_inc(mo_made, 1)
                        pe.wait_ge(mo_done, n)
                        pe.matmul(out_ps[:, 0:D], w_cols[:, 3, :], attended[:], start=True, stop=True).then_inc(out_made, 1)
                tiles(pe, slot)

            @block.scalar
            def _(act):
                def slot(n, j, this, prev, more):
                    u, v = j % 2, (j - 1) % 2
                    if this:
                        act.wait_ge(conv_made, n + 1)
                        for i in range(2):
                            last = act.activation(maps[u][:, i, :], conv_ps[:, i, :], ACT.Identity, bias=bias[:, i:i + 1])
                        last.then_inc(maps_done, 1)
                    if prev:
                        act.wait_ge(top_done, n * 2)
                        for i in range(NB):
                            last = act.activation(expd[:, i, :], score_ps[:, i // CH, i % CH, :], ACT.Exp,
                                                  bias=top[:, i:i + 1], accum_out=total[:, i:i + 1])
                        last.then_inc(exp_done, 1)
                        act.wait_ge(turned, n)
                        act.activation(weight_t[:].rearrange("p b c t -> p (b c t)"),
                                       turned_ps[:].rearrange("p b c t -> p (b c t)"), ACT.Copy).then_inc(turned_taken, 1)
                        act.wait_ge(mo_made, n)
                        act.activation(attended[:], mo_ps[:, 0:D], ACT.Identity, bias=bias[:, 2:3]).then_inc(mo_done, 1)
                act.wait_ge(b_in, 16 * 4 * HB)
                tiles(act, slot)

            @block.vector
            def _(dve):
                def prepare(n, u):
                    for i, src in enumerate((chip.x, context)):
                        tile = src[:, bass.ds(n, 1), :].rearrange("p a d -> p (a d)")
                        dve.tensor_scalar(normed[u][:, i, :], tile,
                                          moments[:, i, bass.ds(n, 1), 0], inverse[:, i, bass.ds(n, 1)],
                                          ALU.subtract, ALU.mult)
                    dve.tensor_copy(held[u][:], tile).then_inc(normed_done, 1)

                def slot(n, j, this, prev, more):
                    u, v = j % 2, (j - 1) % 2
                    if prev:
                        dve.wait_ge(score_made, n)
                        dve.tensor_reduce(top[:], score_ps[:].rearrange("p b t s -> p (b t) s"), AX, ALU.max).then_inc(top_done, 1)
                        dve.wait_ge(top_done, n * 2 - 1)
                        dve.tensor_scalar(top[:], top[:], -1.0, None, ALU.mult).then_inc(top_done, 1)
                    if this:
                        dve.wait_ge(value_made, n + 1)
                        dve.tensor_copy(value_t[u][:].rearrange("p c n -> p (c n)"), value_ps[:, 0:D]).then_inc(value_done, 1)
                    if more:
                        prepare(n + 1, 1 - u)
                    if prev:
                        dve.wait_ge(exp_done, n)
                        dve.reciprocal(inv[:], total[:]).then_inc(inv_done, 1)
                        dve.wait_ge(inv_done, n)
                        for i in range(NB):
                            last = dve.tensor_scalar(weight[:, i, :], expd[:, i, :], inv[:, i:i + 1], None, ALU.mult)
                        last.then_inc(weight_done, 1)
                        dve.wait_ge(out_made, n)
                        tile = chip.x[:, bass.ds(n - 1, 1), :].rearrange("p a d -> p (a d)")
                        dve.scalar_tensor_tensor(tile, out_ps[:, 0:D], bias[:, 3:4], tile, ALU.add, ALU.add).then_inc(out_done, 1)
                dve.wait_ge(b_in, 16 * 4 * HB)
                prepare(0, 0)
                tiles(dve, slot)
    chip.end_stage()


def build(nc, inputs, out):
    with ExitStack() as stack:
        chip = Chip(nc, inputs, stack)
        load(chip)
        layer0(chip)
        layer1(chip)
        layer2(chip)
        layer3(chip)
        store(chip, out)


_OUT = (BATCH, SEQ, D)


def kernel(**inputs):
    import concourse.bacc as _bacc
    from concourse.bass_utils import run_bass_kernel_spmd as _run

    nc = _bacc.Bacc("TRN2", target_bir_lowering=False, num_devices=1)
    arrays, aps = {}, {}
    for name, a in inputs.items():
        a = np.ascontiguousarray(a)
        arrays[f"in_{name}_dram"] = a
        aps[name] = nc.dram_tensor(f"in_{name}_dram", a.shape, mybir.dt.from_np(a.dtype), kind="ExternalInput").ap()
    out = nc.dram_tensor("out_0_dram", _OUT, F32, kind="ExternalOutput").ap()
    build(nc, aps, out)
    r = _run(nc, [arrays], core_ids=[0])
    return r.results[0]["out_0_dram"]
```

```python
from contextlib import ExitStack

import numpy as np
import concourse.bass as bass
from concourse import mybir

F32 = mybir.dt.float32
F32R = mybir.dt.float32r
ALU = mybir.AluOpType
ACT = mybir.ActivationFunctionType
AX = mybir.AxisListType.X

P = 128
BATCH, SEQ, D = 32, 64, 256
TOK = BATCH * SEQ
NT = TOK // P
GT = 4
NG = NT // GT
GN = GT * P
CH = D // P
HB = P // SEQ


class Chip:

    def __init__(self, nc, inputs, stack):
        self.nc, self.inputs, self.stack = nc, inputs, stack
        self.stage_sems = []
        self.x = self.sb("x", [P, NT, D])
        self.ident = self.sb("ident", [P, P])
        self.one = self.sb("one", [P, 1])
        self.ctx_moments = self.sb("ctx_moments", [P, NT, 2])
        self.x_stats = self.sb("x_stats", [P, NT, 6])
        self.x_moments = self.sb("x_moments", [P, NT, 2])
        self.ctx_inverse = self.sb("ctx_inverse", [P, NT])
        self.minus_half = self.sb("minus_half", [P, 1])
        self.ctx_hi = self.sb("ctx_hi", [P, CH, TOK], F32R)
        self.ctx_lo = self.sb("ctx_lo", [P, CH, TOK], F32R)
        self.h_hi = self.sb("h_hi", [P, CH, TOK], F32R)
        self.h_lo = self.sb("h_lo", [P, CH, TOK], F32R)

    def sb(self, name, shape, dtype=F32, stack=None):
        return (stack or self.stack).enter_context(self.nc.sbuf_tensor(name, shape, dtype))

    def ps(self, name, shape, stack):
        return stack.enter_context(self.nc.psum_tensor(name, shape, F32))

    def sem(self, name):
        self.stage_sems.append(self.nc.alloc_semaphore(name=name))
        return self.stage_sems[-1]

    def end_stage(self):
        self.nc.clear_and_free_semaphores(self.stage_sems)
        self.nc.all_engine_barrier()
        self.stage_sems = []


def tile_of(tensor, t):
    return tensor[:, t, :] if isinstance(t, int) else tensor[:, bass.ds(t, 1), :].rearrange("p a d -> p (a d)")


def measure(chip, dve, t):
    return dve.bn_stats(tile_of(chip.x_stats, t), tile_of(chip.x, t))


def gather_moments(chip, dve, gathered):
    for g in range(NG):
        for t in range(g * GT, (g + 1) * GT):
            last = dve.bn_aggr(chip.x_moments[:, t, :], chip.x_stats[:, t, :])
        last.then_inc(gathered, 1)


def invert_spread(chip, pool, epsilon, spread, inverse, gathered, spread_done, inverse_done):
    for g in range(NG):
        part = slice(g * GT, (g + 1) * GT)
        pool.wait_ge(gathered, g + 1)
        pool.tensor_scalar(spread[:, part], chip.x_moments[:, part, 1], epsilon, None, ALU.add).then_inc(spread_done, 1)
        pool.wait_ge(spread_done, g + 1)
        pool.tensor_tensor(inverse[:, part], spread[:, part], chip.minus_half[:].to_broadcast([P, GT]),
                           ALU.pow).then_inc(inverse_done, 1)


def product(pe, out, wh, wl, mh, ml, start=True, stop=True):
    pe.matmul(out, wh, mh, start=start, stop=False)
    pe.matmul(out, wh, ml, start=False, stop=False)
    return pe.matmul(out, wl, mh, start=False, stop=stop)


def keep_warm(chip, pe, bank, count):
    for _ in range(count):
        pe.transpose(bank[:, 0:P], chip.ident[:], chip.ident[:])


def columns(vector):
    return vector.rearrange("(c p) -> p c", p=P)


def load(chip):
    nc, I = chip.nc, chip.inputs
    with ExitStack() as stack:
        rows = chip.sb("ctx_rows", [P, NT, D], F32, stack)
        turned = [chip.ps(f"ctx_turned{g}", [P, CH, GN], stack) for g in range(NG)]
        whole = [chip.sb(f"ctx_whole{i}", [P, CH, GN], F32, stack) for i in range(2)]
        whole_done = chip.sem("ctx_whole_done")
        x_in = [chip.sem(f"x_in{g}") for g in range(NG)]
        rows_in = [chip.sem(f"ctx_rows_in{g}") for g in range(NG)]
        ident_set, ctx_turned, stats_done = chip.sem("ident_set"), chip.sem("ctx_turned"), chip.sem("ctx_stats_done")
        stats = chip.sb("ctx_stats", [P, NT, 6], F32, stack)
        hi_done, lo_done = chip.sem("ctx_hi_done"), chip.sem("ctx_lo_done")
        x_rows = I["x"].rearrange("b s d -> (b s) d").rearrange("(t p) d -> p t d", p=P)
        ctx_rows = I["ctx_2048"].rearrange("b s d -> (b s) d").rearrange("(t p) d -> p t d", p=P)

        with nc.Block() as block:
            @block.sync
            def _(sp):
                for g in range(NG):
                    sp.dma_start(rows[:, g * GT:(g + 1) * GT, :],
                                 ctx_rows[:, g * GT:(g + 1) * GT, :]).then_inc(rows_in[g], 16)
                for g in range(NG):
                    sp.dma_start(chip.x[:, g * GT:(g + 1) * GT, :], x_rows[:, g * GT:(g + 1) * GT, :]).then_inc(x_in[g], 16)

            @block.gpsimd
            def _(pool):
                pool.memset(chip.one[:], 1.0)
                pool.memset(chip.minus_half[:], -0.5)
                pool.memset(chip.ident[:], 0.0).then_inc(ident_set, 1)
                pool.wait_ge(ident_set, 1)
                pool.affine_select(out=chip.ident[:], in_=chip.ident[:], compare_op=ALU.not_equal, fill=1.0,
                                   base=0, pattern=[[-1, P]], channel_multiplier=1).then_inc(ident_set, 1)
                for g in range(NG):
                    for c in range(CH):
                        pool.wait_ge(whole_done, CH * g + c + 1)
                        pool.tensor_tensor(chip.ctx_lo[:, c, g * GN:(g + 1) * GN], whole[g % 2][:, c, :],
                                           chip.ctx_hi[:, c, g * GN:(g + 1) * GN].bitcast(F32), ALU.subtract).then_inc(lo_done, 1)

            @block.tensor
            def _(pe):
                pe.wait_ge(ident_set, 2)
                for g in range(NG):
                    pe.wait_ge(rows_in[g], 16)
                    for c in range(CH):
                        for j in range(GT):
                            last = pe.transpose(turned[g][:, c, j * P:(j + 1) * P],
                                                rows[:, g * GT + j, c * P:(c + 1) * P], chip.ident[:])
                        last.then_inc(ctx_turned, 1)

            @block.scalar
            def _(act):
                for g in range(NG):
                    for c in range(CH):
                        act.wait_ge(ctx_turned, CH * g + c + 1)
                        act.activation(chip.ctx_hi[:, c, g * GN:(g + 1) * GN], turned[g][:, c, :],
                                       ACT.Copy).then_inc(hi_done, 1)
                        if g >= 2:
                            act.wait_ge(lo_done, (g - 2) * CH + c + 1)
                        act.activation(whole[g % 2][:, c, :], turned[g][:, c, :], ACT.Copy).then_inc(whole_done, 1)

            @block.vector
            def _(dve):
                for g in range(NG):
                    dve.wait_ge(rows_in[g], 16)
                    for t in range(g * GT, (g + 1) * GT):
                        dve.bn_stats(stats[:, t, :], rows[:, t, :]).then_inc(stats_done, 1)
                    for t in range(g * GT, (g + 1) * GT):
                        dve.wait_ge(stats_done, t + 1)
                        dve.bn_aggr(chip.ctx_moments[:, t, :], stats[:, t, :])
                for g in range(NG):
                    dve.wait_ge(x_in[g], 16)
                    for t in range(g * GT, (g + 1) * GT):
                        measure(chip, dve, t)


def turn_input(chip, tag, scale=None, offset=None, beside=None):
    nc = chip.nc
    norm = scale is not None
    beside = beside or {}
    with ExitStack() as stack:
        def sb(name, shape, dtype=F32):
            return chip.sb(f"{tag}_{name}", shape, dtype, stack)

        def sem(name):
            return chip.sem(f"{tag}_{name}")
        spread, inverse = sb("spread", [P, NT]), sb("inverse", [P, NT])
        rows = sb("rows", [P, NT, D]) if norm else chip.x
        TB = 3
        whole = [sb(f"whole{b}", [P, CH, GN]) for b in range(2)]
        gain = sb("gain", [P, 2, CH])
        turned = [chip.ps(f"{tag}_turned{b}", [P, CH, GN], stack) for b in range(TB)]
        idle_ps = chip.ps(f"{tag}_idle_ps", [P, P], stack)
        gain_in, gathered, spread_done, inverse_done, rows_done, turned_done, hi_done, whole_done, lo_done = (
            sem(s) for s in ("gain_in", "gathered", "spread_done", "inverse_done", "rows_done", "turned_done",
                             "hi_done", "whole_done", "lo_done"))

        with nc.Block() as block:
            @block.sync
            def _(sp):
                if norm:
                    sp.dma_start(gain[:, 0, :], columns(scale), allow_slow_non_contiguous=True).then_inc(gain_in, 16)
                    sp.dma_start(gain[:, 1, :], columns(offset), allow_slow_non_contiguous=True).then_inc(gain_in, 16)
                if "sync" in beside:
                    beside["sync"](sp)
                if norm:
                    sp.wait_ge(gain_in, 32)

            @block.gpsimd
            def _(pool):
                if norm:
                    invert_spread(chip, pool, 1e-5, spread, inverse, gathered, spread_done, inverse_done)
                if "gpsimd" in beside:
                    beside["gpsimd"](pool)

            @block.tensor
            def _(pe):
                for g in range(NG):
                    for c in range(CH):
                        if g >= TB:
                            pe.wait_ge(whole_done if norm else lo_done, (g - TB) * CH + c + 1)
                        for j in range(GT):
                            if norm and c == 0:
                                pe.wait_ge(rows_done, g * GT + j + 1)
                            last = pe.transpose(turned[g % TB][:, c, j * P:(j + 1) * P],
                                                rows[:, g * GT + j, c * P:(c + 1) * P], chip.ident[:])
                        last.then_inc(turned_done, 1)
                if "tensor" in beside:
                    beside["tensor"](pe)
                for done in range(CH * 2, CH * NG):
                    pe.wait_ge(whole_done if norm else hi_done, done)
                    keep_warm(chip, pe, idle_ps, 10 if norm else 6)

            @block.scalar
            def _(act):
                if norm:
                    act.wait_ge(gain_in, 32)
                for g in range(NG):
                    if g == NG - 1 and "scalar" in beside:
                        beside["scalar"](act)
                    for c in range(CH):
                        act.wait_ge(turned_done, g * CH + c + 1)
                        hi = chip.h_hi[:, c, g * GN:(g + 1) * GN]
                        if norm:
                            scaled = dict(bias=gain[:, 1, c:c + 1], scale=gain[:, 0, c:c + 1])
                            act.activation(hi, turned[g % TB][:, c, :], ACT.Identity, **scaled).then_inc(hi_done, 1)
                            if g >= 2:
                                act.wait_ge(lo_done, (g - 2) * CH + c + 1)
                            act.activation(whole[g % 2][:, c, :], turned[g % TB][:, c, :], ACT.Identity,
                                           **scaled).then_inc(whole_done, 1)
                        else:
                            act.activation(hi, turned[g % TB][:, c, :], ACT.Copy).then_inc(hi_done, 1)

            @block.vector
            def _(dve):
                def rest(g):
                    for c in range(CH):
                        dve.wait_ge(whole_done if norm else hi_done, g * CH + c + 1)
                        dve.tensor_tensor(chip.h_lo[:, c, g * GN:(g + 1) * GN], (whole[g % 2] if norm else turned[g % TB])[:, c, :],
                                          chip.h_hi[:, c, g * GN:(g + 1) * GN].bitcast(F32), ALU.subtract).then_inc(lo_done, 1)
                if norm:
                    gather_moments(chip, dve, gathered)
                    for t in range(NT):
                        if t % GT == 0:
                            dve.wait_ge(inverse_done, t // GT + 1)
                        dve.tensor_scalar(rows[:, t, :], chip.x[:, t, :], chip.x_moments[:, t, 0:1], inverse[:, t:t + 1],
                                          ALU.subtract, ALU.mult).then_inc(rows_done, 1)
                for g in range(NG):
                    if g == NG - 1 and "vector" in beside:
                        beside["vector"](dve)
                    rest(g)


def store(chip, out):
    rows = out.rearrange("b s d -> (b s) d").rearrange("(t p) d -> p t d", p=P)
    stored = chip.sem("stored")
    with chip.nc.Block() as block:
        @block.sync
        def _(sp):
            sp.dma_start(rows, chip.x[:]).then_inc(stored, 16)
            sp.wait_ge(stored, 16)


def wide_attention(chip, tag, n):
    nc = chip.nc
    H, K = 16, 128
    SCALE = 1.0 / float(np.sqrt(np.float32(K)))
    I = chip.inputs
    wt = {k: I[f"L0_xattn_{k}{n}"] for k in ("wq", "wk", "wv", "wo", "bq", "bk", "bv", "bo", "bias_k", "bias_v")}
    wq_d, wk_d, wv_d = (wt[k].rearrange("(c p) n -> p c n", p=P) for k in ("wq", "wk", "wv"))
    wo_d = wt["wo"].rearrange("(h d) n -> d h n", d=K)
    VW = 32
    BQ, BK, KEY, BV, VALUE = range(5)
    HP = 2
    ITEMS = HP * NG
    PASSES = H // HP

    with ExitStack() as keep:
        def sbk(name, shape, dtype=F32):
            return chip.sb(f"{tag}_{name}", shape, dtype, keep)
        bias_cols = sbk("bias_cols", [P, 5, H])
        learned_weight = sbk("learned_weight", [P, NT, VW])
        value_rows = sbk("value_rows", [P, GT, D])
        wo_all = sbk("wo_all", [P, H, D])
        spread_v = sbk("spread_v", [P, H, P])
        bo_rows = sbk("bo_rows", [P, D])
        wo_in, bo_in, spread_done = (chip.sem(f"{tag}_{s}") for s in ("wo_in", "bo_in", "spread_done"))
        raw = [sbk(f"raw{p}", [P, 2, CH, K]) for p in range(HP)]
        raw_v, raw_o = sbk("raw_v", [P, CH, HP * K]), sbk("raw_o", [P, HP, D])
        raw_in = [chip.sem(f"{tag}_raw_in{p}") for p in range(HP)]
        raw_v_in, raw_o_in = chip.sem(f"{tag}_raw_v_in"), chip.sem(f"{tag}_raw_o_in")

        def fetch(sp, cols, both):
            for p in range(HP):
                for x, src in enumerate((wq_d, wk_d)):
                    sp.dma_start(raw[p][:, x, :, :], src[:, :, cols[p]]).then_inc(raw_in[p], 16)
            sp.dma_start(raw_v[:], wv_d[:, :, both]).then_inc(raw_v_in, 16)
            for p in range(HP):
                sp.dma_start(raw_o[:, p, :], wt["wo"][cols[p], :]).then_inc(raw_o_in, 16)

        with ExitStack() as stack:
            def sb(name, shape, dtype=F32):
                return chip.sb(f"{tag}_{name}", shape, dtype, stack)
            bias_rows = sb("bias_rows", [H, 5, K])
            cols_ps = chip.ps(f"{tag}_cols_ps", [P, 5, H], stack)
            rows_in, zeroed, cols_turned, cols_done = (
                chip.sem(f"{tag}_{s}") for s in ("rows_in", "zeroed", "cols_turned", "cols_done"))

            def sync(sp):
                fetch(sp, [slice(p * K, (p + 1) * K) for p in range(HP)], slice(0, HP * K))
                for i, name in ((BQ, "bq"), (BK, "bk"), (BV, "bv")):
                    sp.dma_start(bias_rows[:, i, :], wt[name].rearrange("(h k) -> h k", k=K)).then_inc(rows_in, 16)
                for i, name in ((KEY, "bias_k"), (VALUE, "bias_v")):
                    sp.dma_start(bias_rows[:, i, :], wt[name].rearrange("a b h k -> (a b h) k")).then_inc(rows_in, 16)
                sp.dma_start(wo_all[:], wo_d).then_inc(wo_in, 16)
                sp.wait_ge(zeroed, 4)
                for r in range(0, P, VW):
                    sp.dma_start(bo_rows[r:r + 1, :], wt["bo"].rearrange("(a n) -> a n", a=1)).then_inc(bo_in, 16)

            def gpsimd(pool):
                pool.memset(bo_rows[:], 0.0).then_inc(zeroed, 1)
                pool.memset(learned_weight[:], 0.0).then_inc(zeroed, 1)
                pool.memset(spread_v[:], 0.0).then_inc(zeroed, 1)
                pool.memset(value_rows[:], 0.0).then_inc(zeroed, 1)
                pool.wait_ge(zeroed, 2)
                pool.memset(learned_weight[:, :, 0:1], 1.0)
                if n == 1:
                    pool.tensor_scalar(chip.ctx_inverse[:], chip.ctx_moments[:, :, 1], 1e-5, None, ALU.add).then_inc(zeroed, 1)
                    pool.wait_ge(zeroed, 5)
                    pool.tensor_tensor(chip.ctx_inverse[:], chip.ctx_inverse[:], chip.minus_half[:].to_broadcast([P, NT]), ALU.pow)

            def tensor(pe):
                pe.wait_ge(rows_in, 80)
                for i in range(5):
                    last = pe.transpose(cols_ps[:, i, :], bias_rows[:, i, :], chip.ident[0:H, 0:H])
                last.then_inc(cols_turned, 1)

            def vector(dve):
                dve.wait_ge(cols_turned, 1)
                dve.tensor_copy(bias_cols[:], cols_ps[:]).then_inc(cols_done, 1)
                dve.wait_ge(cols_done, 1)
                dve.wait_ge(zeroed, 4)
                for r in range(0, P, VW):
                    flat = spread_v[:].rearrange("p h c -> p (h c)")
                    dve.tensor_copy(spread_v[:, :, r], bias_cols[:, BV, :])
                    diag = flat[:, r + 1:r + 1 + (P + 1) * (H - 1) + 1:P + 1]
                    last = dve.tensor_tensor(diag, bias_cols[:, VALUE, :], bias_cols[:, BV, :], ALU.subtract)
                last.then_inc(spread_done, 1)

            turn_input(chip, f"{tag}h", I[f"L0_xattn_ln{n}_scale"], I[f"L0_xattn_ln{n}_offset"],
                       dict(sync=sync, gpsimd=gpsimd, tensor=tensor, vector=vector))

        with ExitStack() as stack:
            def sb(name, shape, dtype=F32):
                return chip.sb(f"{tag}_{name}", shape, dtype, stack)

            def split(name, shape):
                return sb(name + "_hi", shape, F32R), sb(name + "_lo", shape, F32R)
            w = [split(f"w{p}", [P, 2, CH, K]) for p in range(HP)]
            wv, wo = split("wv", [P, CH, HP * K]), split("wo", [P, HP, D])
            head_bias = [sb(f"head_bias{p}", [P, 2]) for p in range(HP)]
            q, k = sb("q", [P, GN]), [sb(f"k{p}", [P, GT * HB, SEQ + 1]) for p in range(HP)]
            v = [sb(f"v{b}", [P, GT, HP * K]) for b in range(2)]
            logit = sb("logit", [P, GT, SEQ + 1])
            expd = sb("expd", [P, GT, SEQ + 1])
            top, total, inverse = sb("top", [P, GT]), sb("total", [P, GT]), sb("inverse", [P, GT])
            weight = sb("weight", [P, GT, P])
            weight_t = sb("weight_t", [P, GN])
            c = [split(f"c{p}", [P, GN]) for p in range(HP)]
            q_ps, k_ps, v_ps, s_ps, t_ps, c_ps = (
                chip.ps(f"{tag}_{x}_ps", [P, GN], stack) for x in ("q", "k", "v", "s", "t", "c"))
            o_ps = chip.ps(f"{tag}_o_ps", [P, GT, D], stack)

            w_hi_done, w_split, wv_hi_done, wv_split, wo_hi_done, wo_split = (
                chip.sem(f"{tag}_{s}") for s in ("w_hi_done", "w_split", "wv_hi_done", "wv_split", "wo_hi_done", "wo_split"))
            q_made, k_made, v_made, s_made, t_made, c_made, o_made = (
                chip.sem(f"{tag}_{x}_made") for x in "qkvstco")
            q_done, k_done, v_done, t_done, c_hi, exp_done = (
                chip.sem(f"{tag}_{x}") for x in ("q_done", "k_done", "v_done", "t_done", "c_hi", "exp_done"))
            c_lo, top_done, shifted, total_done, inverse_done, weight_a, added = (
                chip.sem(f"{tag}_{x}") for x in ("c_lo", "top_done", "shifted",
                                                 "total_done", "inverse_done", "weight_a", "added"))
            weight_b, zero_done = chip.sem(f"{tag}_weight_b"), chip.sem(f"{tag}_zero_done")
            weights_t = sb("weights_t", [P, NG, P])
            values_done, kept, learned_done, learned_turned, learned_taken, pair_made, pair_added = (
                chip.sem(f"{tag}_{x}") for x in ("values_done", "kept", "learned_done", "learned_turned", "learned_taken", "pair_made", "pair_added"))
            pair_ps = (k_ps, v_ps, s_ps)
            PAIRS = NT // 2

            def tiles(j):
                g = (j % ITEMS) // HP
                return slice(g * GT, (g + 1) * GT), slice(g * GN, (g + 1) * GN)

            def passes(engine, slots):
                slots(0, 0, True, False, False)
                slots(0, 1, True, True, False)
                with engine.Fori(0, PASSES - 1) as i:
                    for j in range(2, ITEMS + 2):
                        slots(i, j, True, True, True)
                for j in range(2, ITEMS + 2):
                    slots(PASSES - 1, j, j < ITEMS, j <= ITEMS, True)

            def next_head(i, j):
                more = not (isinstance(i, int) and i == PASSES - 1)
                return j - ITEMS + 1 if more and ITEMS - 1 <= j <= ITEMS else None

            with nc.Block() as block:
                @block.sync
                def _(sp):
                    with sp.Fori(1, PASSES) as i:
                        starts = [sp.snap((i * HP + p) * K) for p in range(HP)]
                        ends, count = sp.snap(i * HP), sp.snap(i * 1)
                        sp.wait_ge(w_split, ends)
                        sp.wait_ge(wv_split, count)
                        sp.wait_ge(wo_split, count)
                        fetch(sp, [bass.ds(start, K) for start in starts], bass.ds(starts[0], HP * K))
                    for p in range(HP):
                        sp.wait_ge(raw_in[p], 32 * PASSES)
                    sp.wait_ge(raw_v_in, 16 * PASSES)
                    sp.wait_ge(raw_o_in, 32 * PASSES)

                @block.gpsimd
                def _(pool):
                    def split_w(i, p):
                        pool.tensor_copy(head_bias[p][:], bias_cols[:, BQ:BK + 1, bass.ds(i * HP + p, 1)]
                                         .rearrange("p a b -> p (a b)"))
                        pool.tensor_copy(k[p][:, :, SEQ:SEQ + 1], bias_cols[:, KEY:KEY + 1, bass.ds(i * HP + p, 1)]
                                         .to_broadcast([P, GT * HB, 1]))
                        pool.wait_ge(w_hi_done, i * HP + p + 1)
                        pool.tensor_tensor(w[p][1][:], raw[p][:], w[p][0][:].bitcast(F32),
                                           ALU.subtract).then_inc(w_split, 1)

                    def slots(i, j, this, mid, prev):
                        n = i * ITEMS + j
                        if j < HP and not prev:
                            split_w(0, j)
                        if mid:
                            if next_head(i, j) is not None:
                                pool.wait_ge(shifted, n)
                                split_w(i + 1, next_head(i, j))
                                pool.wait_ge(w_split, (i + 1) * HP + next_head(i, j) + 1)
                            pool.wait_ge(inverse_done, n)
                            pool.tensor_tensor(weight[SEQ:P, :, SEQ:P], expd[SEQ:P, :, 0:SEQ],
                                               inverse[SEQ:P].rearrange("p (t a) -> p t a", a=1)
                                               .to_broadcast([SEQ, GT, SEQ]), ALU.mult).then_inc(weight_b, 1)
                            pool.wait_ge(weight_b, n)
                        if prev and j == 2:
                            pool.wait_ge(wo_hi_done, i + 1)
                            pool.tensor_tensor(wo[1][:], raw_o[:], wo[0][:].bitcast(F32),
                                               ALU.subtract).then_inc(wo_split, 1)
                            pool.wait_ge(wo_split, i + 1)

                    pool.memset(weight[:], 0.0).then_inc(zero_done, 1)
                    passes(pool, slots)

                @block.tensor
                def _(pe):
                    def slots(i, j, this, mid, prev):
                        n = i * ITEMS + j
                        p = j % HP
                        _, cols = tiles(j)

                        def project(x):
                            out, made = ((q_ps, q_made), (k_ps, k_made))[x]
                            src = ((chip.h_hi, chip.h_lo), (chip.ctx_hi, chip.ctx_lo))[x]
                            for ch in range(CH):
                                last = product(pe, out[:], w[p][0][:, x, ch, :], w[p][1][:, x, ch, :],
                                               src[0][:, ch, cols], src[1][:, ch, cols],
                                               start=ch == 0, stop=ch == CH - 1)
                            last.then_inc(made, 1)
                        def values(heads):
                            for h in heads:
                                last = pe.matmul(o_ps[:, 0, :], spread_v[:, h, :], wo_all[:, h, :], start=h == 0, stop=h == H - 1)
                            if h == H - 1:
                                last.then_inc(values_done, 1)
                        if not mid and this:
                            pe.wait_ge(spread_done, 1)
                            pe.wait_ge(wo_in, 16)
                            values(range(H // 2))
                        if prev:
                            pe.wait_ge(weight_a, n - 1)
                            pe.wait_ge(weight_b, n - 1)
                            for t in range(GT):
                                last = pe.transpose(t_ps[:, t * P:(t + 1) * P], weight[:, t, :], chip.ident[:])
                            last.then_inc(t_made, 1)
                        if prev and not mid:
                            pe.wait_ge(learned_done, 1)
                            for g in range(NG):
                                last = pe.transpose(q_ps[:, g * P:(g + 1) * P], learned_weight[:, g * GT:(g + 1) * GT, :]
                                                    .rearrange("p t w -> p (t w)"), chip.ident[:])
                            last.then_inc(learned_turned, 1)
                        if this:
                            if j % ITEMS < HP:
                                pe.wait_ge(w_split, (i + j // ITEMS) * HP + p + 1)
                            project(0)
                        if prev:
                            pe.wait_ge(t_done, n - 1)
                            if p == 0:
                                pe.wait_ge(v_done, n)
                            for t in range(GT):
                                last = pe.matmul(c_ps[:, t * P:(t + 1) * P], v[(j - HP) // HP % 2][:, t, p * K:(p + 1) * K],
                                                 weight_t[:, t * P:(t + 1) * P], start=True, stop=True)
                            last.then_inc(c_made, 1)
                        if this:
                            project(1)
                        if this:
                            if j % ITEMS == 0:
                                pe.wait_ge(wv_split, i + j // ITEMS + 1)
                            if mid:
                                pe.wait_ge(v_done, n)
                            for t in range(GT // HP):
                                start = cols.start + (p * GT // HP + t) * P
                                tok = slice(start, start + P)
                                for ch in range(CH):
                                    last = product(pe, v_ps[:, t * HP * K:(t + 1) * HP * K], chip.ctx_hi[:, ch, tok],
                                                   chip.ctx_lo[:, ch, tok], wv[0][:, ch, :], wv[1][:, ch, :],
                                                   start=ch == 0, stop=ch == CH - 1)
                            last.then_inc(v_made, 1)
                        if prev and not mid:
                            pe.wait_ge(learned_taken, 1)
                            for i_ in range(PAIRS):
                                if i_ >= len(pair_ps):
                                    pe.wait_ge(pair_added, i_ - len(pair_ps) + 1)
                                for t in (2 * i_, 2 * i_ + 1):
                                    last = pe.matmul(pair_ps[i_ % len(pair_ps)][:, t % 2 * D:(t % 2 + 1) * D],
                                                     weights_t[:, t // GT, :], value_rows[:, t % GT, :], start=True, stop=True)
                                last.then_inc(pair_made, 1)
                        if prev and p == HP - 1:
                            pe.wait_ge(c_hi, n - 1)
                            pe.wait_ge(c_lo, n - 1)
                            pe.wait_ge(wo_split, i + 1)
                            for t in range(GT):
                                tok = slice(t * P, (t + 1) * P)
                                for x in range(HP):
                                    last = product(pe, o_ps[:, t, :], c[x][0][:, tok], c[x][1][:, tok],
                                                   wo[0][:, x, :], wo[1][:, x, :], start=x == 0, stop=x == HP - 1)
                            last.then_inc(o_made, 1)
                        if this:
                            pe.wait_ge(q_done, n + 1)
                            pe.wait_ge(k_done, n + 1)
                            if mid:
                                pe.wait_ge(shifted, n)
                            for t in range(GT):
                                for b in range(HB):
                                    at = (t * HB + b) * SEQ
                                    last = pe.matmul(s_ps[b * SEQ:(b + 1) * SEQ, t * (SEQ + 1):(t + 1) * (SEQ + 1)],
                                                     q[:, at:at + SEQ], k[p][:, t * HB + b, :], start=True, stop=True)
                            last.then_inc(s_made, 1)
                            if not mid:
                                values(range(H // 2, H))
                        if prev and p == 0:
                            pe.wait_ge(c_hi, n - 1)
                            pe.wait_ge(c_lo, n - 1)
                    passes(pe, slots)

                @block.scalar
                def _(act):
                    def split_w(i, p):
                        act.wait_ge(raw_in[p], i * 32 + 32)
                        act.activation(w[p][0][:].rearrange("p x c k -> p (x c k)"),
                                       raw[p][:].rearrange("p x c k -> p (x c k)"), ACT.Copy).then_inc(w_hi_done, 1)

                    def split_wv(i):
                        act.wait_ge(raw_v_in, i * 16 + 16)
                        act.activation(wv[0][:], raw_v[:], ACT.Copy).then_inc(wv_hi_done, 1)

                    def slots(i, j, this, mid, prev):
                        n = i * ITEMS + j
                        p = j % HP
                        if j < HP and not prev:
                            split_w(0, j)
                            if j == 0:
                                split_wv(0)
                        if prev:
                            act.wait_ge(t_made, n - 1)
                            act.activation(weight_t[:], t_ps[:], ACT.Copy).then_inc(t_done, 1)
                        if next_head(i, j) == HP - 1:
                            split_wv(i + 1)
                        if next_head(i, j) == 0:
                            split_w(i + 1, 0)
                        if this:
                            act.wait_ge(q_made, n + 1)
                            act.activation(q[:], q_ps[:], ACT.Identity, bias=head_bias[p][:, 0:1]).then_inc(q_done, 1)
                        if prev:
                            act.wait_ge(c_made, n - 1)
                            act.activation(c[p][0][:], c_ps[:], ACT.Copy).then_inc(c_hi, 1)
                        if mid:
                            act.wait_ge(shifted, n)
                            act.activation(expd[:], logit[:], ACT.Exp, scale=SCALE).then_inc(exp_done, 1)
                        if this:
                            act.wait_ge(k_made, n + 1)
                            act.activation(k[p][:, :, 0:SEQ], k_ps[:].rearrange("p (b k) -> p b k", k=SEQ), ACT.Identity,
                                           bias=head_bias[p][:, 1:2]).then_inc(k_done, 1)
                        if next_head(i, j) == HP - 1:
                            split_w(i + 1, HP - 1)
                        if prev and j == 2:
                            act.wait_ge(raw_o_in, i * 32 + 32)
                            act.activation(wo[0][:], raw_o[:], ACT.Copy).then_inc(wo_hi_done, 1)
                        if this:
                            act.wait_ge(v_made, n + 1)
                            act.activation(v[j // HP % 2][:, p * GT // HP:(p + 1) * GT // HP, :]
                                           .rearrange("p t k -> p (t k)"), v_ps[:], ACT.Copy).then_inc(v_done, 1)
                    passes(act, slots)

                @block.vector
                def _(dve):
                    def split_wv(i):
                        dve.wait_ge(wv_hi_done, i + 1)
                        dve.tensor_tensor(wv[1][:], raw_v[:], wv[0][:].bitcast(F32), ALU.subtract).then_inc(wv_split, 1)

                    def slots(i, j, this, mid, prev):
                        n = i * ITEMS + j
                        p = j % HP
                        if j == 0:
                            split_wv(0)
                        if mid:
                            dve.wait_ge(s_made, n)
                            dve.tensor_reduce(top[:], s_ps[:, 0:GT * (SEQ + 1)].rearrange("p (t k) -> p t k", t=GT),
                                              AX, ALU.max).then_inc(top_done, 1)
                            dve.wait_ge(top_done, n)
                            if j >= 2:
                                dve.wait_ge(exp_done, n - 1)
                            dve.tensor_tensor(logit[:], s_ps[:, 0:GT * (SEQ + 1)].rearrange("p (t k) -> p t k", t=GT),
                                              top[:].rearrange("p (t a) -> p t a", a=1).to_broadcast([P, GT, SEQ + 1]),
                                              ALU.subtract).then_inc(shifted, 1)
                        if next_head(i, j) == HP - 1:
                            split_wv(i + 1)
                        if prev:
                            dve.wait_ge(c_hi, n - 1)
                            dve.tensor_tensor(c[p][1][:], c_ps[:], c[p][0][:].bitcast(F32), ALU.subtract).then_inc(c_lo, 1)
                        if mid:
                            dve.wait_ge(exp_done, n)
                            dve.tensor_reduce(total[:], expd[:], AX, ALU.add).then_inc(total_done, 1)
                            dve.wait_ge(total_done, n)
                            dve.reciprocal(inverse[:], total[:]).then_inc(inverse_done, 1)
                            dve.wait_ge(inverse_done, n)
                            dve.tensor_tensor(weight[0:SEQ, :, 0:SEQ], expd[0:SEQ, :, 0:SEQ],
                                              inverse[0:SEQ].rearrange("p (t a) -> p t a", a=1)
                                              .to_broadcast([SEQ, GT, SEQ]), ALU.mult).then_inc(weight_a, 1)
                            learned = dve.tensor_tensor(
                                learned_weight[:, tiles(j - 1)[0], bass.ds((i + (j - 1) // ITEMS) * HP + (j - 1) % HP + 1, 1)],
                                expd[:, :, SEQ:SEQ + 1], inverse[:].rearrange("p (t a) -> p t a", a=1), ALU.mult)
                            if not this:
                                learned.then_inc(learned_done, 1)
                        if mid and not prev:
                            dve.wait_ge(values_done, 1)
                            dve.wait_ge(bo_in, 16 * (P // VW))
                            for t in range(GT):
                                r = slice(VW * t, VW * (t + 1))
                                dve.tensor_tensor(value_rows[r, t, :], o_ps[r, 0, :], bo_rows[r, :], ALU.add).then_inc(kept, 1)
                        if prev and not mid:
                            dve.wait_ge(learned_turned, 1)
                            dve.tensor_copy(weights_t[:].rearrange("p g q -> p (g q)"), q_ps[:]).then_inc(learned_taken, 1)
                        if prev and not mid:
                            for i_ in range(PAIRS):
                                pair = chip.x[:, 2 * i_:2 * i_ + 2, :]
                                dve.wait_ge(pair_made, i_ + 1)
                                dve.tensor_tensor(pair, pair_ps[i_ % len(pair_ps)][:].rearrange("p (t n) -> p t n", t=2), pair,
                                                  ALU.add).then_inc(pair_added, 1)
                                if 0 < i_ <= (NT - GT) // 2:
                                    dve.wait_ge(pair_added, i_)
                                    measure(chip, dve, 2 * i_ - 2)
                                    measure(chip, dve, 2 * i_ - 1)
                        if prev and p == HP - 1:
                            rows, _ = tiles(j - 2)
                            if not mid:
                                dve.wait_ge(pair_added, PAIRS)
                            dve.wait_ge(o_made, i * NG + (j - 1) // HP)
                            dve.tensor_tensor(chip.x[:, rows, :], o_ps[:], chip.x[:, rows, :], ALU.add).then_inc(added, 1)
                            if not mid:
                                dve.wait_ge(added, PASSES * NG)
                                for t in range(NT - GT, NT):
                                    measure(chip, dve, t)

                    dve.wait_ge(zero_done, 1)
                    passes(dve, slots)




def dense_mlp(chip, tag, scale, offset, w1, b1, w2, b2, function):
    nc = chip.nc
    FC = w1.shape[1] // P
    LEAD = 2
    with ExitStack() as stack:
        def sb(name, shape, dtype=F32):
            return chip.sb(f"{tag}_{name}", shape, dtype, stack)

        def sem(name):
            return chip.sem(f"{tag}_{name}")
        raw1, raw2 = sb("raw1", [P, CH, FC * P]), sb("raw2", [P, FC, D])
        w1_hi, w1_lo = sb("w1_hi", [P, CH, FC * P], F32R), sb("w1_lo", [P, CH, FC * P], F32R)
        w2_hi, w2_lo = sb("w2_hi", [P, FC, D], F32R), sb("w2_lo", [P, FC, D], F32R)
        b1_rows, b1_cols, b2_row = sb("b1_rows", [FC, P]), sb("b1_cols", [P, FC]), sb("b2_row", [P, D])
        b1_in, b2_in, w1_in, w2_in, b1_turned, b1_ready, w_hi_done, w_lo_done = (
            sem(s) for s in ("b1_in", "b2_in", "w1_in", "w2_in", "b1_turned", "b1_ready", "w_hi_done", "w_lo_done"))

        with ExitStack() as before:
            b1_ps = chip.ps(f"{tag}_b1_ps", [P, FC], before)

            def sync(sp):
                sp.dma_start(raw1[:], w1.rearrange("(c p) n -> p c n", p=P)).then_inc(w1_in, 16)
                sp.dma_start(b1_rows[:], b1.rearrange("(f p) -> f p", p=P)).then_inc(b1_in, 16)
                sp.dma_start(raw2[:], w2.rearrange("(f p) n -> p f n", p=P)).then_inc(w2_in, 16)
                sp.dma_start(b2_row[:], b2.rearrange("(a n) -> a n", a=1).to_broadcast([P, D])).then_inc(b2_in, 16)

            def gpsimd(pool):
                pool.wait_ge(w1_in, 16)
                pool.tensor_tensor(w1_hi[:].rearrange("p c n -> p (c n)"), raw1[:].rearrange("p c n -> p (c n)"),
                                   chip.one[:].to_broadcast([P, CH * FC * P]), ALU.mult).then_inc(w_hi_done, 1)

            def tensor(pe):
                pe.wait_ge(b1_in, 16)
                pe.transpose(b1_ps[:], b1_rows[:], chip.ident[0:FC, 0:FC]).then_inc(b1_turned, 1)

            def vector(dve):
                dve.wait_ge(w_hi_done, 1)
                dve.tensor_tensor(w1_lo[:], raw1[:], w1_hi[:].bitcast(F32), ALU.subtract).then_inc(w_lo_done, 1)
                dve.wait_ge(b1_turned, 1)
                dve.tensor_copy(b1_cols[:], b1_ps[:]).then_inc(b1_ready, 1)
            turn_input(chip, f"{tag}h", scale, offset, dict(sync=sync, gpsimd=gpsimd, tensor=tensor, vector=vector))

        hidden = [sb(f"hidden{b}", [P, GN]) for b in range(2)]
        hidden_hi = [sb(f"hidden_hi{b}", [P, GN], F32R) for b in range(2)]
        hidden_lo = [sb(f"hidden_lo{b}", [P, GN], F32R) for b in range(2)]
        idle = sb("idle", [P, 1])
        hidden_ps = [chip.ps(f"{tag}_hidden_ps{b}", [P, GN], stack) for b in range(2)]
        out_ps = chip.ps(f"{tag}_out_ps", [P, GT, 512], stack)
        b2_added, hidden_made, hidden_done, hi_done, lo_done, used, out_free = (
            sem(s) for s in ("b2_added", "hidden_made", "hidden_done", "hi_done", "lo_done", "used", "out_free"))

        with nc.Block() as block:
            @block.gpsimd
            def _(pool):
                pool.wait_ge(b2_in, 16)
                pool.tensor_tensor(chip.x[:], chip.x[:], b2_row[:].rearrange("p (a n) -> p a n", a=1)
                                   .to_broadcast([P, NT, D]), ALU.add).then_inc(b2_added, 1)

            @block.tensor
            def _(pe):
                def first(g, f):
                    tokens = slice(g * GN, (g + 1) * GN) if isinstance(g, int) else bass.ds(g * GN, GN)
                    if not (isinstance(g, int) and g == 0 and f < 2):
                        pe.wait_ge(hidden_done, g * FC + f - 1)
                    for c in range(CH):
                        last = product(pe, hidden_ps[f % 2][:], w1_hi[:, c, f * P:(f + 1) * P],
                                       w1_lo[:, c, f * P:(f + 1) * P], chip.h_hi[:, c, tokens],
                                       chip.h_lo[:, c, tokens], start=c == 0, stop=c == CH - 1)
                    last.then_inc(hidden_made, 1)

                def group(g, more):
                    for f in range(FC):
                        if f + LEAD < FC:
                            first(g, f + LEAD)
                        elif more:
                            first(g + 1, f + LEAD - FC)
                        if f == 0:
                            pe.wait_ge(w_lo_done, 2)
                            pe.wait_ge(out_free, g + 1)
                        pe.wait_ge(hi_done, g * FC + f + 1)
                        pe.wait_ge(lo_done, g * FC + f + 1)
                        for t in range(GT):
                            tok = slice(t * P, (t + 1) * P)
                            last = product(pe, out_ps[:, t, 0:D], hidden_hi[f % 2][:, tok], hidden_lo[f % 2][:, tok],
                                           w2_hi[:, f, :], w2_lo[:, f, :], start=f == 0, stop=f == FC - 1)
                        last.then_inc(used, 1)
                for f in range(LEAD):
                    first(0, f)
                with pe.Fori(0, NG - 1) as g:
                    group(g, True)
                group(NG - 1, False)

            @block.scalar
            def _(act):
                def chunk(g, f):
                    again = not (isinstance(g, int) and g == 0 and f < 2)
                    act.wait_ge(hidden_made, g * FC + f + 1)
                    if again:
                        act.wait_ge(lo_done, g * FC + f - 1)
                    act.activation(hidden[f % 2][:], hidden_ps[f % 2][:], function,
                                   bias=b1_cols[:, f:f + 1]).then_inc(hidden_done, 1)
                    act.wait_ge(hidden_done, g * FC + f + 1)
                    if again:
                        act.wait_ge(used, g * FC + f - 1)
                    act.activation(hidden_hi[f % 2][:], hidden[f % 2][:], ACT.Copy).then_inc(hi_done, 1)
                for f in range(FC):
                    chunk(0, f)
                    if f == 0:
                        act.wait_ge(w2_in, 16)
                        act.activation(w2_hi[:], raw2[:], ACT.Copy).then_inc(w_hi_done, 1)
                with act.Fori(1, NG) as g:
                    for f in range(FC):
                        chunk(g, f)

            @block.vector
            def _(dve):
                def low(g, f):
                    dve.wait_ge(hi_done, g * FC + f + 1)
                    dve.tensor_tensor(hidden_lo[f % 2][:], hidden[f % 2][:], hidden_hi[f % 2][:].bitcast(F32),
                                      ALU.subtract).then_inc(lo_done, 1)

                def lows(g, done=None):
                    for f in range(LEAD, FC):
                        low(g, f)
                        if done is not None and f - LEAD < GT:
                            measure(chip, dve, done * GT + f - LEAD)

                def lead(g):
                    for f in range(LEAD):
                        low(g, f)

                def output(g):
                    dve.wait_ge(used, g * FC + FC)
                    rows = chip.x[:, g * GT:(g + 1) * GT, :] if isinstance(g, int) else chip.x[:, bass.ds(g * GT, GT), :]
                    dve.tensor_tensor(rows, out_ps[:, :, 0:D], rows, ALU.add).then_inc(out_free, 1)
                    dve.wait_ge(out_free, g + 2)
                dve.memset(idle[:], 0.0).then_inc(out_free, 1)
                low(0, 0)
                dve.wait_ge(w_hi_done, 2)
                dve.tensor_tensor(w2_lo[:], raw2[:], w2_hi[:].bitcast(F32), ALU.subtract).then_inc(w_lo_done, 1)
                for f in range(1, LEAD):
                    low(0, f)
                dve.wait_ge(b2_added, 1)
                lows(0)
                lead(1)
                with dve.Fori(0, NG - 2) as g:
                    output(g)
                    lows(g + 1, g)
                    lead(g + 2)
                output(NG - 2)
                lows(NG - 1, NG - 2)
                output(NG - 1)
                for t in range(NT - GT, NT):
                    measure(chip, dve, t)


def narrow_attention(chip, tag, heads, kv_heads, norm, q_in, k_in, v_in, out_in, source, mask, multiply, score_scale):
    nc = chip.nc
    HD = D // heads
    GROUPS = heads // kv_heads
    HALF = 64
    QB = D // P
    QS = 2 * QB
    PER = HALF // HD
    VC = kv_heads * HD
    KB = max(1, VC // P)
    UT = 2
    UN = UT * P
    UNITS = NT // UT
    CHUNK = 16
    CT = heads // CHUNK
    SC = CT * UT
    CB = QB // CT
    HW = HD + 1
    Q_STEP, K_STEP, V_STEP = 0, 1, 2
    STEPS = V_STEP + UT
    BQ, BK, BV = 0, QB, QB + KB
    NV = BV + CH
    mask_tiles = 1 if multiply and mask.shape[0] == 1 else NT
    chip_h = (chip.h_hi, chip.h_lo)

    def sem(name):
        return chip.sem(f"{tag}_{name}")

    def chunked(w):
        return w.rearrange("(c p) n -> p c n", p=P)

    def by_set(t):
        return t.rearrange("p (k s f) -> p s k f", s=QS, f=HD)

    def ordered(t):
        return t.rearrange("p (s k f) -> p s k f", s=QS, f=HD)

    with ExitStack() as keep:
        def sb(name, shape, dtype=F32):
            return chip.sb(f"{tag}_{name}", shape, dtype, keep)

        def split(name, shape):
            return sb(name + "_hi", shape, F32R), sb(name + "_lo", shape, F32R)
        wq, wk, wv, wo = split("wq", [P, CH, D]), split("wk", [P, CH, KB * P]), split("wv", [P, CH, VC]), split("wo", [P, CH, D])
        bias_cols = sb("bias_cols", [P, NV])
        bo_row = sb("bo_row", [P, D])
        masks = sb("masks", [P, mask_tiles, SEQ])
        mask_bias = sb("mask_bias", [P, mask_tiles, SEQ]) if multiply else None
        head_mask = sb("head_mask", [P, PER])
        side_mask = sb("side_mask", [P, kv_heads, HD])
        q = [sb(f"q{b}", [P, QS, UT, P]) for b in range(2)]
        vb = [sb(f"vb{b}", [P, UT * HB, kv_heads, HW]) for b in range(2)]
        bo_in = sem("bo_in")

        with ExitStack() as stack:
            def sbp(name, shape):
                return chip.sb(f"{tag}_{name}", shape, F32, stack)
            raw_q, raw_k, raw_v, raw_o = sbp("raw_q", [P, CH, D]), sbp("raw_k", [P, CH, VC]), sbp("raw_v", [P, CH, VC]), sbp("raw_o", [P, CH, D])
            set_q = raw_q if GROUPS == 1 else sbp("set_q", [P, CH, D])
            set_k = raw_k if VC == KB * P else sbp("set_k", [P, CH, P])
            bias_in_rows, bias_rows = sbp("bias_in_rows", [1, D + 2 * VC]), sbp("bias_rows", [1, NV, P])
            head_pick = sbp("head_pick", [P, 2, PER])
            cols_ps = chip.ps(f"{tag}_cols_ps", [P, NV], stack)
            raw_in, mask_in, bias_in, masks_made, bias_spread, bias_turned, bias_ready, mask_ready, ordered_done, w_hi_done, w_lo_done = (
                sem(s) for s in ("raw_in", "mask_in", "bias_in", "masks_made", "bias_spread", "bias_turned", "bias_ready",
                                 "mask_ready", "ordered_done", "w_hi_done", "w_lo_done"))

            def sync(sp):
                for t, src in ((raw_q, q_in), (raw_k, k_in), (raw_v, v_in), (raw_o, out_in)):
                    sp.dma_start(t[:], chunked(src[0])).then_inc(raw_in, 16)
                for start, n, src in ((0, D, q_in), (D, VC, k_in), (D + VC, VC, v_in)):
                    sp.dma_start(bias_in_rows[0:1, start:start + n], src[1].rearrange("(a n) -> a n", a=1)).then_inc(bias_in, 16)
                if mask_tiles == 1:
                    for b in range(HB):
                        sp.dma_start(masks[b * SEQ:(b + 1) * SEQ, 0, :], mask[0, 0]).then_inc(mask_in, 16)
                else:
                    sp.dma_start(masks[:], mask.rearrange("b a q k -> (b a q) k")
                                 .rearrange("(t p) k -> p t k", p=P)).then_inc(mask_in, 16)
                sp.dma_start(bo_row[:], out_in[1].rearrange("(a n) -> a n", a=1).to_broadcast([P, D])).then_inc(bo_in, 16)
                sp.wait_ge(mask_in, 32 if mask_tiles == 1 else 16)
                sp.wait_ge(bo_in, 16)

            def gpsimd(pool):
                pool.memset(head_pick[:], 1.0)
                pool.memset(side_mask[:], 1.0).then_inc(masks_made, 1)
                pool.wait_ge(masks_made, 1)
                pool.affine_select(out=head_pick[:], in_=head_pick[:], compare_op=ALU.is_ge, fill=0.0, base=0,
                                   pattern=[[-HALF, 2], [-HD, PER]], channel_multiplier=1).then_inc(masks_made, 1)
                pool.wait_ge(masks_made, 2)
                pool.affine_select(out=head_pick[:], in_=head_pick[:], compare_op=ALU.is_ge, fill=0.0, base=HD - 1,
                                   pattern=[[HALF, 2], [HD, PER]], channel_multiplier=-1).then_inc(masks_made, 1)
                side = side_mask[:].rearrange("p (m j) d -> p m j d", j=2)
                pool.affine_select(out=side, in_=side, compare_op=ALU.is_ge, fill=0.0, base=0,
                                   pattern=[[0, kv_heads // 2], [-SEQ, 2], [0, HD]], channel_multiplier=1).then_inc(masks_made, 1)
                pool.wait_ge(masks_made, 4)
                pool.affine_select(out=side, in_=side, compare_op=ALU.is_ge, fill=0.0, base=SEQ - 1,
                                   pattern=[[0, kv_heads // 2], [SEQ, 2], [0, HD]], channel_multiplier=-1).then_inc(masks_made, 1)
                pool.wait_ge(masks_made, 5)
                pool.tensor_tensor(head_mask[:], head_pick[:, 0, :], head_pick[:, 1, :], ALU.add)
                for b in range(2):
                    pool.memset(q[b][:], 0.0)
                    pool.tensor_copy(vb[b][:, :, :, HD], side_mask[:, :, 0].rearrange("p (a h) -> p a h", a=1)
                                     .to_broadcast([P, UT * HB, kv_heads]))

            def tensor(pe):
                pe.wait_ge(bias_spread, 1)
                for i in range(NV):
                    last = pe.matmul(cols_ps[:, i:i + 1], bias_rows[0:1, i, :], chip.one[0:1, 0:1], start=True, stop=True)
                last.then_inc(bias_turned, 1)

            def scalar(act):
                act.wait_ge(raw_in, 64)
                for i, (w_, src) in enumerate(((wv, raw_v), (wo, raw_o), (wq, set_q), (wk, set_k))):
                    if i == 2 and GROUPS > 1:
                        act.wait_ge(ordered_done, 1)
                    act.activation(w_[0][:], src[:], ACT.Copy).then_inc(w_hi_done, 1)

            def vector(dve):
                dve.wait_ge(raw_in, 64)
                dve.wait_ge(bias_in, 48)
                if GROUPS == 1:
                    dve.tensor_copy(bias_rows[:, BQ:BV, :].rearrange("p c f -> p (c f)"), bias_in_rows[:, 0:D + VC])
                else:
                    for c in range(CH):
                        dve.tensor_copy(ordered(set_q[:, c, :]), by_set(raw_q[:, c, :]))
                    dve.tensor_copy(ordered(bias_rows[:, BQ:BK, :].rearrange("p c f -> p (c f)")), by_set(bias_in_rows[:, 0:D]))
                    for side in range(2):
                        half = slice(side * HALF, (side + 1) * HALF)
                        dve.tensor_copy(bias_rows[:, BK, half], bias_in_rows[:, D:D + VC])
                        last = dve.tensor_copy(set_k[:, :, half], raw_k[:])
                    last.then_inc(ordered_done, 1)
                value_bias = bias_in_rows[:, D + VC:D + 2 * VC]
                if GROUPS == 1:
                    last = dve.tensor_copy(bias_rows[:, BV:NV, :].rearrange("p c f -> p (c f)"), value_bias)
                else:
                    last = dve.tensor_copy(bias_rows[:, BV:NV, :].rearrange("p c (k g f) -> p (c k) g f", g=GROUPS, f=HD),
                                           value_bias.rearrange("p (k a f) -> p k a f", a=1, f=HD)
                                           .to_broadcast([1, kv_heads, GROUPS, HD]))
                last.then_inc(bias_spread, 1)
                if multiply:
                    dve.wait_ge(mask_in, 32 if mask_tiles == 1 else 16)
                    dve.tensor_scalar(mask_bias[:], masks[:], -1.0, 10000.0, ALU.add, ALU.mult).then_inc(mask_ready, 1)
                    dve.wait_ge(mask_ready, 1)
                    dve.tensor_scalar(masks[:], masks[:], score_scale, None, ALU.mult)
                if GROUPS > 1:
                    dve.wait_ge(ordered_done, 1)
                for i, (w_, src) in enumerate(((wv, raw_v), (wo, raw_o), (wq, set_q), (wk, set_k))):
                    dve.wait_ge(w_hi_done, i + 1)
                    dve.tensor_tensor(w_[1][:], src[:], w_[0][:].bitcast(F32), ALU.subtract).then_inc(w_lo_done, 1)
                dve.wait_ge(bias_turned, 1)
                dve.tensor_copy(bias_cols[:], cols_ps[:]).then_inc(bias_ready, 1)

            turn_input(chip, f"{tag}h", *norm, beside=dict(sync=sync, gpsimd=gpsimd, tensor=tensor, scalar=scalar, vector=vector))

        stack = keep
        kc = sb("kc", [P, 2, KB * UT, SEQ])
        kb = [sb(f"kb{b}", [P, 2, KB * UT, PER, SEQ]) for b in range(2)]
        score = [sb(f"score{b}", [P, CHUNK, SEQ]) for b in range(2)]
        top = [sb(f"top{b}", [P, CHUNK]) for b in range(2)]
        weight_t = [sb(f"weight_t{b}", [P, CHUNK // 2, P]) for b in range(2)]
        inverse = sb("inverse", [P, heads])
        rows = sb("rows", [P, D])
        o_t = split("o_t", [P, CH, P])
        proj_ps = [chip.ps(f"{tag}_proj_ps{b}", [P, 512], stack) for b in range(2)]
        score_ps = [chip.ps(f"{tag}_score_ps{b}", [P, CHUNK, SEQ], stack) for b in range(2)]
        attn_ps = chip.ps(f"{tag}_attn_ps", [P, 512], stack)
        out_ps = chip.ps(f"{tag}_out_ps", [P, 2, D], stack)
        bo_added = sem("bo_added")
        proj_made, q_taken, k_taken, v_taken, kb_made, scores_made, masked, biased, top_done, shifted, exp_done = (
            sem(s) for s in ("proj_made", "q_taken", "k_taken", "v_taken", "kb_made", "scores_made", "masked", "biased", "top_done", "shifted", "exp_done"))
        turned, turned_taken, attn_made, inverse_done, rows_done, rows_turned, o_hi_done, o_lo_done, out_made, out_added = (
            sem(s) for s in ("turned", "turned_taken", "attn_made", "inverse_done", "rows_done", "rows_turned", "o_hi_done", "o_lo_done", "out_made", "out_added"))

        stage = [split(f"stage{b}", [P, CH, UT * HB * P]) for b in range(2)]
        staged_hi, staged_lo = sem("staged_hi"), sem("staged_lo")

        FILL = ([([Q_STEP], [K_STEP]), ([V_STEP], [V_STEP + 1])] if SC == 2 else
                [([Q_STEP], []), ([K_STEP], []), ([V_STEP], []), ([V_STEP + 1], [])])
        LAG = 1 if SC == 2 else 2
        SPREAD = (SC // 2, SC - 1)

        def units(engine, slot):
            slot(0, 0, True, False, False)
            slot(1, 1, True, True, False)
            with engine.Fori(0, UNITS // 2 - 1) as i:
                for j in (2, 3):
                    slot(i * 2 + j, j, True, True, True)
            slot(UNITS, UNITS, False, True, True)
            slot(UNITS + 1, UNITS + 1, False, False, True)

        def steps(n, mid, prev):
            for s in range(SC):
                def exists(k):
                    return mid if s >= k else prev
                end = s - LAG - 1
                ended = n * UT - UT + end // CT if exists(LAG + 1) and end % CT == CT - 1 else None
                yield s, n * SC - SC + s, exists(1), exists(LAG), ended

        def token_range(n):
            return bass.ds(n * UN, UN) if not isinstance(n, int) else slice(n * UN, (n + 1) * UN)

        with nc.Block() as block:
            @block.gpsimd
            def _(pool):
                pool.tensor_tensor(chip.x[:], chip.x[:], bo_row[:].rearrange("p (a n) -> p a n", a=1)
                                   .to_broadcast([P, NT, D]), ALU.add).then_inc(bo_added, 1)

                def spread_keys(n, u, r):
                    pool.wait_ge(k_taken, n + 1)
                    pool.tensor_tensor(kb[u][:, r, :, :, :],
                                       kc[:, r, :, :].rearrange("p t (a k) -> p t a k", a=1).to_broadcast([P, KB * UT, PER, SEQ]),
                                       head_mask[:].rearrange("p (a h b) -> p a h b", a=1, b=1).to_broadcast([P, KB * UT, PER, SEQ]),
                                       ALU.mult).then_inc(kb_made, 1)

                def slot(n, j, this, mid, prev):
                    u = j % 2
                    for s, m, last, lagged, ended in steps(n, mid, prev):
                        if this and s == SPREAD[0]:
                            spread_keys(n, u, 0)
                        if mid:
                            score_ = score[s % 2]
                            if multiply:
                                mb = mask_bias[:, 0:1, :] if mask_tiles == 1 else mask_bias[:, bass.ds((n - 1) * UT + s // CT, 1), :]
                                pool.wait_ge(masked, m + 1)
                                pool.tensor_tensor(score_[:], score_[:], mb.to_broadcast([P, CHUNK, SEQ]),
                                                   ALU.add).then_inc(biased, 1)
                        if this and s == SPREAD[1]:
                            spread_keys(n, u, 1)
                        if mid:
                            pool.wait_ge(top_done, m + 1)
                            pool.tensor_tensor(score_[:], score_[:], top[s % 2][:].rearrange("p (h a) -> p h a", a=1)
                                               .to_broadcast([P, CHUNK, SEQ]), ALU.subtract).then_inc(shifted, 1)
                units(pool, slot)

            @block.tensor
            def _(pe):
                def project(n, u, s):
                    tokens = token_range(n)
                    out = proj_ps[s % 2]
                    if s == 0 and (not isinstance(n, int) or n > 0):
                        pe.wait_ge(v_taken, n * UT)
                    if s == V_STEP:
                        pe.wait_ge(staged_hi, n + 1)
                        pe.wait_ge(staged_lo, n + 1)
                    if s >= V_STEP:
                        pe.wait_ge(q_taken if s == V_STEP else k_taken, n + 1)
                    if s < V_STEP:
                        src, w_ = (chip_h, wq) if s == Q_STEP else (source, wk)
                        for x in range(QB if s == Q_STEP else KB):
                            feats = slice(x * P, (x + 1) * P)
                            for c in range(CH):
                                last = product(pe, out[:, x * UN:(x + 1) * UN], w_[0][:, c, feats], w_[1][:, c, feats],
                                               src[0][:, c, tokens], src[1][:, c, tokens], start=c == 0, stop=c == CH - 1)
                    else:
                        t = s - V_STEP
                        for b in range(HB):
                            for c in range(CH):
                                both = [stage[u][x][:, c, (t * HB + b) * P:(t * HB + b + 1) * P] for x in range(2)]
                                last = product(pe, out[:, b * VC:(b + 1) * VC], both[0], both[1], wv[0][:, c, :], wv[1][:, c, :],
                                               start=c == 0, stop=c == CH - 1)
                    last.then_inc(proj_made, 1)

                def scores(n, v, s, m):
                    t, part = s // CT, s % CT
                    if s == 0:
                        pe.wait_ge(kb_made, n * 2)
                        pe.wait_ge(q_taken, n)
                    if not isinstance(m, int) or m >= 2:
                        pe.wait_ge(turned_taken, m - 1)
                    flat = score_ps[s % 2][:].rearrange("p h k -> p (h k)")
                    for x in range(2 * CB):
                        block, r = part * CB + x // 2, x % 2
                        last = pe.matmul(flat[:, x * PER * SEQ:(x + 1) * PER * SEQ], q[v][:, block * 2 + r, t, :],
                                         kb[v][:, r, block % KB * UT + t, :, :].rearrange("p h k -> p (h k)"),
                                         start=True, stop=True)
                    last.then_inc(scores_made, 1)

                def turn(m, b):
                    pe.wait_ge(exp_done, m + 1)
                    flat = score[b][:].rearrange("p h k -> p (h k)")
                    out = score_ps[b][:].rearrange("p h k -> p (h k)")
                    for x in range(CHUNK // 2):
                        last = pe.transpose(out[:, x * P:(x + 1) * P], flat[:, x * P:(x + 1) * P], chip.ident[:])
                    last.then_inc(turned, 1)

                def attend(n, m, s, values):
                    tile, t, part = n * UT - UT + s // CT, s // CT % UT, s % CT
                    pe.wait_ge(turned_taken, m + 1)
                    if s == 0:
                        pe.wait_ge(v_taken, n * UT)
                    if part == 0 and (not isinstance(tile, int) or tile > 0):
                        pe.wait_ge(rows_done, tile)
                    for x in range(CHUNK // 2):
                        product_, pair = x // (PER // 2), x % (PER // 2)
                        block, r = part * CB + product_ // 2, product_ % 2
                        for b in range(HB):
                            set_ = block * 2 + (b ^ r)
                            head = set_ * PER + 2 * pair
                            value, col = (head if GROUPS == 1 else 2 * pair), head * HW
                            last = pe.matmul(attn_ps[b * SEQ:(b + 1) * SEQ, col:col + 2 * HW],
                                             weight_t[s % 2][:, x, b * SEQ:(b + 1) * SEQ],
                                             values[:, t * HB + b, value:value + 2, :].rearrange("p h w -> p (h w)"),
                                             start=True, stop=True)
                    last.then_inc(attn_made, 1)

                def turn_rows(tile):
                    pe.wait_ge(rows_done, tile + 1)
                    if not isinstance(tile, int) or tile > 0:
                        pe.wait_ge(out_added, tile)
                    for c in range(CH):
                        last = pe.transpose(out_ps[:, 0, c * P:(c + 1) * P], rows[:, c * P:(c + 1) * P], chip.ident[:])
                    last.then_inc(rows_turned, 1)

                def output(tile):
                    pe.wait_ge(o_hi_done, tile + 1)
                    pe.wait_ge(o_lo_done, tile + 1)
                    for c in range(CH):
                        last = product(pe, out_ps[:, 1, :], o_t[0][:, c, :], o_t[1][:, c, :], wo[0][:, c, :], wo[1][:, c, :],
                                       start=c == 0, stop=c == CH - 1)
                    last.then_inc(out_made, 1)

                def slot(n, j, this, mid, prev):
                    u, v = j % 2, (j - 1) % 2
                    for s, m, last, lagged, ended in steps(n, mid, prev):
                        if mid:
                            scores(n, v, s, m)
                        if ended is not None:
                            turn_rows(ended)
                        if this:
                            for x in FILL[s][0]:
                                project(n, u, x)
                        if last:
                            turn(m - 1, (s - 1) % 2)
                        if lagged and LAG > 1:
                            attend(n, m - LAG, s - LAG, vb[v] if s >= LAG else vb[u])
                        if ended is not None:
                            output(ended)
                        if this:
                            for x in FILL[s][1]:
                                project(n, u, x)
                        if lagged and LAG == 1:
                            attend(n, m - LAG, s - LAG, vb[v] if s >= LAG else vb[u])
                units(pe, slot)

            @block.scalar
            def _(act):
                def slot(n, j, this, mid, prev):
                    u = j % 2

                    def take(s):
                        if s >= V_STEP:
                            return
                        act.wait_ge(proj_made, n * STEPS + s + 1)
                        if s == K_STEP and mid:
                            act.wait_ge(kb_made, n * 2)
                        for x in range(QB if s == Q_STEP else KB):
                            part = proj_ps[s % 2][:, x * UN:(x + 1) * UN].rearrange("p (t b k) -> p t b k", b=HB, k=SEQ)
                            for r in range(2):
                                for b in range(HB):
                                    half, seq = slice(b * HALF, (b + 1) * HALF), b ^ r
                                    if s == Q_STEP:
                                        out, i = q[u][half, x * 2 + r, :, seq * SEQ:(seq + 1) * SEQ], BQ + x
                                    else:
                                        out, i = kc[half, r, x * UT:(x + 1) * UT, :], BK + x
                                    last = act.activation(out, part[half, :, seq, :], ACT.Identity, bias=bias_cols[half, i:i + 1])
                        last.then_inc(q_taken if s == Q_STEP else k_taken, 1)

                    for s, m, last, lagged, ended in steps(n, mid, prev):
                        if last:
                            act.wait_ge(shifted, m)
                            act.activation(score[(s - 1) % 2][:], score[(s - 1) % 2][:], ACT.Exp).then_inc(exp_done, 1)
                        if ended is not None:
                            act.wait_ge(rows_turned, ended + 1)
                            for c in range(CH):
                                hi = act.activation(o_t[0][:, c, :], out_ps[:, 0, c * P:(c + 1) * P], ACT.Identity,
                                                    bias=bias_cols[:, BV + c:BV + c + 1])
                            hi.then_inc(o_hi_done, 1)
                        if this:
                            for x in FILL[s][0]:
                                take(x)
                        if last:
                            act.wait_ge(turned, m)
                            act.activation(weight_t[(s - 1) % 2][:].rearrange("p x q -> p (x q)"),
                                           score_ps[(s - 1) % 2][:].rearrange("p h k -> p (h k)"), ACT.Copy).then_inc(turned_taken, 1)
                        if this:
                            for x in FILL[s][1]:
                                take(x)
                            if s == 0:
                                for c in range(CH):
                                    hi = act.activation(
                                        stage[u][0][:, c, :].rearrange("p (b r k) -> p b r k", r=2, k=SEQ),
                                        source[0][:, c, token_range(n)].bitcast(F32).rearrange("p (b a k) -> p b a k", a=1, k=SEQ)
                                        .to_broadcast([P, UT * HB, 2, SEQ]), ACT.Copy)
                                hi.then_inc(staged_hi, 1)
                units(act, slot)

            @block.vector
            def _(dve):
                def slot(n, j, this, mid, prev):
                    u = j % 2

                    def mask_scores(s, m):
                        mk = masks[:, 0:1, :] if mask_tiles == 1 else masks[:, bass.ds((n - 1) * UT + s // CT, 1), :]
                        mk = mk.to_broadcast([P, CHUNK, SEQ])
                        dve.wait_ge(scores_made, m + 1)
                        if multiply:
                            dve.tensor_tensor(score[s % 2][:], score_ps[s % 2][:], mk, ALU.mult).then_inc(masked, 1)
                        else:
                            dve.scalar_tensor_tensor(score[s % 2][:], score_ps[s % 2][:], score_scale, mk,
                                                     ALU.mult, ALU.add).then_inc(masked, 1)

                    def take_values(x):
                        if x < V_STEP:
                            return
                        t = x - V_STEP
                        dve.wait_ge(proj_made, n * STEPS + x + 1)
                        dve.tensor_tensor(vb[u][:, t * HB:(t + 1) * HB, :, 0:HD],
                                          proj_ps[x % 2][:, 0:HB * VC].rearrange("p (b h f) -> p b h f", b=HB, f=HD),
                                          side_mask[:].rearrange("p (a h) f -> p a h f", a=1).to_broadcast([P, HB, kv_heads, HD]),
                                          ALU.mult).then_inc(v_taken, 1)

                    def normalise(tile):
                        dve.wait_ge(attn_made, tile * CT + CT)
                        done = attn_ps[:, 0:heads * HW].rearrange("p (h w) -> p h w", w=HW)
                        dve.reciprocal(inverse[:], done[:, :, HD]).then_inc(inverse_done, 1)
                        dve.wait_ge(inverse_done, tile + 1)
                        if GROUPS == 1:
                            dve.tensor_tensor(rows[:].rearrange("p (h f) -> p h f", f=HD), done[:, :, 0:HD],
                                              inverse[:].rearrange("p (h a) -> p h a", a=1).to_broadcast([P, heads, HD]),
                                              ALU.mult).then_inc(rows_done, 1)
                        else:
                            dve.tensor_tensor(rows[:].rearrange("p (k g f) -> p g k f", g=GROUPS, f=HD),
                                              done[:, :, 0:HD].rearrange("p (g k) f -> p g k f", g=GROUPS),
                                              inverse[:].rearrange("p (g k a) -> p g k a", g=GROUPS, a=1)
                                              .to_broadcast([P, GROUPS, kv_heads, HD]), ALU.mult).then_inc(rows_done, 1)

                    for s, m, last, lagged, ended in steps(n, mid, prev):
                        if ended is not None:
                            normalise(ended)
                        if mid:
                            mask_scores(s, m)
                        if ended is not None:
                            dve.wait_ge(o_hi_done, ended + 1)
                            for c in range(CH):
                                lo = dve.scalar_tensor_tensor(o_t[1][:, c, :], out_ps[:, 0, c * P:(c + 1) * P],
                                                              bias_cols[:, BV + c:BV + c + 1],
                                                              o_t[0][:, c, :].bitcast(F32), ALU.add, ALU.subtract)
                            lo.then_inc(o_lo_done, 1)
                        if this and s == 0:
                            for c in range(CH):
                                lo = dve.tensor_copy(
                                    stage[u][1][:, c, :].rearrange("p (b r k) -> p b r k", r=2, k=SEQ),
                                    source[1][:, c, token_range(n)].bitcast(F32).rearrange("p (b a k) -> p b a k", a=1, k=SEQ)
                                    .to_broadcast([P, UT * HB, 2, SEQ]))
                            lo.then_inc(staged_lo, 1)
                        if mid:
                            dve.wait_ge(biased if multiply else masked, m + 1)
                            dve.tensor_reduce(top[s % 2][:], score[s % 2][:], AX, ALU.max).then_inc(top_done, 1)
                        if this:
                            for x in FILL[s][0]:
                                take_values(x)
                        if ended is not None:
                            if isinstance(ended, int) and ended == 0:
                                dve.wait_ge(bo_added, 1)
                            dve.wait_ge(out_made, ended + 1)
                            tile = (chip.x[:, ended, :] if isinstance(ended, int) else
                                    chip.x[:, bass.ds(ended, 1), :].rearrange("p a d -> p (a d)"))
                            dve.tensor_tensor(tile, out_ps[:, 1, :], tile, ALU.add).then_inc(out_added, 1)
                        if this:
                            for x in FILL[s][1]:
                                take_values(x)
                        if ended is not None:
                            dve.wait_ge(out_added, ended + 1)
                            measure(chip, dve, ended)
                units(dve, slot)


def normalise_rows(chip, tag, gamma, beta, beside):
    nc = chip.nc
    with ExitStack() as stack:
        def sb(name, shape):
            return chip.sb(f"{tag}_{name}", shape, F32, stack)
        spread, inverse, away = sb("spread", [P, NT]), sb("inverse", [P, NT]), sb("away", [P, NT])
        gain, shift = sb("gain", [P, D]), sb("shift", [P, D])
        rows = sb("rows", [P, NT, D])
        idle_ps = chip.ps(f"{tag}_idle_ps", [P, P], stack)
        gain_in, shift_in, gathered, spread_done, inverse_done, away_done, rows_done, scaled, done = (
            chip.sem(f"{tag}_{s}") for s in ("gain_in", "shift_in", "gathered", "spread_done", "inverse_done", "away_done",
                                             "rows_done", "scaled", "done"))

        measured, regathered = chip.sem(f"{tag}_measured"), chip.sem(f"{tag}_regathered")

        def same_for_all(vector):
            return vector[:].rearrange("p (a n) -> p a n", a=1).to_broadcast([P, GT, D])
        with nc.Block() as block:
            @block.sync
            def _(sp):
                sp.dma_start(gain[:], gamma.rearrange("(a n) -> a n", a=1).to_broadcast([P, D])).then_inc(gain_in, 16)
                sp.dma_start(shift[:], beta.rearrange("(a n) -> a n", a=1).to_broadcast([P, D])).then_inc(shift_in, 16)
                beside["sync"](sp)

            @block.gpsimd
            def _(pool):
                beside["gpsimd"](pool)
                invert_spread(chip, pool, 1e-6, spread, inverse, gathered, spread_done, inverse_done)
                pool.wait_ge(gain_in, 16)
                for g in range(NG):
                    pool.wait_ge(rows_done, g * GT + GT)
                    part = rows[:, g * GT:(g + 1) * GT, :]
                    pool.tensor_tensor(part, part, same_for_all(gain), ALU.mult).then_inc(scaled, 1)

            @block.tensor
            def _(pe):
                pe.wait_ge(done, NG - 1)
                keep_warm(chip, pe, idle_ps, 24)

            @block.scalar
            def _(act):
                for g in range(NG):
                    act.wait_ge(away_done, g + 1)
                    for j in range(GT):
                        t = g * GT + j
                        act.activation(rows[:, t, :], chip.x[:, t, :], ACT.Identity, bias=away[:, t:t + 1],
                                       scale=inverse[:, t:t + 1]).then_inc(rows_done, 1)

            @block.vector
            def _(dve):
                gather_moments(chip, dve, gathered)
                for g in range(NG):
                    part = slice(g * GT, (g + 1) * GT)
                    dve.wait_ge(inverse_done, g + 1)
                    dve.scalar_tensor_tensor(away[:, part], chip.x_moments[:, part, 0], -1.0, inverse[:, part],
                                             ALU.mult, ALU.mult).then_inc(away_done, 1)
                dve.wait_ge(away_done, NG)
                dve.wait_ge(shift_in, 16)
                for g in range(NG):
                    dve.wait_ge(scaled, g + 1)
                    dve.tensor_tensor(chip.x[:, g * GT:(g + 1) * GT, :], rows[:, g * GT:(g + 1) * GT, :], same_for_all(shift),
                                      ALU.add).then_inc(done, 1)
                    dve.wait_ge(done, g + 1)
                    for t in range(g * GT, (g + 1) * GT):
                        last = measure(chip, dve, t)
                    last.then_inc(measured, 1)
                dve.wait_ge(measured, NG)
                gather_moments(chip, dve, regathered)


def layer0(chip):
    for n in (1, 2):
        wide_attention(chip, f"l0a{n}", n)
        chip.end_stage()
    layer0_mlp(chip)


def layer0_mlp(chip):
    I = chip.inputs
    dense_mlp(chip, "l0m", I["L0_xattn_ln_mlp_scale"], I["L0_xattn_ln_mlp_offset"],
              I["L0_xattn_w_fc1"], I["L0_xattn_b_fc1"], I["L0_xattn_w_fc2"], I["L0_xattn_b_fc2"], ACT.Gelu)
    chip.end_stage()


def layer1(chip):
    I = {k[9:]: v for k, v in chip.inputs.items() if k.startswith("L1_xattn_")}
    narrow_attention(chip, "l1a", 32, 8, (None, None), (I["Wq"], I["bq"]), (I["Wk"], I["bk"]), (I["Wv"], I["bv"]), (I["Wo"], I["bo"]),
                     (chip.ctx_hi, chip.ctx_lo), chip.inputs["mask_Bx1xSxS2_ff0"], False,
                     1.0 / float(np.sqrt(np.float32(8))))
    chip.end_stage()


def layer3(chip):
    I = {k[9:]: v for k, v in chip.inputs.items() if k.startswith("L3_xattn_")}
    scale = 1.0 / float(np.sqrt(np.float32(16)))
    w, b = I["w_qkv"], I["b_qkv"]
    parts = [(w[:, i * D:(i + 1) * D], b[i * D:(i + 1) * D]) for i in range(3)]
    narrow_attention(chip, "l3a1", 16, 16, (I["ln1_s"], I["ln1_b"]), *parts, (I["w_ao"], I["b_ao"]), (chip.h_hi, chip.h_lo),
                     chip.inputs["mask_1x1xSxS2_fc1"], True, scale)
    chip.end_stage()
    w, b = I["w_kv"], I["b_kv"]
    parts = [(w[:, i * D:(i + 1) * D], b[i * D:(i + 1) * D]) for i in range(2)]
    narrow_attention(chip, "l3a2", 16, 16, (I["ln2_s"], I["ln2_b"]), (I["w_q"], I["b_q"]), *parts, (I["w_co"], I["b_co"]), (chip.ctx_hi, chip.ctx_lo),
                     chip.inputs["mask_Bx1xSxS2_ff1"], True, scale)
    chip.end_stage()
    dense_mlp(chip, "l3m", I["ln3_s"], I["ln3_b"], I["w1"], I["b1"], I["w2"], I["b2"], ACT.Gelu_apprx_tanh)


def layer2(chip):
    nc = chip.nc
    I = {k[9:]: v for k, v in chip.inputs.items() if k.startswith("L2_xattn_")}
    NB = HB * CH
    tag = "l2"
    with ExitStack() as stack:
        def sb(name, shape):
            return chip.sb(f"{tag}_{name}", shape, F32, stack)

        def sem(name):
            return chip.sem(f"{tag}_{name}")
        context = sb("context", [P, NT, D])
        w_rows, w_cols = sb("w_rows", [P, 4, P]), sb("w_cols", [P, 4, P])
        bias = sb("bias", [P, 4])
        spread, inverse = sb("spread", [P, NT]), sb("inverse", [P, NT])
        w_zeroed, w_in, b_in, ctx_in, w_turned, w_ready, spread_done, inverse_done, held_done = (
            sem(s) for s in ("w_zeroed", "w_in", "b_in", "ctx_in", "w_turned", "w_ready", "spread_done",
                             "inverse_done", "held_done"))

        def sync(sp):
            sp.dma_start(context[:], chip.inputs["ctx_2048"].rearrange("b s d -> (b s) d")
                         .rearrange("(t p) d -> p t d", p=P)).then_inc(ctx_in, 16)
            sp.wait_ge(w_zeroed, 1)
            for i, k in enumerate(("Wn", "Wm", "Wl", "Wo")):
                for b in range(HB):
                    half = slice(b * SEQ, (b + 1) * SEQ)
                    sp.dma_start(w_rows[half, i, half], I[k]).then_inc(w_in, 16)
                    sp.dma_start(bias[half, i:i + 1], I["b" + k[1]].rearrange("(p a) -> p a", a=1)).then_inc(b_in, 16)

        def gpsimd(pool):
            pool.memset(w_rows[:], 0.0).then_inc(w_zeroed, 1)
        normalise_rows(chip, "l1n", chip.inputs["L1_xattn_gamma"], chip.inputs["L1_xattn_beta"],
                       dict(sync=sync, gpsimd=gpsimd))

        normed = [sb(f"normed{b}", [P, 2, D]) for b in range(2)]
        held = [sb(f"held{b}", [P, D]) for b in range(2)]
        maps = [sb(f"maps{b}", [P, 2, D]) for b in range(2)]
        value_t = [sb(f"value_t{b}", [P, CH, P]) for b in range(2)]
        top, total, inv = sb("top", [P, NB]), sb("total", [P, NB]), sb("inv", [P, NB])
        expd, weight = sb("expd", [P, NB, D]), sb("weight", [P, NB, D])
        weight_t = sb("weight_t", [P, HB, CH, D])
        attended = sb("attended", [P, D])
        conv_ps = chip.ps(f"{tag}_conv_ps", [P, 2, D], stack)
        value_ps = chip.ps(f"{tag}_value_ps", [P, 512], stack)
        score_ps = chip.ps(f"{tag}_score_ps", [P, HB, CH, D], stack)
        turned_ps = chip.ps(f"{tag}_turned_ps", [P, HB, CH, D], stack)
        mo_ps, out_ps = chip.ps(f"{tag}_mo_ps", [P, 512], stack), chip.ps(f"{tag}_out_ps", [P, 512], stack)
        normed_done, conv_made, value_made, maps_done, value_done, score_made, top_done, exp_done, inv_done, weight_a, weight_b = (
            sem(s) for s in ("normed_done", "conv_made", "value_made", "maps_done", "value_done", "score_made",
                             "top_done", "exp_done", "inv_done", "weight_a", "weight_b"))
        turned_taken = [sem(f"turned_taken{b}") for b in range(HB)]
        turned, mo_made, mo_done, out_made, out_done = (
            sem(s) for s in ("turned", "mo_made", "mo_done", "out_made", "out_done"))

        def tiles(engine, slot):
            for n in range(4):
                slot(n, n, True, n >= 1, n >= 2, n >= 3)
            with engine.Fori(2, NT // 2) as i:
                for j in range(2):
                    slot(i * 2 + j, j, True, True, True, True)
            for n in range(NT, NT + 3):
                slot(n, n, False, n == NT, n <= NT + 1, True)

        with nc.Block() as block:
            @block.tensor
            def _(pe):
                def slot(n, j, conv, soft, attend, out):
                    u, v = j % 2, (j - 1) % 2
                    if soft:
                        pe.wait_ge(maps_done, n)
                        if attend:
                            pe.wait_ge(exp_done, n - 1)
                        for b in range(HB):
                            half = slice(b * SEQ, (b + 1) * SEQ)
                            for t in range(CH):
                                last = pe.matmul(score_ps[:, b, t, :], maps[v][half, 0, t * P:(t + 1) * P], maps[v][half, 1, :],
                                                 start=True, stop=True)
                        last.then_inc(score_made, 1)
                    if out:
                        pe.wait_ge(mo_done, n - 2)
                        if not isinstance(n, int) or n >= 4:
                            pe.wait_ge(out_done, n - 3)
                        pe.matmul(out_ps[:, 0:D], w_cols[:, 3, :], attended[:], start=True, stop=True).then_inc(out_made, 1)
                    if attend:
                        pe.wait_ge(weight_a, n - 1)
                        pe.wait_ge(weight_b, n - 1)
                        for b in range(HB):
                            for t in range(CH):
                                for c in range(CH):
                                    last = pe.transpose(turned_ps[:, b, c, t * P:(t + 1) * P],
                                                        weight[:, b * CH + t, c * P:(c + 1) * P], chip.ident[:])
                        last.then_inc(turned, 1)
                    if conv:
                        pe.wait_ge(normed_done, n + 1)
                        for i in range(2):
                            last = pe.matmul(conv_ps[:, i, :], w_cols[:, i, :], normed[u][:, i, :], start=True, stop=True)
                        last.then_inc(conv_made, 1)
                    if attend:
                        pe.wait_ge(value_done, n - 1)
                        for b in range(HB):
                            pe.wait_ge(turned_taken[b], n - 1)
                            half = slice(b * SEQ, (b + 1) * SEQ)
                            for c in range(CH):
                                last = pe.matmul(mo_ps[half, 0:D], value_t[u][:, c, half], weight_t[:, b, c, :],
                                                 start=c == 0, stop=c == CH - 1)
                        last.then_inc(mo_made, 1)
                    if conv:
                        if soft:
                            pe.wait_ge(value_done, n)
                        for c in range(CH):
                            if c == 0:
                                pe.wait_ge(held_done, n + 1)
                            last = pe.matmul(value_ps[:, c * P:(c + 1) * P], held[u][:, c * P:(c + 1) * P], w_cols[:, 2, :],
                                             start=True, stop=True)
                        last.then_inc(value_made, 1)
                pe.wait_ge(w_in, 16 * 4 * HB)
                for i in range(4):
                    last = pe.transpose(value_ps[:, i * P:(i + 1) * P], w_rows[:, i, :], chip.ident[:])
                last.then_inc(w_turned, 1)
                pe.wait_ge(w_ready, 1)
                tiles(pe, slot)

            @block.gpsimd
            def _(pool):
                pool.tensor_scalar(spread[:], chip.x_moments[:, :, 1], 1e-5, None, ALU.add).then_inc(spread_done, 1)
                pool.wait_ge(spread_done, 1)
                for g in range(NG):
                    part = slice(g * GT, (g + 1) * GT)
                    pool.tensor_tensor(inverse[:, part], spread[:, part], chip.minus_half[:].to_broadcast([P, GT]),
                                       ALU.pow).then_inc(inverse_done, 1)

                def slot(n, j, conv, soft, attend, out):
                    if conv:
                        if attend:
                            pool.wait_ge(value_made, n - 1)
                        pool.tensor_copy(held[j % 2][:], tile_of(context, n)).then_inc(held_done, 1)
                pool.wait_ge(ctx_in, 16)
                tiles(pool, slot)

            @block.scalar
            def _(act):
                def slot(n, j, conv, soft, attend, out):
                    u, v = j % 2, (j - 1) % 2
                    if attend:
                        act.wait_ge(turned, n - 1)
                        act.activation(weight_t[:, 0, :, :].rearrange("p c t -> p (c t)"),
                                       turned_ps[:, 0, :, :].rearrange("p c t -> p (c t)"), ACT.Copy).then_inc(turned_taken[0], 1)
                    if soft:
                        act.wait_ge(top_done, n * 2)
                        if attend:
                            act.wait_ge(weight_a, n - 1)
                            act.wait_ge(weight_b, n - 1)
                        for i in range(NB):
                            last = act.activation(expd[:, i, :], score_ps[:, i // CH, i % CH, :], ACT.Exp,
                                                  bias=top[:, i:i + 1], accum_out=total[:, i:i + 1])
                        last.then_inc(exp_done, 1)
                    if attend:
                        act.wait_ge(mo_made, n - 1)
                        act.activation(attended[:], mo_ps[:, 0:D], ACT.Identity, bias=bias[:, 2:3]).then_inc(mo_done, 1)
                    if conv:
                        act.wait_ge(value_made, n + 1)
                        act.activation(value_t[u][:].rearrange("p c n -> p (c n)"), value_ps[:, 0:D], ACT.Copy).then_inc(value_done, 1)
                    if soft:
                        act.wait_ge(inv_done, n)
                        for i in range(NB // 2, NB):
                            last = act.activation(weight[:, i, :], expd[:, i, :], ACT.Copy, scale=inv[:, i:i + 1])
                        last.then_inc(weight_b, 1)
                act.wait_ge(b_in, 16 * 4 * HB)
                tiles(act, slot)

            @block.vector
            def _(dve):
                def prepare(n, u):
                    for i, src, mean, inv_ in ((0, chip.x, chip.x_moments, inverse), (1, context, chip.ctx_moments, chip.ctx_inverse)):
                        last = dve.tensor_scalar(normed[u][:, i, :], tile_of(src, n), mean[:, bass.ds(n, 1), 0],
                                                 inv_[:, bass.ds(n, 1)], ALU.subtract, ALU.mult)
                    last.then_inc(normed_done, 1)

                def slot(n, j, conv, soft, attend, out):
                    if conv:
                        if attend:
                            dve.wait_ge(value_made, n - 1)
                        if isinstance(n, int):
                            dve.wait_ge(inverse_done, 1 if n < 3 else NG)
                        prepare(n, j % 2)
                    if soft:
                        dve.wait_ge(score_made, n)
                        dve.tensor_reduce(top[:], score_ps[:].rearrange("p b t s -> p (b t) s"), AX, ALU.max).then_inc(top_done, 1)
                        dve.wait_ge(top_done, n * 2 - 1)
                        dve.tensor_scalar(top[:], top[:], -1.0, None, ALU.mult).then_inc(top_done, 1)
                    if out:
                        dve.wait_ge(out_made, n - 2)
                        tile = tile_of(chip.x, n - 3)
                        dve.scalar_tensor_tensor(tile, out_ps[:, 0:D], bias[:, 3:4], tile, ALU.add, ALU.add).then_inc(out_done, 1)
                    if attend:
                        dve.wait_ge(turned, n - 1)
                        if out:
                            dve.wait_ge(mo_made, n - 2)
                        dve.tensor_copy(weight_t[:, 1, :, :].rearrange("p c t -> p (c t)"),
                                        turned_ps[:, 1, :, :].rearrange("p c t -> p (c t)")).then_inc(turned_taken[1], 1)
                    if conv:
                        dve.wait_ge(conv_made, n + 1)
                        for i in range(2):
                            last = dve.tensor_scalar(maps[j % 2][:, i, :], conv_ps[:, i, :], bias[:, i:i + 1], None, ALU.add)
                        last.then_inc(maps_done, 1)
                    if soft:
                        dve.wait_ge(exp_done, n)
                        if attend:
                            dve.wait_ge(weight_b, n - 1)
                        dve.reciprocal(inv[:], total[:]).then_inc(inv_done, 1)
                        dve.wait_ge(inv_done, n)
                        for i in range(NB // 2):
                            last = dve.tensor_scalar(weight[:, i, :], expd[:, i, :], inv[:, i:i + 1], None, ALU.mult)
                        last.then_inc(weight_a, 1)
                    if out:
                        dve.wait_ge(out_done, n - 2)
                        measure(chip, dve, n - 3)
                dve.wait_ge(ctx_in, 16)
                dve.wait_ge(b_in, 16 * 4 * HB)
                dve.wait_ge(w_turned, 1)
                dve.tensor_copy(w_cols[:].rearrange("p i n -> p (i n)"), value_ps[:]).then_inc(w_ready, 1)
                tiles(dve, slot)
    chip.end_stage()


def build(nc, inputs, out):
    with ExitStack() as stack:
        chip = Chip(nc, inputs, stack)
        load(chip)
        layer0(chip)
        layer1(chip)
        layer2(chip)
        layer3(chip)
        store(chip, out)


_OUT = (BATCH, SEQ, D)


def kernel(**inputs):
    import concourse.bacc as _bacc
    from concourse.bass_utils import run_bass_kernel_spmd as _run

    nc = _bacc.Bacc("TRN2", target_bir_lowering=False, num_devices=1)
    arrays, aps = {}, {}
    for name, a in inputs.items():
        a = np.ascontiguousarray(a)
        arrays[f"in_{name}_dram"] = a
        aps[name] = nc.dram_tensor(f"in_{name}_dram", a.shape, mybir.dt.from_np(a.dtype), kind="ExternalInput").ap()
    out = nc.dram_tensor("out_0_dram", _OUT, F32, kind="ExternalOutput").ap()
    build(nc, aps, out)
    r = _run(nc, [arrays], core_ids=[0])
    return r.results[0]["out_0_dram"]
```
